# Optimizing a Trainium2 kernel written in Bass

```python
import numpy as np
import jax
import jax.numpy as jnp

def _softmax(x, axis=-1):
    return jax.nn.softmax(x, axis=axis)

def _gelu(x):
    return jax.nn.gelu(x, approximate=True)

def _silu(x):
    return jax.nn.silu(x)

def _sigmoid(x):
    return jax.nn.sigmoid(x)

def _layernorm(x, axis=-1, eps=1e-05):
    m = jnp.mean(x, axis=axis, keepdims=True)
    v = jnp.var(x, axis=axis, keepdims=True)
    return (x - m) / jnp.sqrt(v + eps)

def _scatter_add(tgt, idx, src, axis=0):
    return tgt.at[idx].add(src)

def _segment_sum(src, seg, n):
    return jax.ops.segment_sum(src, seg, n)
kernel_name = 'mk_xattn_ffn_d2_seqx_r8_8961c0'

def setup_inputs(seed: int=0):
    np.random.seed(seed)
    _w = jnp.asarray

    def _rec_inputs():
        import jax
        import jax.numpy as jnp
        _rk = jax.random.key(seed)
        x = -0.0003929 + 0.9999 * jax.random.normal(jax.random.fold_in(_rk, 1), (32, 64, 512), jnp.float32)
        _lenS = 64 - jax.random.randint(jax.random.fold_in(_rk, 7), (32,), 0, max(1, 64 // 4) + 1, jnp.int32)
        _lenS2 = 64 - jax.random.randint(jax.random.fold_in(_rk, 8), (32,), 0, max(1, 64 // 4) + 1, jnp.int32)
        _ctx_4096P = jax.random.normal(jax.random.fold_in(_rk, 11), (32, 16, 512), jnp.float32)
        _ctx_4096c = jax.random.dirichlet(jax.random.fold_in(_rk, 511), 0.3 * jnp.ones((16,), jnp.float32), (32, 64))
        _ctx_4096t = jnp.einsum('bsk,bkd->bsd', _ctx_4096c, _ctx_4096P)
        _ctx_4096t = _ctx_4096t * jax.lax.rsqrt(jnp.mean(jnp.square(_ctx_4096t)) + 1e-12) * 0.953939
        ctx_4096 = 2.81802e-05 + 1.00001 * (_ctx_4096t + 0.3 * jax.random.normal(jax.random.fold_in(_rk, 611), (32, 64, 512), jnp.float32))
        return (x, ctx_4096)
    x, ctx_4096 = _rec_inputs()

    def _L0_xattn_setup():
        import jax, jax.numpy as jnp
        import numpy as np
        DIM = 64
        HEADS = 8
        DIM_HEAD = 64
        HIDDEN = HEADS * DIM_HEAD
        SCALE = DIM_HEAD ** (-0.5)
        key = jax.random.key(seed)
        ks = jax.random.split(key, 9)
        b, n = (8, 512)
        std = 1.0 / np.sqrt(DIM)
        return {'q': jax.random.normal(ks[0], (b, DIM, n), jnp.float32), 'k': jax.random.normal(ks[1], (b, DIM, n), jnp.float32), 'v': jax.random.normal(ks[2], (b, DIM, n), jnp.float32), 'Wq': jax.random.normal(ks[3], (HIDDEN, DIM), jnp.float32) * std, 'Wk': jax.random.normal(ks[4], (HIDDEN, DIM), jnp.float32) * std, 'Wv': jax.random.normal(ks[5], (HIDDEN, DIM), jnp.float32) * std, 'Wo': jax.random.normal(ks[6], (DIM, HIDDEN), jnp.float32) * (1.0 / np.sqrt(HIDDEN)), 'bo': jax.random.normal(ks[7], (DIM,), jnp.float32) * 0.01, 'g': jnp.ones((1, DIM, 1), jnp.float32)}
    _L0_xattn_all = _L0_xattn_setup()
    _L0_xattn_in = {k: v for k, v in _L0_xattn_all.items() if k in ('Wq', 'Wk', 'Wv', 'Wo', 'bo', 'g')}
    del _L0_xattn_all

    def _L0_ffn_setup():
        import jax, jax.numpy as jnp
        import numpy as np
        ALPHA = 32
        R = 16
        SCALING = ALPHA / R
        key = jax.random.key(seed)
        k1, k2, k3, k4 = jax.random.split(key, 4)
        B_, S, D = (4, 256, 512)
        H, r, O = (8, R, 512)
        x = jax.random.normal(k1, (B_, S, D), dtype=jnp.float32)
        A = jax.random.normal(k2, (H, r, D), dtype=jnp.float32) * 0.02
        Bm = jax.random.normal(k3, (H, O, r), dtype=jnp.float32) * 0.02
        Wr = jax.random.normal(k4, (H, D), dtype=jnp.float32) * 0.02
        br = jnp.zeros((H,), dtype=jnp.float32)
        return {'x': x, 'A': A, 'B': Bm, 'Wr': Wr, 'br': br}
    _L0_ffn_all = _L0_ffn_setup()
    _L0_ffn_in = {k: v for k, v in _L0_ffn_all.items() if k in ('A', 'B', 'Wr', 'br')}
    del _L0_ffn_all

    def _L1_xattn_setup():
        import jax, jax.numpy as jnp
        import numpy as np
        HEADS = 32
        KV_HEADS = 8
        HEAD_DIM = 128
        EPS = 1e-06

        def rms_norm(x, w):
            var = jnp.mean(jnp.square(x.astype(jnp.float32)), axis=-1, keepdims=True)
            return (x.astype(jnp.float32) * jax.lax.rsqrt(var + EPS)).astype(x.dtype) * w
        key = jax.random.key(seed)
        ks = jax.random.split(key, 6)
        bsz, n_lat, seq, hidden = (8, 64, 512, 512)
        return {'latents': jax.random.normal(ks[0], (bsz, n_lat, hidden), jnp.float32), 'context': jax.random.normal(ks[1], (bsz, seq, hidden), jnp.float32), 'Wq': jax.random.normal(ks[2], (hidden, HEADS * HEAD_DIM), jnp.float32) * 0.02, 'Wk': jax.random.normal(ks[3], (hidden, KV_HEADS * HEAD_DIM), jnp.float32) * 0.02, 'Wv': jax.random.normal(ks[4], (hidden, KV_HEADS * HEAD_DIM), jnp.float32) * 0.02, 'Wo': jax.random.normal(ks[5], (HEADS * HEAD_DIM, hidden), jnp.float32) * 0.02, 'q_norm_w': jnp.ones((HEAD_DIM,), jnp.float32), 'k_norm_w': jnp.ones((HEAD_DIM,), jnp.float32)}
    _L1_xattn_all = _L1_xattn_setup()
    _L1_xattn_in = {k: v for k, v in _L1_xattn_all.items() if k in ('Wq', 'Wk', 'Wv', 'Wo', 'q_norm_w', 'k_norm_w')}
    del _L1_xattn_all

    def _L1_ffn_setup():
        import jax, jax.numpy as jnp
        import numpy as np
        BLOCK = 32
        key = jax.random.key(seed)
        k1, k2, k3 = jax.random.split(key, 3)
        B, S, I, O = (2, 256, 512, 512)
        A = jax.random.normal(k1, (B, S, I), dtype=jnp.float32)
        w_q = jax.random.randint(k2, (O, I), 0, 255, dtype=jnp.int32)
        scales = jax.random.uniform(k3, (O, I // BLOCK), dtype=jnp.float32) * 0.05
        return {'A': A, 'w_q': w_q, 'scales': scales}
    _L1_ffn_all = _L1_ffn_setup()
    _L1_ffn_in = {k: v for k, v in _L1_ffn_all.items() if k in ('w_q', 'scales')}
    del _L1_ffn_all
    return {'x': x, 'ctx_4096': ctx_4096, 'L0_xattn_Wq': _L0_xattn_in['Wq'], 'L0_xattn_Wk': _L0_xattn_in['Wk'], 'L0_xattn_Wv': _L0_xattn_in['Wv'], 'L0_xattn_Wo': _L0_xattn_in['Wo'], 'L0_xattn_bo': _L0_xattn_in['bo'], 'L0_xattn_g': _L0_xattn_in['g'], 'L0_ffn_A': _L0_ffn_in['A'], 'L0_ffn_B': _L0_ffn_in['B'], 'L0_ffn_Wr': _L0_ffn_in['Wr'], 'L0_ffn_br': _L0_ffn_in['br'], 'L1_xattn_Wq': _L1_xattn_in['Wq'], 'L1_xattn_Wk': _L1_xattn_in['Wk'], 'L1_xattn_Wv': _L1_xattn_in['Wv'], 'L1_xattn_Wo': _L1_xattn_in['Wo'], 'L1_xattn_q_norm_w': _L1_xattn_in['q_norm_w'], 'L1_xattn_k_norm_w': _L1_xattn_in['k_norm_w'], 'L1_ffn_w_q': _L1_ffn_in['w_q'], 'L1_ffn_scales': _L1_ffn_in['scales']}

def reference(x, ctx_4096, L0_xattn_Wq, L0_xattn_Wk, L0_xattn_Wv, L0_xattn_Wo, L0_xattn_bo, L0_xattn_g, L0_ffn_A, L0_ffn_B, L0_ffn_Wr, L0_ffn_br, L1_xattn_Wq, L1_xattn_Wk, L1_xattn_Wv, L1_xattn_Wo, L1_xattn_q_norm_w, L1_xattn_k_norm_w, L1_ffn_w_q, L1_ffn_scales):
    import jax
    import jax.numpy as jnp

    def _L0_xattn_ref(q, k, v, Wq, Wk, Wv, Wo, bo, g):
        import jax, jax.numpy as jnp
        import numpy as np
        DIM = 64
        HEADS = 8
        DIM_HEAD = 64
        HIDDEN = HEADS * DIM_HEAD
        SCALE = DIM_HEAD ** (-0.5)
        b = q.shape[0]
        qh = jnp.einsum('bcn,oc->bon', q, Wq).reshape(b, HEADS, DIM_HEAD, -1)
        kh = jnp.einsum('bcn,oc->bon', k, Wk).reshape(b, HEADS, DIM_HEAD, -1)
        vh = jnp.einsum('bcn,oc->bon', v, Wv).reshape(b, HEADS, DIM_HEAD, -1)
        qh = jax.nn.softmax(qh, axis=-2) * SCALE
        kh = jax.nn.softmax(kh, axis=-1)
        context = jnp.einsum('bhdn,bhen->bhde', kh, vh)
        out = jnp.einsum('bhde,bhdn->bhen', context, qh)
        out = out.reshape(b, HIDDEN, -1)
        out = jnp.einsum('bcn,oc->bon', out, Wo) + bo[None, :, None]
        norm = jnp.maximum(jnp.sqrt(jnp.sum(out * out, axis=1, keepdims=True)), 1e-12)
        return out / norm * g * np.sqrt(DIM)

    def _L0_ffn_ref(x, A, B, Wr, br):
        import jax, jax.numpy as jnp
        import numpy as np
        ALPHA = 32
        R = 16
        SCALING = ALPHA / R
        H = A.shape[0]
        router_logits = jnp.einsum('bsd,hd->bsh', x, Wr) + br
        scores = H * jax.nn.softmax(router_logits, axis=-1)
        low = jnp.einsum('bsd,hrd->bshr', x, A)
        out = jnp.einsum('bshr,hor,bsh->bso', low, B, scores)
        return SCALING * out

    def _L1_xattn_ref(latents, context, Wq, Wk, Wv, Wo, q_norm_w, k_norm_w):
        import jax, jax.numpy as jnp
        import numpy as np
        HEADS = 32
        KV_HEADS = 8
        HEAD_DIM = 128
        EPS = 1e-06

        def rms_norm(x, w):
            var = jnp.mean(jnp.square(x.astype(jnp.float32)), axis=-1, keepdims=True)
            return (x.astype(jnp.float32) * jax.lax.rsqrt(var + EPS)).astype(x.dtype) * w
        bsz, q_len, hidden = latents.shape
        kv = jnp.concatenate([context, latents], axis=1)
        kv_len = kv.shape[1]
        groups = HEADS // KV_HEADS
        q = (latents @ Wq).reshape(bsz, q_len, HEADS, HEAD_DIM).transpose(0, 2, 1, 3)
        k = (kv @ Wk).reshape(bsz, kv_len, KV_HEADS, HEAD_DIM).transpose(0, 2, 1, 3)
        v = (kv @ Wv).reshape(bsz, kv_len, KV_HEADS, HEAD_DIM).transpose(0, 2, 1, 3)
        q = rms_norm(q, q_norm_w)
        k = rms_norm(k, k_norm_w)
        qg = q.reshape(bsz, KV_HEADS, groups, q_len, HEAD_DIM)
        scale = 1.0 / np.sqrt(HEAD_DIM)
        scores = jnp.einsum('bhgqd,bhkd->bhgqk', qg, k) * scale
        probs = jax.nn.softmax(scores.astype(jnp.float32), axis=-1).astype(q.dtype)
        out = jnp.einsum('bhgqk,bhkd->bhgqd', probs, v)
        out = out.reshape(bsz, HEADS, q_len, HEAD_DIM).transpose(0, 2, 1, 3)
        out = out.reshape(bsz, q_len, HEADS * HEAD_DIM)
        return out @ Wo

    def _L1_ffn_ref(A, w_q, scales):
        import jax, jax.numpy as jnp
        import numpy as np
        BLOCK = 32
        O, I = w_q.shape
        q = w_q.astype(jnp.float32) - 128.0
        W = (q.reshape(O, I // BLOCK, BLOCK) * scales[:, :, None]).reshape(O, I)
        return jnp.einsum('bsi,oi->bso', A, W)
    x = x + _L0_xattn_ref(_layernorm(x, axis=-1), ctx_4096, ctx_4096, L0_xattn_Wq, L0_xattn_Wk, L0_xattn_Wv, L0_xattn_Wo, L0_xattn_bo, L0_xattn_g)
    x = x + _L0_ffn_ref(_layernorm(x, axis=-1), L0_ffn_A, L0_ffn_B, L0_ffn_Wr, L0_ffn_br)
    x = x + _L1_xattn_ref(_layernorm(x, axis=-1), ctx_4096, L1_xattn_Wq, L1_xattn_Wk, L1_xattn_Wv, L1_xattn_Wo, L1_xattn_q_norm_w, L1_xattn_k_norm_w)
    x = x + _L1_ffn_ref(_layernorm(x, axis=-1), L1_ffn_w_q, L1_ffn_scales)
    return x

_drawn_inputs = setup_inputs


def setup_inputs(seed=0):
    import zlib

    import numpy as np

    out = dict(_drawn_inputs(seed))
    spreads = {'L0_xattn_g': (1.0, 0.2),
     'L0_ffn_br': (0.0, 0.1),
     'L1_xattn_q_norm_w': (1.0, 0.6),
     'L1_xattn_k_norm_w': (1.0, 0.6)}
    factors = {}
    for name, (base, spread) in spreads.items():
        noise = np.random.default_rng([zlib.crc32(name.encode()), seed]).standard_normal(out[name].shape)
        drawn = base * np.exp(spread * noise) if base else spread * noise
        out[name] = jnp.asarray(drawn.astype(out[name].dtype))
    for name, factor in factors.items():
        out[name] = (out[name] * factor).astype(out[name].dtype)
    return out
```

```python
import math
from contextlib import ExitStack, contextmanager

import concourse.bass as bass
from concourse import mybir

P = 128
FP32 = mybir.dt.float32
FP32R = mybir.dt.float32r
INT32 = mybir.dt.int32
ALU = mybir.AluOpType
ACT = mybir.ActivationFunctionType
AX = mybir.AxisListType

BATCHES, SEQ, HIDDEN = 32, 64, 512
HC = HIDDEN // P
HALVES = 2
HB = BATCHES // HALVES
HP = HB // 2
L0_HEADS, L0_DH = 8, 64
FFN_HEADS, FFN_R, FFN_SCALING = 8, 16, 32 / 16
FFN_LOW = FFN_HEADS * FFN_R
L1_HEADS, L1_KV, L1_DH = 32, 8, 128
GROUP = L1_HEADS // L1_KV
L1_SCALE = 1.0 / math.sqrt(L1_DH)
LN_EPS, RMS_EPS = 1e-5, 1e-6
LN_COL, RMS_COL = GROUP, GROUP + 1
W_KV, W_Q, W_O = 0, HC * 2 * L1_DH, HC * 2 * L1_DH + HC * GROUP * L1_DH
W_COLS = W_O + GROUP * HIDDEN
W_CHUNKS = HP
W_CHUNK = W_COLS // W_CHUNKS


def at_least(engine, sem, value):
    if not (isinstance(value, int) and value <= 0):
        engine.wait_ge(sem, value)


class Chain:

    def __init__(self, engine, sem):
        self.engine, self.sem, self.count, self.base = engine, sem, 0, 0

    def link(self, instruction):
        instruction.then_inc(self.sem, 1)
        self.count += 1
        self.engine.wait_ge(self.sem, self.base + self.count)

    @contextmanager
    def repeat(self, first, end, links):
        before = self.count
        with self.engine.Fori(first, end) as i:
            self.base = (i - first) * links
            yield i
            assert self.count - before == links, f"{self.count - before} links"
        self.base, self.count = 0, before + links * (end - first)


def plain(ap):
    return ap.bitcast(FP32)


def spread(ap, n):
    return ap.unsqueeze(len(ap.shape)).to_broadcast([*ap.shape, n])


def semaphores(nc, stack, names):
    made = {name: stack.enter_context(nc.semaphore(name)) for name in names.split()}
    numbers = [s.num for s in made.values()]
    assert numbers == list(range(numbers[0], numbers[0] + len(numbers)))
    return made


def clear(nc, sems):
    first = min(s.num for s in sems.values())
    nc.all_engine_barrier(sems_to_clear=range(first, first + len(sems)))


def linear_attention(nc, sems, half, const, xres, kvT, obuf, dram):
    ident, consts = const
    x, ctx, ctx_t, wq_d, wk_d, wv_d, wo_d, bo_d = dram
    st = ExitStack()
    with st:
        sb = lambda name, shape, dt=FP32: st.enter_context(nc.sbuf_tensor(name, shape, dt))
        ps = lambda name: st.enter_context(nc.psum_tensor(name, [P, 512], FP32))
        wq_h, wq_l = sb("l0_wq_h", [P, HIDDEN], FP32R), sb("l0_wq_l", [P, HIDDEN], FP32R)
        wk_h, wk_l = sb("l0_wk_h", [P, HIDDEN], FP32R), sb("l0_wk_l", [P, HIDDEN], FP32R)
        wvo = sb("l0_wvo", [P, HIDDEN])
        bo = sb("l0_bo", [P, 1])
        x_st = [sb(f"x_stack{s}", [P, HIDDEN], FP32R) for s in range(2)]
        c_st = [sb(f"c_stack{s}", [P, HIDDEN], FP32R) for s in range(2)]
        xn = sb("xn", [P, HIDDEN])
        cn = sb("cn", [P, HIDDEN])
        cT = [sb(f"cT{s}", [P, HC, SEQ]) for s in range(2)]
        kexp = [sb(f"kexp{s}", [P, HC, HIDDEN]) for s in range(2)]
        qn = [sb(f"qn{s}", [P, HC, HIDDEN]) for s in range(2)]
        kT = [sb(f"kT{j}", [P, HIDDEN]) for j in range(2)]
        qT = [sb(f"qT{s}", [P, HC, HIDDEN]) for s in range(2)]
        gsb = sb("gsb", [P, HIDDEN])
        mT = [sb(f"mT{s}", [P, HC, SEQ]) for s in range(2)]
        stats, moments, rstd = sb("stats", [P, 6]), sb("moments", [P, 2]), sb("rstd", [P, 2])
        spare = sb("spare1", [P, 1])
        knmax, ksum, krec = (sb(n_, [P, 2, HC]) for n_ in ("knmax", "ksum", "krec"))
        qnmax, qsum = sb("qnmax", [P, HC, L0_HEADS]), sb("qsum", [P, HC, L0_HEADS])
        qrec = sb("qrec", [P, 2, HC, L0_HEADS])
        kp = [ps(f"kp{j}") for j in range(2)]
        qp = [ps(f"qp{j}") for j in range(2)]
        tkp, tqp, gmp, op = ps("tkp"), ps("tqp"), ps("gmp"), ps("op")
        S = sems

        wq_raw, wk_raw = kexp[0][:, 0, :], kexp[0][:, 1, :]
        wv_raw = kexp[1][:, 0, 0:HC * L0_DH].rearrange("p (c e) -> p c e", c=HC)
        wo_raw = kexp[1][:, 1, 0:HC * L0_DH].rearrange("p (c e) -> p c e", c=HC)

        def num(b):
            return 2 * b[0] + b[1]

        def before(b):
            return (b[0] - 1, 1) if b[1] == 0 else (b[0], 0)

        def after(b):
            return (b[0], 1) if b[1] == 0 else (b[0] + 1, 0)

        def rows(s):
            return slice(s * SEQ, s * SEQ + SEQ)

        def heads(t):
            return t.rearrange("p (h d) -> p h d", h=L0_HEADS)

        PEEL = 2

        def steps(repeat, step):
            for p in range(PEEL):
                for s in range(2):
                    step((p, s), True, 2 * p + s >= 1, 2 * p + s >= 2, True)
            with repeat(PEEL, HP - 1) as p:
                for s in range(2):
                    step((p, s), True, True, True, True)
            step((HP - 1, 0), True, True, True, True)
            step((HP - 1, 1), True, True, True, False)
            step((HP, 0), False, True, True, False)
            step((HP, 1), False, False, True, False)

        block = st.enter_context(nc.Block())

        @block.sync
        def _(sp):
            sp.dma_start(xres[:, 0:1, :], x[bass.ds(half * HP * P, P), :].rearrange(
                "(t p) n -> p t n", p=P)).then_inc(S["x_first"], 16)

            def load_c(b):
                at_least(sp, S["c_stacked"], num(b) - 1)
                sp.dma_start(cn[rows(b[1]), :], ctx[bass.ds((half * HB + num(b)) * SEQ, SEQ), :]).then_inc(
                    (S["c_in0"], S["c_in1"])[b[1]], 16)

            def load_ct(b):
                at_least(sp, S["g_step"], HC * (num(b) - 1))
                at_least(sp, S["ct_split"], num(b) - 1)
                sp.dma_start(cT[b[1]][:], ctx_t[bass.ds(half * HB + num(b), 1), :, :].rearrange(
                    "b p (c t) -> p (b c) t", c=HC)).then_inc((S["ct_in0"], S["ct_in1"])[b[1]], 16)

            load_c((0, 0))
            for dst, src in ((wq_raw, wq_d), (wk_raw, wk_d), (wv_raw, wv_d), (wo_raw, wo_d), (bo[:], bo_d)):
                sp.dma_start(dst, src).then_inc(S["w_in"], 16)
            sp.dma_start(xres[:, 1:HP, :], x[bass.ds(half * HP * P + P, (HP - 1) * P), :].rearrange(
                "(t p) n -> p t n", p=P)).then_inc(S["x_rest"], 16)
            for p in range(PEEL):
                for s in range(2):
                    load_c(after((p, s)))
                    load_ct((p, s))
            with sp.Fori(PEEL, HP - 1) as p:
                for s in range(2):
                    load_c(after((p, s)))
                    load_ct((p, s))
            load_c((HP - 1, 1))
            load_ct((HP - 1, 0))
            load_ct((HP - 1, 1))

        @block.tensor
        def _(pe):
            pe.wait_ge(S["w_in"], 80)
            for r, bank in ((0, kp[0]), (1, kp[1])):
                for c in range(HC):
                    last = nc.tensor.matmul(bank[0:SEQ, c * L0_DH:(c + 1) * L0_DH], wv_raw[rows(r), c, :],
                                            wo_raw[rows(r), c, :], start=True, stop=True)
            last.then_inc(S["wvo_done"], 1)
            pe.wait_ge(S["w_ready"], 1)

            def project(b, j):
                n, s, cols = num(b), b[1], slice(j * P, (j + 1) * P)
                if j == 0:
                    pe.wait_ge(S["c_stacked"], n + 1)
                    pe.wait_ge(S["x_stacked"], n + 1)
                at_least(pe, S["k_exp"], HC * n + j - 1)
                nc.tensor.matmul(kp[j % 2][:], wk_h[:, cols], c_st[s][:], start=True, stop=False)
                nc.tensor.matmul(kp[j % 2][:], wk_l[:, cols], c_st[s][:], start=False,
                                 stop=True).then_inc(S["k_proj"], 1)
                at_least(pe, S["q_sub"], HC * n + j - 1)
                nc.tensor.matmul(qp[j % 2][:], x_st[s][:, cols], wq_h[:], start=True, stop=False)
                nc.tensor.matmul(qp[j % 2][:], x_st[s][:, cols], wq_l[:], start=False,
                                 stop=True).then_inc(S["q_proj"], 1)

            def transpose_q(m, ms, j):
                if j == 0:
                    pe.wait_ge(S["q_norm"], HC * (m + 1))
                at_least(pe, S["qt_copied"], HC * m + j)
                for c in range(HC):
                    mm = nc.tensor.transpose(tqp[:, c * P:(c + 1) * P], qn[ms][:, c, j * P:(j + 1) * P], ident[:])
                mm.then_inc(S["tq_done"], 1)

            def transpose_k(m, ms, j):
                if j == 0:
                    pe.wait_ge(S["k_exp"], HC * (m + 1))
                at_least(pe, S["kt_copied"], HC * m + j)
                for c in range(HC):
                    mm = nc.tensor.transpose(tkp[:, c * P:(c + 1) * P], kexp[ms][:, c, j * P:(j + 1) * P], ident[:])
                mm.then_inc(S["tk_done"], 1)

            def context(b, m, ms, j):
                if j == 0:
                    pe.wait_ge((S["ct_in0"], S["ct_in1"])[ms], 16 * (before(b)[0] + 1))
                    at_least(pe, S["m_scaled"], m)
                pe.wait_ge(S["kt_copied"], HC * m + j + 1)
                nc.tensor.matmul(gmp[0:SEQ, :], cT[ms][:, j, :], kT[j % 2][:], start=(j == 0),
                                 stop=(j == HC - 1)).then_inc(S["g_step"], 1)

            project((0, 0), 0)

            def step(b, front, back, last_, more):
                n, s = num(b), b[1]
                m, ms = n - 1, 1 - s
                o = n - 2
                for j in range(HC):
                    if last_ and j == 0:
                        transpose_q(o, s, HC - 1)
                    if back and j >= 1:
                        transpose_q(m, ms, j - 1)
                    if back:
                        transpose_k(m, ms, j)
                    if last_ and j == 0:
                        pe.wait_ge(S["g_copied"], o + 1)
                        for c in range(HC):
                            mm = nc.tensor.matmul(gmp[:, c * P:(c + 1) * P], gsb[:, c * P:(c + 1) * P],
                                                  wvo[:, c * P:(c + 1) * P], start=True, stop=True)
                        mm.then_inc(S["m_done"], 1)
                    if front and j < HC - 1:
                        project(b, j + 1)
                    if more and j == HC - 1:
                        project(after(b), 0)
                    if last_ and j == 2:
                        pe.wait_ge(S["m_scaled"], o + 1)
                        pe.wait_ge(S["qt_copied"], HC * (o + 1))
                        at_least(pe, S["o_stored"], o)
                        for c in range(HC):
                            mm = nc.tensor.matmul(op[rows(s), :], mT[s][:, c, :], qT[s][:, c, :], start=(c == 0),
                                                  stop=(c == HC - 1))
                        mm.then_inc(S["o_done"], 1)
                    if back and j >= 1:
                        context(b, m, ms, j - 1)
                if back:
                    context(b, m, ms, HC - 1)

            steps(pe.Fori, step)

        @block.scalar
        def _(act):
            def stack_high(b):
                s, r = b[1], rows(b[1])
                act.wait_ge(S["xn_ready"], b[0] + 1)
                at_least(act, S["q_proj"], HC * (num(b) - 1))
                nc.scalar.activation(x_st[s][r, :], xn[r, :], ACT.Copy).then_inc(S["x_high"], 1)
                act.wait_ge((S["c_in0"], S["c_in1"])[s], 16 * (b[0] + 1))
                nc.scalar.activation(c_st[s][r, :], cn[r, :], ACT.Copy).then_inc(S["c_high"], 1)

            act.wait_ge(S["w_ready"], 1)
            stack_high((0, 0))

            def copy_q(m, ms, j):
                act.wait_ge(S["tq_done"], HC * m + j + 1)
                at_least(act, S["o_done"], m - 1)
                nc.scalar.activation(qT[ms][:, j, :], tqp[:], ACT.Copy).then_inc(S["qt_copied"], 1)

            def step(b, front, back, last_, more):
                n, s = num(b), b[1]
                m, ms = n - 1, 1 - s
                o = n - 2
                for j in range(HC):
                    if last_ and j == 0:
                        copy_q(o, s, HC - 1)
                    if back and j >= 1:
                        copy_q(m, ms, j - 1)
                    if back:
                        act.wait_ge(S["tk_done"], HC * m + j + 1)
                        at_least(act, S["g_step"], HC * m + j - 1)
                        nc.scalar.activation(kT[j % 2][:], tkp[:], ACT.Copy).then_inc(S["kt_copied"], 1)
                    if front:
                        if j == 0:
                            at_least(act, S["tk_done"], HC * (n - 1))
                            at_least(act, S["krec_done"], n - 1)
                        act.wait_ge(S["k_max"], HC * n + j + 1)
                        nc.scalar.activation(kexp[s][:, j, :], kp[j % 2][:], ACT.Exp, bias=knmax[:, s, j:j + 1],
                                             accum_out=ksum[:, s, j:j + 1]).then_inc(S["k_exp"], 1)
                        act.wait_ge(S["q_sub"], HC * n + j + 1)
                        nc.scalar.activation(qn[s][:, j, :], qn[s][:, j, :], ACT.Exp).then_inc(S["q_exp"], 1)
                    if more and j == 1:
                        stack_high(after(b))
                    if back and j == 2:
                        act.wait_ge((S["ct_in0"], S["ct_in1"])[ms], 16 * (before(b)[0] + 1))
                        nc.scalar.activation(context_columns(kvT, before(b), 0), cT[ms][:],
                                             ACT.Copy).then_inc(S["ct_high"], 1)
                if last_:
                    act.wait_ge(S["o_done"], o + 1)
                    nc.scalar.activation(pair_rows(obuf, b[0] - 1, rows(s)), op[rows(s), :], ACT.Identity,
                                         bias=bo[rows(s), :]).then_inc(S["o_stored"], 1)
                if back:
                    act.wait_ge(S["g_step"], HC * (m + 1))
                    at_least(act, S["m_done"], m)
                    nc.scalar.activation(gsb[0:SEQ, :], gmp[0:SEQ, :], ACT.Copy).then_inc(S["g_copied"], 1)

            steps(act.Fori, step)

        @block.vector
        def _(dve):
            chain = Chain(dve, S["dve_chain"])
            link = chain.link

            def layer_stats(p):
                link(nc.vector.bn_stats(stats[:], pair_of(xres, p)))
                nc.vector.memset(spare[:], 0.0)
                nc.vector.bn_aggr(moments[:], stats[:]).then_inc(S["stats_ready"], 1)

            def normalise(p):
                dve.wait_ge(S["rstd_ready"], p + 1)
                nc.vector.tensor_scalar(xn[:], pair_of(xres, p), moments[:, 0:1], rstd[:, 1:2],
                                        ALU.subtract, ALU.mult).then_inc(S["xn_ready"], 1)

            def stack_low(b):
                s, r, other = b[1], rows(b[1]), rows(1 - b[1])
                dve.wait_ge(S["x_high"], num(b) + 1)
                nc.vector.tensor_tensor(x_st[s][other, :], xn[r, :], plain(x_st[s][r, :]),
                                        ALU.subtract).then_inc(S["x_stacked"], 1)
                dve.wait_ge(S["c_high"], num(b) + 1)
                nc.vector.tensor_tensor(c_st[s][other, :], cn[r, :], plain(c_st[s][r, :]),
                                        ALU.subtract).then_inc(S["c_stacked"], 1)

            dve.wait_ge(S["x_first"], 16)
            layer_stats(0)
            dve.wait_ge(S["w_in"], 80)
            nc.vector.memset(wvo[SEQ:P, :], 0.0)
            nc.vector.memset(gsb[SEQ:P, :], 0.0)
            nc.vector.tensor_copy(wq_h[:], wq_raw)
            link(nc.vector.tensor_copy(wk_h[:], wk_raw))
            nc.vector.tensor_tensor(wq_l[:], wq_raw, plain(wq_h[:]), ALU.subtract)
            nc.vector.tensor_tensor(wk_l[:], wk_raw, plain(wk_h[:]), ALU.subtract)
            normalise(0)
            dve.wait_ge(S["wvo_done"], 1)
            by_head = wvo[0:SEQ, :].rearrange("p (c r o) -> p c r o", c=HC, r=2)
            for r in range(2):
                last = nc.vector.tensor_scalar(by_head[:, :, r, :],
                                               kp[r][0:SEQ, 0:HC * L0_DH].rearrange("p (c o) -> p c o", c=HC),
                                               L0_DH ** -0.5, None, ALU.mult)
            link(last)
            nc.vector.memset(krec[:], 0.0).then_inc(S["w_ready"], 1)
            stack_low((0, 0))
            dve.wait_ge(S["x_rest"], 16)

            def q_sum(n, s, j):
                dve.wait_ge(S["q_exp"], HC * n + j + 1)
                link(nc.vector.tensor_reduce(qsum[:, j, :], heads(qn[s][:, j, :]), AX.X, ALU.add))
                nc.vector.reciprocal(qrec[:, s, j, :], qsum[:, j, :]).then_inc(S["q_rec"], 1)

            def step(b, front, back, last_, more):
                n, s = num(b), b[1]
                m, ms = n - 1, 1 - s
                o = n - 2
                if more and s == 1:
                    layer_stats(b[0] + 1)
                for j in range(HC):
                    if front:
                        dve.wait_ge(S["q_proj"], HC * n + j + 1)
                        nc.vector.tensor_reduce(knmax[:, s, j:j + 1], kp[j % 2][:], AX.X, ALU.max,
                                                negate=True).then_inc(S["k_max"], 1)
                        nc.vector.tensor_reduce(qnmax[:, j, :], heads(qp[j % 2][:]), AX.X, ALU.max,
                                                negate=True).then_inc(S["q_max"], 1)
                        dve.wait_ge(S["q_max"], HC * n + j + 1)
                        if j == 0:
                            at_least(dve, S["tq_done"], HC * (n - 1))
                        nc.vector.tensor_tensor(heads(qn[s][:, j, :]), heads(qp[j % 2][:]),
                                                spread(qnmax[:, j, :], L0_DH), ALU.add).then_inc(S["q_sub"], 1)
                    if back and j == 0:
                        dve.wait_ge(S["k_exp"], HC * (m + 1))
                        nc.vector.reciprocal(krec[:, ms, :], ksum[:, ms, :]).then_inc(S["krec_done"], 1)
                    if last_ and j == 0:
                        dve.wait_ge(S["m_done"], o + 1)
                        dve.wait_ge(S["krec_done"], o + 1)
                        at_least(dve, S["o_done"], o - 1)
                        for r in range(2):
                            mm = nc.vector.tensor_tensor(
                                mT[s][rows(r), :, :],
                                gmp[rows(r), :].rearrange("p (c r o) -> p c r o", c=HC, r=2)[:, :, r, :],
                                spread(krec[rows(r), s, :], SEQ), ALU.mult)
                        mm.then_inc(S["m_scaled"], 1)
                    if more and s == 1 and j == 0:
                        normalise(b[0] + 1)
                    if more and j == 2:
                        stack_low(after(b))
                    if front and j >= 1:
                        q_sum(n, s, j - 1)
                if front:
                    q_sum(n, s, HC - 1)

            steps(lambda a, b: chain.repeat(a, b, 1 + 2 * HC), step)

        @block.gpsimd
        def _(pool):
            chain = Chain(pool, S["pool_chain"])

            def layer_rstd(p):
                pool.wait_ge(S["stats_ready"], p + 1)
                chain.link(nc.gpsimd.tensor_tensor(rstd[:, 0:1], moments[:, 1:2], consts[:, LN_COL:LN_COL + 1],
                                                   ALU.add))
                nc.gpsimd.tensor_tensor(rstd[:, 1:2], rstd[:, 0:1], consts[:, 0:1],
                                        ALU.pow).then_inc(S["rstd_ready"], 1)

            layer_rstd(0)

            def step(b, front, back, last_, more):
                n, s = num(b), b[1]
                m, ms = n - 1, 1 - s
                if more and s == 1:
                    layer_rstd(b[0] + 1)
                for j in range(HC):
                    if front:
                        pool.wait_ge(S["q_rec"], HC * n + j + 1)
                        nc.gpsimd.tensor_tensor(heads(qn[s][:, j, :]), heads(qn[s][:, j, :]),
                                                spread(qrec[:, s, j, :], L0_DH), ALU.mult).then_inc(S["q_norm"], 1)
                    if back and j == 2:
                        pool.wait_ge(S["ct_high"], m + 1)
                        nc.gpsimd.tensor_tensor(context_columns(kvT, before(b), 1), cT[ms][:],
                                                plain(context_columns(kvT, before(b), 0)),
                                                ALU.subtract).then_inc(S["ct_split"], 1)

            steps(lambda a, b: chain.repeat(a, b, 1), step)


def pair_of(t, p):
    return t[:, bass.ds(p, 1), :].rearrange("p t n -> p (t n)")


def context_columns(kvT, batch, part):
    pair, s = batch
    return kvT[:, :, bass.ds(pair, 1), part, s * 3 * SEQ:s * 3 * SEQ + SEQ].rearrange("p c b t -> p (c b) t")


def x_columns(kvT, p, part):
    return kvT[:, :, bass.ds(p, 1), part, SEQ:3 * SEQ].rearrange("p c b t -> p (c b) t")


def pair_rows(t, p, r):
    return t[r, bass.ds(p, 1), :].rearrange("p t n -> p (t n)")


def norm_and_ffn(nc, sems, const, xres, kvT, obuf, dram):
    ident, consts = const
    g_d, in_d, out_d, br_d = dram
    NR = FFN_LOW + FFN_HEADS
    st = ExitStack()
    with st:
        sb = lambda name, shape, dt=FP32: st.enter_context(nc.sbuf_tensor(name, shape, dt))
        ps = lambda name: st.enter_context(nc.psum_tensor(name, [P, 512], FP32))
        w_in, w_out = sb("ffn_in", [P, HC, NR]), sb("ffn_out", [P, HIDDEN])
        g, g8, br = sb("g", [P, 1]), sb("g8", [P, 1]), sb("br", [P, FFN_HEADS])
        same_batch = sb("same_batch", [P, P])
        sq, rinv, scaled = sb("sq", [P, HIDDEN]), sb("rinv", [P, HIDDEN]), sb("scaled", [P, HIDDEN])
        yn, yT = sb("yn", [P, HIDDEN]), sb("yT", [P, HIDDEN])
        zn = sb("zn", [P, HIDDEN])
        logit, share = sb("logit", [P, FFN_HEADS]), sb("share", [P, FFN_HEADS])
        e8, small = sb("e8", [P, FFN_HEADS]), sb("small", [P, 4])
        low, lowT = sb("low", [P, FFN_LOW]), sb("lowT", [P, FFN_LOW])
        ystats, ymom, yrstd = sb("ystats", [P, 6]), sb("ymom", [P, 2]), sb("yrstd", [P, 2])
        spare = sb("spare2", [P, 1])
        zstats, zmom, zrstd = sb("zstats", [P, 6]), sb("zmom", [P, 2]), sb("zrstd", [P, 2])
        ssp, ytp, ztp, rlp, ltp, fp = ps("ssp"), ps("ytp"), ps("ztp"), ps("rlp"), ps("ltp"), ps("fp")
        S = sems
        block = st.enter_context(nc.Block())

        def steps(repeat, step):
            for k in range(3):
                step(k, True, k >= 1, k >= 2)
            with repeat(3, HP) as k:
                step(k, True, True, True)
            step(HP, False, True, True)
            step(HP + 1, False, False, True)

        @block.sync
        def _(sp):
            for dst, src in ((w_in[:], in_d), (w_out[:], out_d), (g[:], g_d), (br[:], br_d)):
                sp.dma_start(dst, src).then_inc(S["f_in"], 16)

        @block.tensor
        def _(pe):
            pe.wait_ge(S["f_ready"], 1)

            def step(k, a, f, z):
                if a:
                    pe.wait_ge(S["sq_done"], k + 1)
                    at_least(pe, S["r2_ready"], k)
                    nc.tensor.matmul(ssp[:], same_batch[:], sq[:], start=True, stop=True).then_inc(S["ss_done"], 1)
                if f:
                    pe.wait_ge(S["yn_ready"], k)
                    at_least(pe, S["yt_copied"], k - 1)
                    for c in range(HC):
                        mm = nc.tensor.transpose(ytp[:, c * P:(c + 1) * P], yn[:, c * P:(c + 1) * P], ident[:])
                    mm.then_inc(S["yt_done"], 1)
                if z:
                    pe.wait_ge(S["zn_ready"], k - 1)
                    at_least(pe, S["z_split"], k - 2)
                    for c in range(HC):
                        mm = nc.tensor.transpose(ztp[:, c * P:(c + 1) * P], zn[:, c * P:(c + 1) * P], ident[:])
                    mm.then_inc(S["zt_done"], 1)
                if f:
                    pe.wait_ge(S["yt_copied"], k)
                    at_least(pe, S["low_ready"], k - 1)
                    for c in range(HC):
                        mm = nc.tensor.matmul(rlp[:, 0:NR], yT[:, c * P:(c + 1) * P], w_in[:, c, :],
                                              start=(c == 0), stop=(c == HC - 1))
                    mm.then_inc(S["rl_done"], 1)
                    pe.wait_ge(S["low_ready"], k)
                    at_least(pe, S["lt_copied"], k - 1)
                    nc.tensor.transpose(ltp[:, 0:P], low[:], ident[:]).then_inc(S["lt_done"], 1)
                    pe.wait_ge(S["lt_copied"], k)
                    at_least(pe, S["x2_ready"], k - 1)
                    nc.tensor.matmul(fp[:], lowT[:], w_out[:], start=True, stop=True).then_inc(S["f_done"], 1)

            steps(pe.Fori, step)

        @block.scalar
        def _(act):
            def step(k, a, f, z):
                if a:
                    at_least(act, S["ss_done"], k)
                    nc.scalar.activation(sq[:], pair_of(obuf, k), ACT.Square).then_inc(S["sq_done"], 1)
                if f:
                    act.wait_ge(S["yt_done"], k)
                    at_least(act, S["rl_done"], k - 1)
                    nc.scalar.activation(yT[:], ytp[:], ACT.Copy).then_inc(S["yt_copied"], 1)
                if z:
                    act.wait_ge(S["zt_done"], k - 1)
                    nc.scalar.activation(x_columns(kvT, k - 2, 0), ztp[:].rearrange("p (c t) -> p c t", c=HC),
                                         ACT.Copy).then_inc(S["z_high"], 1)
                if f:
                    act.wait_ge(S["logit_ready"], k)
                    nc.scalar.activation(e8[:], logit[:], ACT.Exp, bias=small[:, 0:1],
                                         accum_out=small[:, 1:2]).then_inc(S["e_done"], 1)
                if a:
                    act.wait_ge(S["r2_ready"], k + 1)
                    nc.scalar.activation(rinv[:], rinv[:], ACT.Sqrt).then_inc(S["rinv_done"], 1)
                if f:
                    act.wait_ge(S["lt_done"], k)
                    nc.scalar.activation(lowT[:], ltp[:, 0:P], ACT.Copy).then_inc(S["lt_copied"], 1)

            steps(act.Fori, step)

        @block.gpsimd
        def _(pool):
            chain = Chain(pool, S["pool_chain2"])

            def step(k, a, f, z):
                if f:
                    pool.wait_ge(S["ystats_ready"], k)
                    chain.link(nc.gpsimd.tensor_tensor(yrstd[:, 0:1], ymom[:, 1:2], consts[:, LN_COL:LN_COL + 1], ALU.add))
                    nc.gpsimd.tensor_tensor(yrstd[:, 1:2], yrstd[:, 0:1], consts[:, 0:1],
                                            ALU.pow).then_inc(S["yrstd_ready"], 1)
                if z:
                    pool.wait_ge(S["zstats_ready"], k - 1)
                    chain.link(nc.gpsimd.tensor_tensor(zrstd[:, 0:1], zmom[:, 1:2], consts[:, LN_COL:LN_COL + 1], ALU.add))
                    nc.gpsimd.tensor_tensor(zrstd[:, 1:2], zrstd[:, 0:1], consts[:, 0:1],
                                            ALU.pow).then_inc(S["zrstd_ready"], 1)

            steps(lambda a, b: chain.repeat(a, b, 2), step)

        @block.vector
        def _(dve):
            chain = Chain(dve, S["dve_chain2"])
            link = chain.link
            dve.wait_ge(S["f_in"], 64)
            link(nc.vector.memset(same_batch[:], 0.0))
            nc.vector.memset(same_batch[0:SEQ, 0:SEQ], 1.0)
            nc.vector.memset(same_batch[SEQ:P, SEQ:P], 1.0)
            link(nc.vector.tensor_scalar(g8[:], g[:], math.sqrt(SEQ), None, ALU.mult))
            nc.vector.memset(small[:], 0.0).then_inc(S["f_ready"], 1)

            def step(k, a, f, z):
                if f:
                    link(nc.vector.bn_stats(ystats[:], pair_of(xres, k - 1)))
                    nc.vector.memset(spare[:], 0.0)
                    nc.vector.bn_aggr(ymom[:], ystats[:]).then_inc(S["ystats_ready"], 1)
                if z:
                    link(nc.vector.bn_stats(zstats[:], pair_of(xres, k - 2)))
                    nc.vector.memset(spare[:], 0.0)
                    nc.vector.bn_aggr(zmom[:], zstats[:]).then_inc(S["zstats_ready"], 1)
                if f:
                    dve.wait_ge(S["yrstd_ready"], k)
                    at_least(dve, S["yt_done"], k - 1)
                    nc.vector.tensor_scalar(yn[:], pair_of(xres, k - 1), ymom[:, 0:1], yrstd[:, 1:2],
                                            ALU.subtract, ALU.mult).then_inc(S["yn_ready"], 1)
                if z:
                    dve.wait_ge(S["zrstd_ready"], k - 1)
                    at_least(dve, S["zt_done"], k - 2)
                    nc.vector.tensor_scalar(zn[:], pair_of(xres, k - 2), zmom[:, 0:1], zrstd[:, 1:2],
                                            ALU.subtract, ALU.mult).then_inc(S["zn_ready"], 1)
                if a:
                    dve.wait_ge(S["ss_done"], k + 1)
                    link(nc.vector.tensor_scalar(rinv[:], ssp[:], 1e-24, None, ALU.max))
                    nc.vector.reciprocal(rinv[:], rinv[:]).then_inc(S["r2_ready"], 1)
                if f:
                    dve.wait_ge(S["rl_done"], k)
                    link(nc.vector.tensor_tensor(logit[:], rlp[:, FFN_LOW:NR], br[:], ALU.add))
                    nc.vector.tensor_reduce(small[:, 0:1], logit[:], AX.X, ALU.max,
                                            negate=True).then_inc(S["logit_ready"], 1)
                if z:
                    dve.wait_ge(S["z_high"], k - 1)
                    nc.vector.tensor_tensor(x_columns(kvT, k - 2, 1), ztp[:].rearrange("p (c t) -> p c t", c=HC),
                                            plain(x_columns(kvT, k - 2, 0)), ALU.subtract).then_inc(S["z_split"], 1)
                if f:
                    dve.wait_ge(S["e_done"], k)
                    link(nc.vector.reciprocal(small[:, 2:3], small[:, 1:2]))
                    link(nc.vector.tensor_scalar(share[:], e8[:], small[:, 2:3], FFN_HEADS * FFN_SCALING,
                                                 ALU.mult, ALU.mult))
                    at_least(dve, S["lt_done"], k - 1)
                    nc.vector.tensor_tensor(low[:].rearrange("p (h r) -> p h r", h=FFN_HEADS),
                                            rlp[:, 0:FFN_LOW].rearrange("p (h r) -> p h r", h=FFN_HEADS),
                                            spread(share[:], FFN_R), ALU.mult).then_inc(S["low_ready"], 1)
                if a:
                    dve.wait_ge(S["rinv_done"], k + 1)
                    link(nc.vector.scalar_tensor_tensor(scaled[:], pair_of(obuf, k), g8[:], rinv[:],
                                                        ALU.mult, ALU.mult))
                    link(nc.vector.tensor_tensor(pair_of(xres, k), pair_of(xres, k), scaled[:], ALU.add))
                if f:
                    dve.wait_ge(S["f_done"], k)
                    link(nc.vector.tensor_tensor(pair_of(xres, k - 1), fp[:], pair_of(xres, k - 1), ALU.add))
                    nc.vector.memset(small[:, 3:4], 0.0).then_inc(S["x2_ready"], 1)

            steps(lambda a, b: chain.repeat(a, b, 9), step)


def grouped_attention(nc, sems, half, const, xres, kvT, dram):
    ident, consts = const
    w_d, qk_d = dram
    STEPS = L1_KV * HP
    LAG = 3
    st = ExitStack()
    with st:
        sb = lambda name, shape, dt=FP32: st.enter_context(nc.sbuf_tensor(name, shape, dt))
        ps = lambda name: st.enter_context(nc.psum_tensor(name, [P, 512], FP32))
        w = sb("l1_w", [P, 2, 2, W_COLS], FP32R)
        raw = [sb(f"l1_raw{j}", [P, W_CHUNK]) for j in range(2)]
        qk_w, qk = sb("qk_w", [P, 2]), sb("qk", [P, 1])
        q_sq, k_sq = sb("q_sq", [P, 512]), sb("k_sq", [P, 2, P])
        q_ss, k_ss = sb("q_ss", [P, GROUP]), sb("k_ss", [P, 2])
        q_ms, k_ms = sb("q_ms", [P, GROUP]), sb("k_ms", [P, 2])
        q_r, k_r = sb("q_r", [P, GROUP]), sb("k_r", [P, 2])
        qs = sb("qs", [P, 512])
        ks = [sb(f"ks{j}", [P, 2, P]) for j in range(2)]
        v = [sb(f"v{j}", [P, 2, 2, P], FP32R) for j in range(4)]
        qT, kT = sb("l1_qT", [P, 2, GROUP * SEQ]), sb("l1_kT", [P, 2, P])
        nmax, bias = sb("nmax", [P, 4]), sb("bias", [P, 4])
        psum_, prec = sb("psums", [P, 4]), sb("prec", [P, 4])
        pe_, pn = sb("p_exp", [P, 4, P]), sb("p_norm", [P, 4, P])
        pT = sb("pT", [P, 2, 2, GROUP * SEQ], FP32R)
        oT = sb("oT", [P, 2, GROUP, P], FP32R)
        kvp, qp, qtp, ktp = ps("kvp"), ps("l1_qp"), ps("qtp"), ps("ktp")
        sp_, ptp, op, yp = ps("scp"), ps("ptp"), ps("l1_op"), ps("yp")
        S = sems
        block = st.enter_context(nc.Block())

        def slot(g):
            return g % 2

        def weights(g, part, first, count):
            sl = slot(g)
            if isinstance(sl, int):
                return w[:, sl, part, first:first + count]
            return w[:, bass.ds(sl, 1), part, first:first + count].rearrange("p s n -> p (s n)")

        def steps(repeat, step):
            for t in range(HP):
                step(0, t, [t >= lag for lag in range(LAG + 1)], True)
            with repeat(1, L1_KV - 1) as g:
                for t in range(HP):
                    step(g, t, [True] * (LAG + 1), True)
            for t in range(HP):
                step(L1_KV - 1, t, [True] * (LAG + 1), False)
            for t in range(LAG):
                step(L1_KV, t, [t < lag for lag in range(LAG + 1)], False)

        @block.sync
        def _(sp):
            sp.dma_start(qk_w[:], qk_d).then_inc(S["qk_in"], 16)

            def load(g, j):
                at_least(sp, S["w_split"], W_CHUNKS * g + j - 1)
                src = w_d[g, :, j * W_CHUNK:(j + 1) * W_CHUNK] if isinstance(g, int) else \
                    w_d[bass.ds(g, 1), :, j * W_CHUNK:(j + 1) * W_CHUNK].rearrange("g p n -> p (g n)")
                sp.dma_start(raw[j % 2][:], src).then_inc((S["w_in0"], S["w_in1"])[j % 2], 16)

            for j in range(W_CHUNKS):
                load(0, j)
            with sp.Fori(1, L1_KV) as g:
                for j in range(W_CHUNKS):
                    load(g, j)

        def chunk_in(engine, g, j):
            engine.wait_ge((S["w_in0"], S["w_in1"])[j % 2], (W_CHUNKS // 2 * g + j // 2 + 1) * 16)

        @block.tensor
        def _(pe):
            def three(out, stationary, moving, first, last):
                nc.tensor.matmul(out, stationary[0], moving[0], start=first, stop=False)
                nc.tensor.matmul(out, stationary[0], moving[1], start=False, stop=False)
                return nc.tensor.matmul(out, stationary[1], moving[0], start=False, stop=last)

            def step(g, t, on, split):
                i = HP * g + t
                if on[0]:
                    if t == 0:
                        pe.wait_ge(S["w_split"], W_CHUNKS * g + 5)
                    at_least(pe, S["k_scaled"], i)
                    for b in range(2):
                        for c in range(HC):
                            mm = three(kvp[:, b * 256:(b + 1) * 256],
                                       [kvT[:, c, t, part, b * P:(b + 1) * P] for part in range(2)],
                                       [weights(g, part, W_KV + c * 256, 256) for part in range(2)],
                                       c == 0, c == HC - 1)
                    mm.then_inc(S["kv_done"], 1)
                if on[1]:
                    pe.wait_ge(S["k_scaled"], i)
                    at_least(pe, S["kt_copied1"], i - 1)
                    for b in range(2):
                        mm = nc.tensor.transpose(ktp[:, b * P:(b + 1) * P], ks[(t - 1) % 2][:, b, :], ident[:])
                    mm.then_inc(S["kt_done"], 1)
                    pe.wait_ge(S["q_scaled"], i)
                    at_least(pe, S["qt_copied1"], i - 1)
                    for h in range(GROUP):
                        mm = nc.tensor.transpose(qtp[:, h * P:(h + 1) * P], qs[:, h * P:(h + 1) * P], ident[:])
                    mm.then_inc(S["qt_done"], 1)
                if on[0]:
                    at_least(pe, S["q_scaled"], i)
                    for c in range(HC):
                        mm = three(qp[:], [kvT[:, c, t, part, SEQ:3 * SEQ] for part in range(2)],
                                   [weights(g, part, W_Q + c * 512, 512) for part in range(2)],
                                   c == 0, c == HC - 1)
                    mm.then_inc(S["q_done"], 1)
                if on[1]:
                    pe.wait_ge(S["kt_copied1"], i)
                    pe.wait_ge(S["qt_copied1"], i)
                    at_least(pe, S["p_done"], i - 1)
                    for b in range(2):
                        for hh in range(2):
                            at = (2 * b + hh) * P
                            mm = nc.tensor.matmul(sp_[:, at:at + P], qT[:, b, hh * P:(hh + 1) * P],
                                                  kT[:, b, :], start=True, stop=True)
                    mm.then_inc(S["s_done"], 1)
                if on[2]:
                    pe.wait_ge(S["p_normed"], i - 1)
                    at_least(pe, S["pt_split"], i - 2)
                    for a in range(4):
                        mm = nc.tensor.transpose(ptp[:, a * P:(a + 1) * P], pn[:, a, :], ident[:])
                    mm.then_inc(S["pt_done"], 1)
                if on[3]:
                    og = g if t >= LAG else g - 1
                    if t == LAG:
                        pe.wait_ge(S["w_split"], W_CHUNKS * (g + 1))
                    pe.wait_ge(S["o_split"], i - 2)
                    at_least(pe, S["y_added"], i - 3)
                    for h in range(GROUP):
                        mm = three(yp[:], [oT[:, part, h, :] for part in range(2)],
                                   [weights(og, part, W_O + h * 512, 512) for part in range(2)],
                                   h == 0, h == GROUP - 1)
                    mm.then_inc(S["y_done"], 1)
                if on[2]:
                    pe.wait_ge(S["pt_split"], i - 1)
                    at_least(pe, S["o_split"], i - 2)
                    vs = v[(t - 2) % 4]
                    for b in range(2):
                        mm = three(op[:, b * 256:(b + 1) * 256], [vs[:, part, b, :] for part in range(2)],
                                   [pT[:, part, b, :] for part in range(2)], True, True)
                    mm.then_inc(S["o_done1"], 1)

            steps(pe.Fori, step)

        def by_batch(t):
            return t.rearrange("p h (b q) -> p b h q", b=2)

        def by_head(t):
            return t[:].rearrange("p (b h q) -> p b h q", b=2, h=GROUP)

        def bank(t, b=2):
            return t[:].rearrange("p (b n) -> p b n", b=b)

        @block.scalar
        def _(act):
            def split_high(g, j):
                chunk_in(act, g, j)
                nc.scalar.activation(weights(g, 0, j * W_CHUNK, W_CHUNK), raw[j % 2][:],
                                     ACT.Copy).then_inc(S["w_high"], 1)

            for j in range(W_CHUNKS):
                split_high(0, j)

            def step(g, t, on, split):
                i = HP * g + t
                if on[3]:
                    act.wait_ge(S["o_done1"], i - 2)
                    at_least(act, S["y_done"], i - 3)
                    nc.scalar.activation(by_batch(oT[:, 0, :, :]), by_head(op), ACT.Copy).then_inc(S["o_high"], 1)
                if on[0]:
                    act.wait_ge(S["kv_done"], i + 1)
                    at_least(act, S["k_summed"], i)
                    nc.scalar.activation(k_sq[:], bank(kvp)[:, :, 0:P], ACT.Square).then_inc(S["k_squared"], 1)
                    at_least(act, S["o_done1"], i - 3)
                    nc.scalar.activation(v[t % 4][:, 0, :, :], bank(kvp)[:, :, P:2 * P],
                                         ACT.Copy).then_inc(S["v_high"], 1)
                if on[1]:
                    act.wait_ge(S["kt_done"], i)
                    at_least(act, S["s_done"], i - 1)
                    nc.scalar.activation(kT[:], bank(ktp)[:, 0, :].rearrange("p (b n) -> p b n", b=2), ACT.Copy,
                                         scale=qk[:, 0:1]).then_inc(S["kt_copied1"], 1)
                    act.wait_ge(S["qt_done"], i)
                    nc.scalar.activation(qT[:].rearrange("p b (h q) -> p h b q", h=GROUP),
                                         qtp[:].rearrange("p (h b q) -> p h b q", h=GROUP, b=2),
                                         ACT.Copy).then_inc(S["qt_copied1"], 1)
                if split:
                    if t <= LAG:
                        at_least(act, S["q_done"], HP * g)
                    else:
                        at_least(act, S["y_done"], HP * g)
                    split_high(g + 1, t)
                if on[0]:
                    act.wait_ge(S["q_done"], i + 1)
                    at_least(act, S["q_summed"], i)
                    nc.scalar.activation(q_sq[:], qp[:], ACT.Square).then_inc(S["q_squared"], 1)
                if on[2]:
                    act.wait_ge(S["pt_done"], i - 1)
                    at_least(act, S["o_done1"], i - 2)
                    nc.scalar.activation(pT[:, 0, :, :].rearrange("p b n -> p (b n)"), ptp[:],
                                         ACT.Copy).then_inc(S["pt_high"], 1)
                if on[1]:
                    act.wait_ge(S["bias_ready"], i)
                    at_least(act, S["p_normed"], i - 1)
                    for a in range(4):
                        last = nc.scalar.activation(pe_[:, a, :], sp_[:, a * P:(a + 1) * P], ACT.Exp,
                                                    bias=bias[:, a:a + 1], scale=L1_SCALE,
                                                    accum_out=psum_[:, a:a + 1])
                    last.then_inc(S["p_done"], 1)

            steps(act.Fori, step)

        @block.gpsimd
        def _(pool):
            chain = Chain(pool, S["pool_chain3"])

            def split_low(g, j):
                pool.wait_ge(S["w_high"], W_CHUNKS * g + j + 1)
                nc.gpsimd.tensor_tensor(weights(g, 1, j * W_CHUNK, W_CHUNK), raw[j % 2][:],
                                        plain(weights(g, 0, j * W_CHUNK, W_CHUNK)),
                                        ALU.subtract).then_inc(S["w_split"], 1)

            for j in range(W_CHUNKS):
                split_low(0, j)

            def rms(total, mean, root, n):
                chain.link(nc.gpsimd.tensor_tensor(mean[:], total[:], consts[:, RMS_COL:RMS_COL + n], ALU.add))
                return nc.gpsimd.tensor_tensor(root[:], mean[:], consts[:, 0:n], ALU.pow)

            def step(g, t, on, split):
                i = HP * g + t
                if on[0]:
                    pool.wait_ge(S["k_summed"], i + 1)
                    rms(k_ss, k_ms, k_r, 2).then_inc(S["k_root"], 1)
                if split:
                    split_low(g + 1, t)
                if on[0]:
                    pool.wait_ge(S["q_summed"], i + 1)
                    rms(q_ss, q_ms, q_r, GROUP).then_inc(S["q_root"], 1)
                if on[1]:
                    pool.wait_ge(S["prec_ready"], i)
                    at_least(pool, S["pt_done"], i - 1)
                    nc.gpsimd.tensor_tensor(pn[:], pe_[:], spread(prec[:], P), ALU.mult).then_inc(S["p_normed"], 1)

            steps(lambda a, b: chain.repeat(a, b, 2 * HP), step)

        @block.vector
        def _(dve):
            chain = Chain(dve, S["dve_chain3"])
            link = chain.link
            dve.wait_ge(S["qk_in"], 16)
            link(nc.vector.scalar_tensor_tensor(qk[:], qk_w[:, 0:1], float(L1_DH), qk_w[:, 1:2], ALU.mult, ALU.mult))

            def step(g, t, on, split):
                i = HP * g + t
                if on[3]:
                    dve.wait_ge(S["o_high"], i - 2)
                    at_least(dve, S["y_done"], i - 3)
                    nc.vector.tensor_tensor(by_batch(oT[:, 1, :, :]), by_head(op),
                                            plain(by_batch(oT[:, 0, :, :])), ALU.subtract).then_inc(S["o_split"], 1)
                if on[0]:
                    dve.wait_ge(S["k_squared"], i + 1)
                    nc.vector.tensor_reduce(k_ss[:], k_sq[:], AX.X, ALU.add).then_inc(S["k_summed"], 1)
                    dve.wait_ge(S["v_high"], i + 1)
                    nc.vector.tensor_tensor(v[t % 4][:, 1, :, :], bank(kvp)[:, :, P:2 * P],
                                            plain(v[t % 4][:, 0, :, :]), ALU.subtract).then_inc(S["v_split"], 1)
                    dve.wait_ge(S["k_root"], i + 1)
                    nc.vector.tensor_tensor(ks[t % 2][:], bank(kvp)[:, :, 0:P], spread(k_r[:], P),
                                            ALU.mult).then_inc(S["k_scaled"], 1)
                    dve.wait_ge(S["q_squared"], i + 1)
                    nc.vector.tensor_reduce(q_ss[:], q_sq[:].rearrange("p (h d) -> p h d", h=GROUP), AX.X,
                                            ALU.add).then_inc(S["q_summed"], 1)
                if on[1]:
                    dve.wait_ge(S["s_done"], i)
                    link(nc.vector.tensor_reduce(nmax[:], sp_[:].rearrange("p (a k) -> p a k", a=4), AX.X,
                                                 ALU.max, negate=True))
                    nc.vector.tensor_scalar(bias[:], nmax[:], L1_SCALE, None, ALU.mult).then_inc(S["bias_ready"], 1)
                if on[0]:
                    dve.wait_ge(S["q_root"], i + 1)
                    nc.vector.tensor_tensor(qs[:].rearrange("p (h d) -> p h d", h=GROUP),
                                            qp[:].rearrange("p (h d) -> p h d", h=GROUP), spread(q_r[:], P),
                                            ALU.mult).then_inc(S["q_scaled"], 1)
                if on[2]:
                    dve.wait_ge(S["pt_high"], i - 1)
                    nc.vector.tensor_tensor(pT[:, 1, :, :].rearrange("p b n -> p (b n)"), ptp[:],
                                            plain(pT[:, 0, :, :].rearrange("p b n -> p (b n)")),
                                            ALU.subtract).then_inc(S["pt_split"], 1)
                if on[1]:
                    dve.wait_ge(S["p_done"], i)
                    nc.vector.reciprocal(prec[:], psum_[:]).then_inc(S["prec_ready"], 1)
                if on[3]:
                    dve.wait_ge(S["y_done"], i - 2)
                    at = xres[:, (t - LAG) % HP, :]
                    nc.vector.tensor_tensor(at, yp[:], at, ALU.add).then_inc(S["y_added"], 1)

            steps(lambda a, b: chain.repeat(a, b, HP), step)


def quantised_ffn(nc, sems, half, const, xres, dram, out):
    ident, consts = const
    wq_d, sc_d = dram
    st = ExitStack()
    with st:
        sb = lambda name, shape, dt=FP32: st.enter_context(nc.sbuf_tensor(name, shape, dt))
        ps = lambda name: st.enter_context(nc.psum_tensor(name, [P, 512], FP32))
        wq, sc, wf = sb("f1_wq", [P, HC * HIDDEN], INT32), sb("f1_sc", [P, HC * HIDDEN]), sb("f1_w", [P, HC * HIDDEN])
        w_h, w_l = sb("f1_wh", [P, HC * HIDDEN], FP32R), sb("f1_wl", [P, HC * HIDDEN], FP32R)
        u = sb("u", [P, HIDDEN])
        uT_h, uT_l = sb("uT_h", [P, HIDDEN], FP32R), sb("uT_l", [P, HIDDEN], FP32R)
        ustats, umom, urstd = sb("ustats", [P, 6]), sb("umom", [P, 2]), sb("urstd", [P, 2])
        spare = sb("spare3", [P, 1])
        utp, fp = ps("utp"), ps("f1p")
        S = sems
        block = st.enter_context(nc.Block())

        def steps(repeat, step):
            step(0, True, False)
            step(1, True, True)
            with repeat(2, HP) as k:
                step(k, True, True)
            step(HP, False, True)

        @block.sync
        def _(sp):
            sp.dma_start(wq[:], wq_d).then_inc(S["u_in"], 16)
            sp.dma_start(sc[:], sc_d).then_inc(S["u_in"], 16)
            with sp.Fori(0, HP) as k:
                sp.wait_ge(S["out_ready"], k + 1)
                sp.dma_start(out[bass.ds((half * HP + k) * P, P), :], pair_of(xres, k)).then_inc(S["stored"], 16)
            sp.wait_ge(S["stored"], 16 * HP)

        @block.tensor
        def _(pe):
            pe.wait_ge(S["u_ready"], 1)

            def step(k, ln, ff):
                if ff:
                    pe.wait_ge(S["ut_split"], k)
                    at_least(pe, S["out_ready"], k - 1)
                    for c in range(HC):
                        xc, wc = slice(c * P, (c + 1) * P), slice(c * HIDDEN, (c + 1) * HIDDEN)
                        nc.tensor.matmul(fp[:], uT_h[:, xc], w_h[:, wc], start=(c == 0), stop=False)
                        nc.tensor.matmul(fp[:], uT_h[:, xc], w_l[:, wc], start=False, stop=False)
                        mm = nc.tensor.matmul(fp[:], uT_l[:, xc], w_h[:, wc], start=False, stop=(c == HC - 1))
                    mm.then_inc(S["uf_done"], 1)
                if ln:
                    pe.wait_ge(S["un_ready"], k + 1)
                    at_least(pe, S["ut_split"], k)
                    for c in range(HC):
                        mm = nc.tensor.transpose(utp[:, c * P:(c + 1) * P], u[:, c * P:(c + 1) * P], ident[:])
                    mm.then_inc(S["ut_done"], 1)

            steps(pe.Fori, step)

        @block.scalar
        def _(act):
            def step(k, ln, ff):
                if ln:
                    act.wait_ge(S["ut_done"], k + 1)
                    at_least(act, S["uf_done"], k)
                    nc.scalar.activation(uT_h[:], utp[:], ACT.Copy).then_inc(S["ut_high"], 1)

            steps(act.Fori, step)

        @block.gpsimd
        def _(pool):
            chain = Chain(pool, S["pool_chain4"])

            def step(k, ln, ff):
                if ln:
                    pool.wait_ge(S["ustats_ready"], k + 1)
                    chain.link(nc.gpsimd.tensor_tensor(urstd[:, 0:1], umom[:, 1:2], consts[:, LN_COL:LN_COL + 1], ALU.add))
                    nc.gpsimd.tensor_tensor(urstd[:, 1:2], urstd[:, 0:1], consts[:, 0:1],
                                            ALU.pow).then_inc(S["urstd_ready"], 1)

            steps(lambda a, b: chain.repeat(a, b, 1), step)

        @block.vector
        def _(dve):
            chain = Chain(dve, S["dve_chain4"])
            link = chain.link

            def ln_stats(k):
                link(nc.vector.bn_stats(ustats[:], pair_of(xres, k)))
                nc.vector.memset(spare[:], 0.0)
                nc.vector.bn_aggr(umom[:], ustats[:]).then_inc(S["ustats_ready"], 1)

            ln_stats(0)
            dve.wait_ge(S["u_in"], 32)
            link(nc.vector.scalar_tensor_tensor(wf[:], wq[:], -128.0, sc[:], ALU.add, ALU.mult))
            link(nc.vector.tensor_copy(w_h[:], wf[:]))
            nc.vector.tensor_tensor(w_l[:], wf[:], plain(w_h[:]), ALU.subtract).then_inc(S["u_ready"], 1)

            def step(k, ln, ff, more=True):
                if ln:
                    dve.wait_ge(S["urstd_ready"], k + 1)
                    at_least(dve, S["ut_done"], k)
                    nc.vector.tensor_scalar(u[:], pair_of(xres, k), umom[:, 0:1], urstd[:, 1:2],
                                            ALU.subtract, ALU.mult).then_inc(S["un_ready"], 1)
                    if more:
                        dve.wait_ge(S["un_ready"], k + 1)
                        ln_stats(k + 1)
                if ff:
                    dve.wait_ge(S["uf_done"], k)
                    nc.vector.tensor_tensor(pair_of(xres, k - 1), fp[:], pair_of(xres, k - 1),
                                            ALU.add).then_inc(S["out_ready"], 1)
                if ln:
                    dve.wait_ge(S["ut_high"], k + 1)
                    nc.vector.tensor_tensor(uT_l[:], utp[:], plain(uT_h[:]), ALU.subtract).then_inc(S["ut_split"], 1)

            step(0, True, False)
            step(1, True, True)
            with chain.repeat(2, HP - 1, 1) as k:
                step(k, True, True)
            step(HP - 1, True, True, more=False)
            step(HP, False, True)


A1_SEMS = """w_in x_first x_rest c_in0 c_in1 ct_in0 ct_in1 wvo_done w_ready stats_ready rstd_ready
    xn_ready x_high c_high x_stacked c_stacked k_proj q_proj k_max k_exp q_max q_sub q_exp q_rec
    q_norm tk_done tq_done kt_copied qt_copied ct_high ct_split g_step g_copied m_done m_scaled
    krec_done o_done o_stored dve_chain pool_chain"""
A2_SEMS = """f_in f_ready sq_done ss_done r2_ready rinv_done yn_ready yt_done yt_copied rl_done
    logit_ready e_done low_ready lt_done lt_copied f_done x2_ready zn_ready zt_done z_high z_split
    ystats_ready yrstd_ready zstats_ready zrstd_ready dve_chain2 pool_chain2"""
B_SEMS = """qk_in w_in0 w_in1 w_high w_split kv_done q_done kt_done qt_done s_done pt_done y_done
    o_done1 k_squared k_summed k_root k_scaled q_squared q_summed q_root q_scaled v_high v_split
    kt_copied1 qt_copied1 bias_ready p_done prec_ready p_normed pt_high pt_split o_high o_split
    y_added dve_chain3 pool_chain3"""
C_SEMS = """u_in u_ready ustats_ready urstd_ready un_ready ut_done ut_high ut_split uf_done
    out_ready stored dve_chain4 pool_chain4"""


def build(nc, x, ctx, ctx_t, l0_wq, l0_wk, l0_wv, l0_wo, l0_bo, l0_g, ffn_in, ffn_out, ffn_br, l1_w, l1_qk,
          f1_wq, f1_sc, out):
    with ExitStack() as st:
        xres = st.enter_context(nc.sbuf_tensor("xres", [P, HP, HIDDEN], FP32))
        kvT = st.enter_context(nc.sbuf_tensor("kvT", [P, HC, HP, 2, 2 * P], FP32R))
        ident = st.enter_context(nc.sbuf_tensor("ident", [P, P], FP32))
        consts = st.enter_context(nc.sbuf_tensor("consts", [P, RMS_COL + GROUP], FP32))
        made = st.enter_context(nc.semaphore("const_made"))
        a1, a2 = semaphores(nc, st, A1_SEMS), semaphores(nc, st, A2_SEMS)
        b_, c_ = semaphores(nc, st, B_SEMS), semaphores(nc, st, C_SEMS)
        const = (ident, consts)
        with nc.Block() as block:
            @block.gpsimd
            def _(pool):
                nc.gpsimd.memset(consts[:, 0:LN_COL], -0.5)
                nc.gpsimd.memset(consts[:, LN_COL:RMS_COL], LN_EPS)
                nc.gpsimd.memset(consts[:, RMS_COL:], L1_DH * RMS_EPS)
                nc.gpsimd.memset(ident[:], 0.0).then_inc(made, 1)
                pool.wait_ge(made, 1)
                nc.gpsimd.affine_select(out=ident[:], in_=ident[:], compare_op=ALU.not_equal, fill=1.0, base=0,
                                        pattern=[[-1, P]], channel_multiplier=1).then_inc(made, 1)
                pool.wait_ge(made, 2)
        with nc.Fori(0, HALVES) as half:
            with nc.sbuf_tensor("obuf", [P, HP, HIDDEN], FP32) as obuf:
                linear_attention(nc, a1, half, const, xres, kvT, obuf,
                                 (x, ctx, ctx_t, l0_wq, l0_wk, l0_wv, l0_wo, l0_bo))
                clear(nc, a1)
                norm_and_ffn(nc, a2, const, xres, kvT, obuf, (l0_g, ffn_in, ffn_out, ffn_br))
                clear(nc, a2)
            grouped_attention(nc, b_, half, const, xres, kvT, (l1_w, l1_qk))
            clear(nc, b_)
            quantised_ffn(nc, c_, half, const, xres, (f1_wq, f1_sc), out)
            clear(nc, c_)


def kernel(**inputs):
    import numpy as _np
    import concourse.bacc as _bacc
    from concourse import mybir as _mybir
    from concourse.bass_utils import run_bass_kernel_spmd as _run

    a = {k: _np.asarray(v) for k, v in inputs.items()}
    x = a["x"].reshape(BATCHES * SEQ, HIDDEN)
    ctx = a["ctx_4096"].reshape(BATCHES * SEQ, HIDDEN)
    ctx_t = a["ctx_4096"].reshape(BATCHES, SEQ, HC, P).transpose(0, 3, 2, 1).reshape(BATCHES, P, HC * SEQ)
    twice = lambda w: _np.concatenate([w, w], axis=0)
    by_chunk = lambda w: w.reshape(-1, P, w.shape[-1]).transpose(1, 0, 2)
    ffn_in = by_chunk(_np.concatenate([a["L0_ffn_A"].reshape(FFN_LOW, HIDDEN), a["L0_ffn_Wr"]], axis=0).T)
    wq, wk, wv = (by_chunk(a[f"L1_xattn_{n}"]) for n in ("Wq", "Wk", "Wv"))
    wo = a["L1_xattn_Wo"].reshape(L1_HEADS, L1_DH, HIDDEN)
    groups = []
    for g in range(L1_KV):
        kv = slice(g * L1_DH, (g + 1) * L1_DH)
        q = slice(g * GROUP * L1_DH, (g + 1) * GROUP * L1_DH)
        groups.append(_np.concatenate([
            _np.concatenate([wk[:, :, kv], wv[:, :, kv]], axis=2).reshape(P, -1),
            wq[:, :, q].reshape(P, -1),
            wo[g * GROUP:(g + 1) * GROUP].transpose(1, 0, 2).reshape(P, -1)], axis=1))
    ins = {
        "x": x, "ctx": ctx, "ctx_t": ctx_t,
        "l0_wq": twice(a["L0_xattn_Wq"].T), "l0_wk": twice(a["L0_xattn_Wk"].T),
        "l0_wv": by_chunk(a["L0_xattn_Wv"]), "l0_wo": by_chunk(a["L0_xattn_Wo"].T),
        "l0_bo": twice(a["L0_xattn_bo"].reshape(SEQ, 1)), "l0_g": twice(a["L0_xattn_g"].reshape(SEQ, 1)),
        "ffn_in": ffn_in, "ffn_out": a["L0_ffn_B"].transpose(0, 2, 1).reshape(FFN_LOW, HIDDEN),
        "ffn_br": _np.repeat(a["L0_ffn_br"].reshape(1, FFN_HEADS), P, axis=0),
        "l1_w": _np.stack(groups),
        "l1_qk": _np.stack([a["L1_xattn_q_norm_w"], a["L1_xattn_k_norm_w"]], axis=1),
        "f1_wq": by_chunk(a["L1_ffn_w_q"].T).reshape(P, -1),
        "f1_sc": by_chunk(_np.repeat(a["L1_ffn_scales"].T, HIDDEN // a["L1_ffn_scales"].shape[1], axis=0)).reshape(P, -1),
    }
    ins = {k: _np.ascontiguousarray(v) for k, v in ins.items()}
    nc = _bacc.Bacc("TRN2", target_bir_lowering=False, num_devices=1)
    args = [nc.dram_tensor(f"in_{k}", v.shape, _mybir.dt.from_np(v.dtype), kind="ExternalInput").ap()
            for k, v in ins.items()]
    out = nc.dram_tensor("out", (BATCHES * SEQ, HIDDEN), FP32, kind="ExternalOutput").ap()
    build(nc, *args, out)
    r = _run(nc, [{f"in_{k}": v for k, v in ins.items()}], core_ids=[0])
    return r.results[0]["out"].reshape(BATCHES, SEQ, HIDDEN)
```

```python
import math
from contextlib import ExitStack, contextmanager

import concourse.bass as bass
from concourse import mybir

P = 128
FP32 = mybir.dt.float32
FP32R = mybir.dt.float32r
INT32 = mybir.dt.int32
ALU = mybir.AluOpType
ACT = mybir.ActivationFunctionType
AX = mybir.AxisListType

BATCHES, SEQ, HIDDEN = 32, 64, 512
HC = HIDDEN // P
HALVES = 2
HB = BATCHES // HALVES
HP = HB // 2
L0_HEADS, L0_DH = 8, 64
FFN_HEADS, FFN_R, FFN_SCALING = 8, 16, 32 / 16
FFN_LOW = FFN_HEADS * FFN_R
L1_HEADS, L1_KV, L1_DH = 32, 8, 128
GROUP = L1_HEADS // L1_KV
L1_SCALE = 1.0 / math.sqrt(L1_DH)
LN_EPS, RMS_EPS = 1e-5, 1e-6
LN_COL = max(GROUP, 2 * HC)
RMS_COL, MINUS_COL = LN_COL + 1, LN_COL + 1 + GROUP
W_KV, W_Q, W_O = 0, HC * 2 * L1_DH, HC * 2 * L1_DH + HC * GROUP * L1_DH
W_COLS = W_O + GROUP * HIDDEN
W_CHUNKS = HP
W_CHUNK = W_COLS // W_CHUNKS


def at_least(engine, sem, value):
    if not (isinstance(value, int) and value <= 0):
        engine.wait_ge(sem, value)


class Chain:

    def __init__(self, engine, sem):
        self.engine, self.sem, self.count, self.base = engine, sem, 0, 0

    def link(self, instruction):
        instruction.then_inc(self.sem, 1)
        self.count += 1
        self.engine.wait_ge(self.sem, self.base + self.count)

    @contextmanager
    def repeat(self, first, end, links):
        before = self.count
        with self.engine.Fori(first, end) as i:
            self.base = (i - first) * links
            yield i
            assert self.count - before == links, f"{self.count - before} links"
        self.base, self.count = 0, before + links * (end - first)


def plain(ap):
    return ap.bitcast(FP32)


def spread(ap, n):
    return ap.unsqueeze(len(ap.shape)).to_broadcast([*ap.shape, n])


def semaphores(nc, stack, names):
    made = {name: stack.enter_context(nc.semaphore(name)) for name in names.split()}
    numbers = [s.num for s in made.values()]
    assert numbers == list(range(numbers[0], numbers[0] + len(numbers)))
    return made


def clear(nc, sems):
    first = min(s.num for s in sems.values())
    nc.all_engine_barrier(sems_to_clear=range(first, first + len(sems)))


def inverse_root(nc, chain, mom, r, consts):
    chain.link(nc.gpsimd.tensor_tensor(r[:, 0:1], mom[:, 1:2], consts[:, LN_COL:LN_COL + 1], ALU.add))
    chain.link(nc.gpsimd.tensor_tensor(r[:, 1:2], r[:, 0:1], consts[:, 0:1], ALU.pow))
    chain.link(nc.gpsimd.tensor_tensor(r[:, 0:1], mom[:, 0:1], r[:, 1:2], ALU.mult))
    return nc.gpsimd.tensor_tensor(r[:, 2:3], r[:, 0:1], consts[:, MINUS_COL:MINUS_COL + 1], ALU.mult)


def linear_attention(nc, sems, half, const, xres, kvT, obuf, dram):
    ident, consts = const
    x, ctx, ctx_t, wq_d, wk_d, wv_d, wo_d, bo_d = dram
    st = ExitStack()
    with st:
        sb = lambda name, shape, dt=FP32: st.enter_context(nc.sbuf_tensor(name, shape, dt))
        ps = lambda name: st.enter_context(nc.psum_tensor(name, [P, 512], FP32))
        wq_h, wq_l = sb("l0_wq_h", [P, HIDDEN], FP32R), sb("l0_wq_l", [P, HIDDEN], FP32R)
        wk_h, wk_l = sb("l0_wk_h", [P, HIDDEN], FP32R), sb("l0_wk_l", [P, HIDDEN], FP32R)
        wvo = sb("l0_wvo", [P, HIDDEN])
        bo = sb("l0_bo", [P, 1])
        x_st = [sb(f"x_stack{s}", [P, HIDDEN], FP32R) for s in range(2)]
        c_st = [sb(f"c_stack{s}", [P, HIDDEN], FP32R) for s in range(2)]
        xn = sb("xn", [P, HIDDEN])
        cn = sb("cn", [P, HIDDEN])
        cT = [sb(f"cT{s}", [P, HC, SEQ]) for s in range(2)]
        kexp = [sb(f"kexp{s}", [P, HC, HIDDEN]) for s in range(2)]
        qn = [sb(f"qn{s}", [P, HC, HIDDEN]) for s in range(2)]
        kT = [sb(f"kT{j}", [P, HIDDEN]) for j in range(2)]
        qT = [sb(f"qT{s}", [P, HC, HIDDEN]) for s in range(2)]
        gsb = sb("gsb", [P, HIDDEN])
        mT = [sb(f"mT{s}", [P, HC, SEQ]) for s in range(2)]
        stats, moments, rstd = sb("stats", [P, 6]), sb("moments", [P, 2]), sb("rstd", [P, 2])
        spare = sb("spare1", [P, 1])
        knmax, ksum, krec = (sb(n_, [P, 2, HC]) for n_ in ("knmax", "ksum", "krec"))
        qnmax, qsum = sb("qnmax", [P, HC, L0_HEADS]), sb("qsum", [P, HC, L0_HEADS])
        qrec = sb("qrec", [P, 2, HC, L0_HEADS])
        kp = [ps(f"kp{j}") for j in range(2)]
        qp = [ps(f"qp{j}") for j in range(2)]
        tkp, tqp, gmp, op = ps("tkp"), ps("tqp"), ps("gmp"), ps("op")
        S = sems

        wq_raw, wk_raw = kexp[0][:, 0, :], kexp[0][:, 1, :]
        wv_raw = kexp[1][:, 0, 0:HC * L0_DH].rearrange("p (c e) -> p c e", c=HC)
        wo_raw = kexp[1][:, 1, 0:HC * L0_DH].rearrange("p (c e) -> p c e", c=HC)

        def num(b):
            return 2 * b[0] + b[1]

        def before(b):
            return (b[0] - 1, 1) if b[1] == 0 else (b[0], 0)

        def after(b):
            return (b[0], 1) if b[1] == 0 else (b[0] + 1, 0)

        def rows(s):
            return slice(s * SEQ, s * SEQ + SEQ)

        def heads(t):
            return t.rearrange("p (h d) -> p h d", h=L0_HEADS)

        PEEL = 2

        def steps(repeat, step):
            for p in range(PEEL):
                for s in range(2):
                    step((p, s), True, 2 * p + s >= 1, 2 * p + s >= 2, True)
            with repeat(PEEL, HP - 1) as p:
                for s in range(2):
                    step((p, s), True, True, True, True)
            step((HP - 1, 0), True, True, True, True)
            step((HP - 1, 1), True, True, True, False)
            step((HP, 0), False, True, True, False)
            step((HP, 1), False, False, True, False)

        block = st.enter_context(nc.Block())

        @block.sync
        def _(sp):
            sp.dma_start(xres[:, 0:1, :], x[bass.ds(half * HP * P, P), :].rearrange(
                "(t p) n -> p t n", p=P)).then_inc(S["x_first"], 16)

            def load_c(b):
                at_least(sp, S["c_stacked"], num(b) - 1)
                sp.dma_start(cn[rows(b[1]), :], ctx[bass.ds((half * HB + num(b)) * SEQ, SEQ), :]).then_inc(
                    (S["c_in0"], S["c_in1"])[b[1]], 16)

            def load_ct(b):
                at_least(sp, S["g_step"], HC * (num(b) - 1))
                at_least(sp, S["ct_split"], num(b) - 1)
                sp.dma_start(cT[b[1]][:], ctx_t[bass.ds(half * HB + num(b), 1), :, :].rearrange(
                    "b p (c t) -> p (b c) t", c=HC)).then_inc((S["ct_in0"], S["ct_in1"])[b[1]], 16)

            load_c((0, 0))
            for dst, src in ((wq_raw, wq_d), (wk_raw, wk_d), (wv_raw, wv_d), (wo_raw, wo_d), (bo[:], bo_d)):
                sp.dma_start(dst, src).then_inc(S["w_in"], 16)
            sp.dma_start(xres[:, 1:HP, :], x[bass.ds(half * HP * P + P, (HP - 1) * P), :].rearrange(
                "(t p) n -> p t n", p=P)).then_inc(S["x_rest"], 16)
            for p in range(PEEL):
                for s in range(2):
                    load_c(after((p, s)))
                    load_ct((p, s))
            with sp.Fori(PEEL, HP - 1) as p:
                for s in range(2):
                    load_c(after((p, s)))
                    load_ct((p, s))
            load_c((HP - 1, 1))
            load_ct((HP - 1, 0))
            load_ct((HP - 1, 1))

        @block.tensor
        def _(pe):
            pe.wait_ge(S["w_in"], 80)
            for r, bank in ((0, kp[0]), (1, kp[1])):
                for c in range(HC):
                    last = nc.tensor.matmul(bank[0:SEQ, c * L0_DH:(c + 1) * L0_DH], wv_raw[rows(r), c, :],
                                            wo_raw[rows(r), c, :], start=True, stop=True)
            last.then_inc(S["wvo_done"], 1)
            pe.wait_ge(S["w_ready"], 1)

            def project(b, j):
                n, s, cols = num(b), b[1], slice(j * P, (j + 1) * P)
                if j == 0:
                    pe.wait_ge(S["c_stacked"], n + 1)
                    pe.wait_ge(S["x_stacked"], n + 1)
                at_least(pe, S["k_exp"], HC * n + j - 1)
                nc.tensor.matmul(kp[j % 2][:], wk_h[:, cols], c_st[s][:], start=True, stop=False)
                nc.tensor.matmul(kp[j % 2][:], wk_l[:, cols], c_st[s][:], start=False,
                                 stop=True).then_inc(S["k_proj"], 1)
                at_least(pe, S["q_sub"], HC * n + j - 1)
                nc.tensor.matmul(qp[j % 2][:], x_st[s][:, cols], wq_h[:], start=True, stop=False)
                nc.tensor.matmul(qp[j % 2][:], x_st[s][:, cols], wq_l[:], start=False,
                                 stop=True).then_inc(S["q_proj"], 1)

            def transpose_q(m, ms, j):
                if j == 0:
                    pe.wait_ge(S["q_norm"], HC * (m + 1))
                at_least(pe, S["qt_copied"], HC * m + j)
                for c in range(HC):
                    mm = nc.tensor.transpose(tqp[:, c * P:(c + 1) * P], qn[ms][:, c, j * P:(j + 1) * P], ident[:])
                mm.then_inc(S["tq_done"], 1)

            def transpose_k(m, ms, j):
                if j == 0:
                    pe.wait_ge(S["k_exp"], HC * (m + 1))
                at_least(pe, S["kt_copied"], HC * m + j)
                for c in range(HC):
                    mm = nc.tensor.transpose(tkp[:, c * P:(c + 1) * P], kexp[ms][:, c, j * P:(j + 1) * P], ident[:])
                mm.then_inc(S["tk_done"], 1)

            def context(b, m, ms, j):
                if j == 0:
                    pe.wait_ge((S["ct_in0"], S["ct_in1"])[ms], 16 * (before(b)[0] + 1))
                    at_least(pe, S["m_scaled"], m)
                pe.wait_ge(S["kt_copied"], HC * m + j + 1)
                nc.tensor.matmul(gmp[0:SEQ, :], cT[ms][:, j, :], kT[j % 2][:], start=(j == 0),
                                 stop=(j == HC - 1)).then_inc(S["g_step"], 1)

            project((0, 0), 0)

            def step(b, front, back, last_, more):
                n, s = num(b), b[1]
                m, ms = n - 1, 1 - s
                o = n - 2
                for j in range(HC):
                    if last_ and j == 0:
                        transpose_q(o, s, HC - 1)
                    if back and j >= 1:
                        transpose_q(m, ms, j - 1)
                    if back:
                        transpose_k(m, ms, j)
                    if last_ and j == 0:
                        pe.wait_ge(S["g_copied"], o + 1)
                        for c in range(HC):
                            mm = nc.tensor.matmul(gmp[:, c * P:(c + 1) * P], gsb[:, c * P:(c + 1) * P],
                                                  wvo[:, c * P:(c + 1) * P], start=True, stop=True)
                        mm.then_inc(S["m_done"], 1)
                    if front and j < HC - 1:
                        project(b, j + 1)
                    if more and j == HC - 1:
                        project(after(b), 0)
                    if last_ and j == 2:
                        pe.wait_ge(S["m_scaled"], o + 1)
                        pe.wait_ge(S["qt_copied"], HC * (o + 1))
                        at_least(pe, S["o_stored"], o)
                        for c in range(HC):
                            mm = nc.tensor.matmul(op[rows(s), :], mT[s][:, c, :], qT[s][:, c, :], start=(c == 0),
                                                  stop=(c == HC - 1))
                        mm.then_inc(S["o_done"], 1)
                    if back and j >= 1:
                        context(b, m, ms, j - 1)
                if back:
                    context(b, m, ms, HC - 1)

            steps(pe.Fori, step)

        @block.scalar
        def _(act):
            def stack_high(b):
                s, r = b[1], rows(b[1])
                act.wait_ge(S["xn_ready"], b[0] + 1)
                at_least(act, S["q_proj"], HC * (num(b) - 1))
                nc.scalar.activation(x_st[s][r, :], xn[r, :], ACT.Copy).then_inc(S["x_high"], 1)
                act.wait_ge((S["c_in0"], S["c_in1"])[s], 16 * (b[0] + 1))
                nc.scalar.activation(c_st[s][r, :], cn[r, :], ACT.Copy).then_inc(S["c_high"], 1)

            act.wait_ge(S["w_ready"], 1)
            stack_high((0, 0))

            def copy_q(m, ms, j):
                act.wait_ge(S["tq_done"], HC * m + j + 1)
                at_least(act, S["o_done"], m - 1)
                nc.scalar.activation(qT[ms][:, j, :], tqp[:], ACT.Copy).then_inc(S["qt_copied"], 1)

            def step(b, front, back, last_, more):
                n, s = num(b), b[1]
                m, ms = n - 1, 1 - s
                o = n - 2
                for j in range(HC):
                    if last_ and j == 0:
                        copy_q(o, s, HC - 1)
                    if back and j >= 1:
                        copy_q(m, ms, j - 1)
                    if back:
                        act.wait_ge(S["tk_done"], HC * m + j + 1)
                        at_least(act, S["g_step"], HC * m + j - 1)
                        nc.scalar.activation(kT[j % 2][:], tkp[:], ACT.Copy).then_inc(S["kt_copied"], 1)
                    if front:
                        if j == 0:
                            at_least(act, S["tk_done"], HC * (n - 1))
                            at_least(act, S["krec_done"], n - 1)
                        act.wait_ge(S["k_max"], HC * n + j + 1)
                        nc.scalar.activation(kexp[s][:, j, :], kp[j % 2][:], ACT.Exp, bias=knmax[:, s, j:j + 1],
                                             accum_out=ksum[:, s, j:j + 1]).then_inc(S["k_exp"], 1)
                        act.wait_ge(S["q_sub"], HC * n + j + 1)
                        nc.scalar.activation(qn[s][:, j, :], qn[s][:, j, :], ACT.Exp).then_inc(S["q_exp"], 1)
                    if more and j == 1:
                        stack_high(after(b))
                    if back and j == 2:
                        act.wait_ge((S["ct_in0"], S["ct_in1"])[ms], 16 * (before(b)[0] + 1))
                        nc.scalar.activation(context_columns(kvT, before(b), 0), cT[ms][:],
                                             ACT.Copy).then_inc(S["ct_high"], 1)
                if last_:
                    act.wait_ge(S["o_done"], o + 1)
                    nc.scalar.activation(pair_rows(obuf, b[0] - 1, rows(s)), op[rows(s), :], ACT.Identity,
                                         bias=bo[rows(s), :]).then_inc(S["o_stored"], 1)
                if back:
                    act.wait_ge(S["g_step"], HC * (m + 1))
                    at_least(act, S["m_done"], m)
                    nc.scalar.activation(gsb[0:SEQ, :], gmp[0:SEQ, :], ACT.Copy).then_inc(S["g_copied"], 1)

            steps(act.Fori, step)

        @block.vector
        def _(dve):
            chain = Chain(dve, S["dve_chain"])
            link = chain.link

            def layer_stats(p):
                link(nc.vector.bn_stats(stats[:], pair_of(xres, p)))
                nc.vector.memset(spare[:], 0.0)
                nc.vector.bn_aggr(moments[:], stats[:]).then_inc(S["stats_ready"], 1)

            def normalise(p):
                dve.wait_ge(S["rstd_ready"], p + 1)
                nc.vector.tensor_scalar(xn[:], pair_of(xres, p), moments[:, 0:1], rstd[:, 1:2],
                                        ALU.subtract, ALU.mult).then_inc(S["xn_ready"], 1)

            def stack_low(b):
                s, r, other = b[1], rows(b[1]), rows(1 - b[1])
                dve.wait_ge(S["x_high"], num(b) + 1)
                nc.vector.tensor_tensor(x_st[s][other, :], xn[r, :], plain(x_st[s][r, :]),
                                        ALU.subtract).then_inc(S["x_stacked"], 1)
                dve.wait_ge(S["c_high"], num(b) + 1)
                nc.vector.tensor_tensor(c_st[s][other, :], cn[r, :], plain(c_st[s][r, :]),
                                        ALU.subtract).then_inc(S["c_stacked"], 1)

            dve.wait_ge(S["x_first"], 16)
            layer_stats(0)
            dve.wait_ge(S["w_in"], 80)
            nc.vector.memset(wvo[SEQ:P, :], 0.0)
            nc.vector.memset(gsb[SEQ:P, :], 0.0)
            nc.vector.tensor_copy(wq_h[:], wq_raw)
            link(nc.vector.tensor_copy(wk_h[:], wk_raw))
            nc.vector.tensor_tensor(wq_l[:], wq_raw, plain(wq_h[:]), ALU.subtract)
            nc.vector.tensor_tensor(wk_l[:], wk_raw, plain(wk_h[:]), ALU.subtract)
            normalise(0)
            dve.wait_ge(S["wvo_done"], 1)
            by_head = wvo[0:SEQ, :].rearrange("p (c r o) -> p c r o", c=HC, r=2)
            for r in range(2):
                last = nc.vector.tensor_scalar(by_head[:, :, r, :],
                                               kp[r][0:SEQ, 0:HC * L0_DH].rearrange("p (c o) -> p c o", c=HC),
                                               L0_DH ** -0.5, None, ALU.mult)
            link(last)
            nc.vector.memset(krec[:], 0.0).then_inc(S["w_ready"], 1)
            stack_low((0, 0))
            dve.wait_ge(S["x_rest"], 16)

            def q_sum(n, s, j):
                dve.wait_ge(S["q_exp"], HC * n + j + 1)
                link(nc.vector.tensor_reduce(qsum[:, j, :], heads(qn[s][:, j, :]), AX.X, ALU.add))
                nc.vector.reciprocal(qrec[:, s, j, :], qsum[:, j, :]).then_inc(S["q_rec"], 1)

            def step(b, front, back, last_, more):
                n, s = num(b), b[1]
                m, ms = n - 1, 1 - s
                o = n - 2
                if more and s == 1:
                    layer_stats(b[0] + 1)
                for j in range(HC):
                    if front:
                        dve.wait_ge(S["q_proj"], HC * n + j + 1)
                        nc.vector.tensor_reduce(knmax[:, s, j:j + 1], kp[j % 2][:], AX.X, ALU.max,
                                                negate=True).then_inc(S["k_max"], 1)
                        nc.vector.tensor_reduce(qnmax[:, j, :], heads(qp[j % 2][:]), AX.X, ALU.max,
                                                negate=True).then_inc(S["q_max"], 1)
                        dve.wait_ge(S["q_max"], HC * n + j + 1)
                        if j == 0:
                            at_least(dve, S["tq_done"], HC * (n - 1))
                        nc.vector.tensor_tensor(heads(qn[s][:, j, :]), heads(qp[j % 2][:]),
                                                spread(qnmax[:, j, :], L0_DH), ALU.add).then_inc(S["q_sub"], 1)
                    if back and j == 0:
                        dve.wait_ge(S["k_exp"], HC * (m + 1))
                        nc.vector.reciprocal(krec[:, ms, :], ksum[:, ms, :]).then_inc(S["krec_done"], 1)
                    if last_ and j == 0:
                        dve.wait_ge(S["m_done"], o + 1)
                        dve.wait_ge(S["krec_done"], o + 1)
                        at_least(dve, S["o_done"], o - 1)
                        for r in range(2):
                            mm = nc.vector.tensor_tensor(
                                mT[s][rows(r), :, :],
                                gmp[rows(r), :].rearrange("p (c r o) -> p c r o", c=HC, r=2)[:, :, r, :],
                                spread(krec[rows(r), s, :], SEQ), ALU.mult)
                        mm.then_inc(S["m_scaled"], 1)
                    if more and s == 1 and j == 0:
                        normalise(b[0] + 1)
                    if more and j == 2:
                        stack_low(after(b))
                    if front and j >= 1:
                        q_sum(n, s, j - 1)
                if front:
                    q_sum(n, s, HC - 1)

            steps(lambda a, b: chain.repeat(a, b, 1 + 2 * HC), step)

        @block.gpsimd
        def _(pool):
            chain = Chain(pool, S["pool_chain"])

            def layer_rstd(p):
                pool.wait_ge(S["stats_ready"], p + 1)
                chain.link(nc.gpsimd.tensor_tensor(rstd[:, 0:1], moments[:, 1:2], consts[:, LN_COL:LN_COL + 1],
                                                   ALU.add))
                nc.gpsimd.tensor_tensor(rstd[:, 1:2], rstd[:, 0:1], consts[:, 0:1],
                                        ALU.pow).then_inc(S["rstd_ready"], 1)

            layer_rstd(0)

            def step(b, front, back, last_, more):
                n, s = num(b), b[1]
                m, ms = n - 1, 1 - s
                if more and s == 1:
                    layer_rstd(b[0] + 1)
                for j in range(HC):
                    if front:
                        pool.wait_ge(S["q_rec"], HC * n + j + 1)
                        nc.gpsimd.tensor_tensor(heads(qn[s][:, j, :]), heads(qn[s][:, j, :]),
                                                spread(qrec[:, s, j, :], L0_DH), ALU.mult).then_inc(S["q_norm"], 1)
                    if back and j == 2:
                        pool.wait_ge(S["ct_high"], m + 1)
                        nc.gpsimd.tensor_tensor(context_columns(kvT, before(b), 1), cT[ms][:],
                                                plain(context_columns(kvT, before(b), 0)),
                                                ALU.subtract).then_inc(S["ct_split"], 1)

            steps(lambda a, b: chain.repeat(a, b, 1), step)


def pair_of(t, p):
    return t[:, bass.ds(p, 1), :].rearrange("p t n -> p (t n)")


def context_columns(kvT, batch, part):
    pair, s = batch
    return kvT[:, :, bass.ds(pair, 1), part, s * 3 * SEQ:s * 3 * SEQ + SEQ].rearrange("p c b t -> p (c b) t")


def x_columns(kvT, p, part):
    return kvT[:, :, bass.ds(p, 1), part, SEQ:3 * SEQ].rearrange("p c b t -> p (c b) t")


def pair_rows(t, p, r):
    return t[r, bass.ds(p, 1), :].rearrange("p t n -> p (t n)")


def norm_and_ffn(nc, sems, const, xres, kvT, obuf, dram):
    ident, consts = const
    g_d, in_d, out_d, br_d = dram
    NR = FFN_LOW + FFN_HEADS
    st = ExitStack()
    with st:
        sb = lambda name, shape, dt=FP32: st.enter_context(nc.sbuf_tensor(name, shape, dt))
        ps = lambda name: st.enter_context(nc.psum_tensor(name, [P, 512], FP32))
        w_in, w_out = sb("ffn_in", [P, HC, NR]), sb("ffn_out", [P, HIDDEN])
        g, g8, br = sb("g", [P, 1]), sb("g8", [P, 1]), sb("br", [P, FFN_HEADS])
        batch_ones = sb("batch_ones", [P, 2])
        sq, scaled = sb("sq", [P, HIDDEN]), sb("scaled", [P, HIDDEN])
        ssum, rnorm = sb("ssum", [P, 2 * HC]), sb("rnorm", [P, 2 * HC])
        rwide = sb("rwide", [P, HC, 2, SEQ])
        yn, yT = sb("yn", [P, HIDDEN]), sb("yT", [P, HIDDEN])
        zn = sb("zn", [P, HIDDEN])
        logit, share = sb("logit", [P, FFN_HEADS]), sb("share", [P, FFN_HEADS])
        e8, small = sb("e8", [P, FFN_HEADS]), sb("small", [P, 4])
        low, lowT = sb("low", [P, FFN_LOW]), sb("lowT", [P, FFN_LOW])
        ystats, ymom, yr = sb("ystats", [P, 6]), sb("ymom", [P, 2]), sb("yr", [P, 3])
        zstats, zmom, zr = sb("zstats", [P, 6]), sb("zmom", [P, 2]), sb("zr", [P, 3])
        spare = sb("spare2", [P, 1])
        ssp, rp, ytp, ztp = ps("ssp"), ps("rp"), ps("ytp"), ps("ztp")
        rlp, ltp, fp = ps("rlp"), ps("ltp"), ps("fp")
        S = sems
        block = st.enter_context(nc.Block())

        def steps(repeat, step):
            for k in range(4):
                step(k, 2, True, k >= 1, k >= 2, k >= 3)
            with repeat(4, HP - 2) as k:
                step(k, 2, True, True, True, True)
            for k in range(HP - 2, HP):
                step(k, HP - 1 - k, True, True, True, True)
            step(HP, 0, False, True, True, True)
            step(HP + 1, 0, False, False, True, True)
            step(HP + 2, 0, False, False, False, True)

        @block.sync
        def _(sp):
            for dst, src in ((w_in[:], in_d), (w_out[:], out_d), (g[:], g_d), (br[:], br_d)):
                sp.dma_start(dst, src).then_inc(S["f_in"], 16)

        @block.tensor
        def _(pe):
            pe.wait_ge(S["f_ready"], 1)

            def sum_squares(k):
                pe.wait_ge(S["sq_done"], k + 1)
                at_least(pe, S["ssum_ready"], k)
                for c in range(HC):
                    mm = nc.tensor.matmul(ssp[:, 2 * c:2 * c + 2], sq[:, c * P:(c + 1) * P], batch_ones[:],
                                          start=True, stop=True)
                mm.then_inc(S["ss_done"], 1)

            sum_squares(0)

            def step(k, ahead, a, r, f, z):
                if a:
                    pe.wait_ge(S["rwide_ready"], k + 1)
                    at_least(pe, S["scaled_ready"], k)
                    for c in range(HC):
                        mm = nc.tensor.transpose(rp[:, c * P:(c + 1) * P],
                                                 rwide[:, c, :, :].rearrange("p b o -> p (b o)"), ident[:])
                    mm.then_inc(S["rp_done"], 1)
                if z:
                    pe.wait_ge(S["zn_ready"], k - 2)
                    at_least(pe, S["z_split"], k - 3)
                    for c in range(HC):
                        mm = nc.tensor.transpose(ztp[:, c * P:(c + 1) * P], zn[:, c * P:(c + 1) * P], ident[:])
                    mm.then_inc(S["zt_done"], 1)
                if f:
                    pe.wait_ge(S["low_ready"], k - 1)
                    at_least(pe, S["lt_copied"], k - 2)
                    nc.tensor.transpose(ltp[:, 0:P], low[:], ident[:]).then_inc(S["lt_done"], 1)
                if ahead >= 1:
                    sum_squares(k + 1)
                if f:
                    pe.wait_ge(S["lt_copied"], k - 1)
                    at_least(pe, S["x2_ready"], k - 2)
                    nc.tensor.matmul(fp[:], lowT[:], w_out[:], start=True, stop=True).then_inc(S["f_done"], 1)
                if r:
                    pe.wait_ge(S["yn_ready"], k)
                    at_least(pe, S["yt_copied"], k - 1)
                    for c in range(HC):
                        mm = nc.tensor.transpose(ytp[:, c * P:(c + 1) * P], yn[:, c * P:(c + 1) * P], ident[:])
                    mm.then_inc(S["yt_done"], 1)
                if r:
                    pe.wait_ge(S["yt_copied"], k)
                    at_least(pe, S["low_ready"], k - 1)
                    for c in range(HC):
                        mm = nc.tensor.matmul(rlp[:, 0:NR], yT[:, c * P:(c + 1) * P], w_in[:, c, :],
                                              start=(c == 0), stop=(c == HC - 1))
                    mm.then_inc(S["rl_done"], 1)

            steps(pe.Fori, step)

        @block.scalar
        def _(act):
            def square(k):
                at_least(act, S["ss_done"], k)
                nc.scalar.activation(sq[:], pair_of(obuf, k), ACT.Square).then_inc(S["sq_done"], 1)

            square(0)
            square(1)

            def step(k, ahead, a, r, f, z):
                if z:
                    act.wait_ge(S["zr_ready"], k - 2)
                    at_least(act, S["zt_done"], k - 3)
                    nc.scalar.activation(zn[:], pair_of(xres, k - 3), ACT.Identity, bias=zr[:, 2:3],
                                         scale=zr[:, 1:2]).then_inc(S["zn_ready"], 1)
                if f:
                    act.wait_ge(S["lt_done"], k - 1)
                    at_least(act, S["f_done"], k - 2)
                    nc.scalar.activation(lowT[:], ltp[:, 0:P], ACT.Copy).then_inc(S["lt_copied"], 1)
                if z:
                    act.wait_ge(S["zt_done"], k - 2)
                    nc.scalar.activation(x_columns(kvT, k - 3, 0), ztp[:].rearrange("p (c t) -> p c t", c=HC),
                                         ACT.Copy).then_inc(S["z_high"], 1)
                if r:
                    act.wait_ge(S["yr_ready"], k)
                    at_least(act, S["yt_done"], k - 1)
                    nc.scalar.activation(yn[:], pair_of(xres, k - 1), ACT.Identity, bias=yr[:, 2:3],
                                         scale=yr[:, 1:2]).then_inc(S["yn_ready"], 1)
                if r:
                    act.wait_ge(S["yt_done"], k)
                    at_least(act, S["rl_done"], k - 1)
                    nc.scalar.activation(yT[:], ytp[:], ACT.Copy).then_inc(S["yt_copied"], 1)
                if ahead == 2:
                    square(k + 2)
                if r:
                    act.wait_ge(S["logit_ready"], k)
                    nc.scalar.activation(e8[:], logit[:], ACT.Exp, bias=small[:, 0:1],
                                         accum_out=small[:, 1:2]).then_inc(S["e_done"], 1)

            steps(act.Fori, step)

        @block.gpsimd
        def _(pool):
            chain = Chain(pool, S["pool_chain2"])

            def inverse_norm(k):
                pool.wait_ge(S["ssum_ready"], k + 1)
                at_least(pool, S["rwide_ready"], k)
                nc.gpsimd.tensor_tensor(rnorm[:], ssum[:], consts[:, 0:2 * HC], ALU.pow).then_inc(S["rnorm_ready"], 1)

            inverse_norm(0)

            def step(k, ahead, a, r, f, z):
                if r:
                    pool.wait_ge(S["ystats_ready"], k)
                    at_least(pool, S["yn_ready"], k - 1)
                    inverse_root(nc, chain, ymom, yr, consts).then_inc(S["yr_ready"], 1)
                if a:
                    pool.wait_ge(S["scaled_ready"], k + 1)
                    nc.gpsimd.tensor_tensor(pair_of(xres, k), pair_of(xres, k), scaled[:],
                                            ALU.add).then_inc(S["x1_ready"], 1)
                if ahead >= 1:
                    inverse_norm(k + 1)
                if f:
                    pool.wait_ge(S["zstats_ready"], k - 1)
                    at_least(pool, S["zn_ready"], k - 2)
                    inverse_root(nc, chain, zmom, zr, consts).then_inc(S["zr_ready"], 1)

            steps(lambda a, b: chain.repeat(a, b, 6), step)

        @block.vector
        def _(dve):
            chain = Chain(dve, S["dve_chain2"])
            link = chain.link
            dve.wait_ge(S["f_in"], 64)
            link(nc.vector.memset(batch_ones[:], 0.0))
            nc.vector.memset(batch_ones[0:SEQ, 0:1], 1.0)
            nc.vector.memset(batch_ones[SEQ:P, 1:2], 1.0)
            link(nc.vector.tensor_scalar(g8[:], g[:], math.sqrt(SEQ), None, ALU.mult))
            nc.vector.memset(small[:], 0.0).then_inc(S["f_ready"], 1)

            def bound_sum(k):
                dve.wait_ge(S["ss_done"], k + 1)
                at_least(dve, S["rnorm_ready"], k)
                nc.vector.tensor_scalar(ssum[:], ssp[:, 0:2 * HC], 1e-24, None, ALU.max).then_inc(S["ssum_ready"], 1)

            def widen(k):
                dve.wait_ge(S["rnorm_ready"], k + 1)
                at_least(dve, S["rp_done"], k)
                nc.vector.tensor_copy(rwide[:], spread(rnorm[:].rearrange("p (c b) -> p c b", c=HC),
                                                       SEQ)).then_inc(S["rwide_ready"], 1)

            bound_sum(0)
            widen(0)

            def step(k, ahead, a, r, f, z):
                if r:
                    dve.wait_ge(S["x1_ready"], k)
                    nc.vector.memset(spare[:], 0.0)
                    link(nc.vector.bn_stats(ystats[:], pair_of(xres, k - 1)))
                    at_least(dve, S["yr_ready"], k - 1)
                    nc.vector.memset(spare[:], 0.0)
                    nc.vector.bn_aggr(ymom[:], ystats[:]).then_inc(S["ystats_ready"], 1)
                if f:
                    dve.wait_ge(S["e_done"], k - 1)
                    link(nc.vector.reciprocal(small[:, 2:3], small[:, 1:2]))
                    link(nc.vector.tensor_scalar(share[:], e8[:], small[:, 2:3], FFN_HEADS * FFN_SCALING,
                                                 ALU.mult, ALU.mult))
                    at_least(dve, S["lt_done"], k - 2)
                    nc.vector.tensor_tensor(low[:].rearrange("p (h r) -> p h r", h=FFN_HEADS),
                                            rlp[:, 0:FFN_LOW].rearrange("p (h r) -> p h r", h=FFN_HEADS),
                                            spread(share[:], FFN_R), ALU.mult).then_inc(S["low_ready"], 1)
                if a:
                    dve.wait_ge(S["rp_done"], k + 1)
                    at_least(dve, S["x1_ready"], k)
                    nc.vector.scalar_tensor_tensor(scaled[:], pair_of(obuf, k), g8[:], rp[:],
                                                   ALU.mult, ALU.mult).then_inc(S["scaled_ready"], 1)
                if ahead >= 1:
                    bound_sum(k + 1)
                if z:
                    dve.wait_ge(S["z_high"], k - 2)
                    nc.vector.tensor_tensor(x_columns(kvT, k - 3, 1), ztp[:].rearrange("p (c t) -> p c t", c=HC),
                                            plain(x_columns(kvT, k - 3, 0)), ALU.subtract).then_inc(S["z_split"], 1)
                if f:
                    dve.wait_ge(S["f_done"], k - 1)
                    nc.vector.tensor_tensor(pair_of(xres, k - 2), fp[:], pair_of(xres, k - 2),
                                            ALU.add).then_inc(S["x2_ready"], 1)
                    dve.wait_ge(S["x2_ready"], k - 1)
                    nc.vector.memset(spare[:], 0.0)
                    link(nc.vector.bn_stats(zstats[:], pair_of(xres, k - 2)))
                    at_least(dve, S["zr_ready"], k - 2)
                    nc.vector.memset(spare[:], 0.0)
                    nc.vector.bn_aggr(zmom[:], zstats[:]).then_inc(S["zstats_ready"], 1)
                if ahead >= 1:
                    widen(k + 1)
                if r:
                    dve.wait_ge(S["rl_done"], k)
                    link(nc.vector.tensor_tensor(logit[:], rlp[:, FFN_LOW:NR], br[:], ALU.add))
                    nc.vector.tensor_reduce(small[:, 0:1], logit[:], AX.X, ALU.max,
                                            negate=True).then_inc(S["logit_ready"], 1)

            steps(lambda a, b: chain.repeat(a, b, 5), step)


def grouped_attention(nc, sems, half, const, xres, kvT, dram):
    ident, consts = const
    w_d, qk_d = dram
    STEPS = L1_KV * HP
    LAG = 3
    RAW = 4
    st = ExitStack()
    with st:
        sb = lambda name, shape, dt=FP32: st.enter_context(nc.sbuf_tensor(name, shape, dt))
        ps = lambda name: st.enter_context(nc.psum_tensor(name, [P, 512], FP32))
        w = sb("l1_w", [P, 2, 2, W_COLS], FP32R)
        raw = [sb(f"l1_raw{j}", [P, W_CHUNK]) for j in range(RAW)]
        qk_w, qk = sb("qk_w", [P, 2]), sb("qk", [P, 1])
        q_sq, k_sq = sb("q_sq", [P, 512]), sb("k_sq", [P, 2, P])
        q_ss, k_ss = sb("q_ss", [P, GROUP]), sb("k_ss", [P, 2])
        q_ms, k_ms = sb("q_ms", [P, GROUP]), sb("k_ms", [P, 2])
        q_r, k_r = sb("q_r", [P, GROUP]), sb("k_r", [P, 2])
        qs = sb("qs", [P, 512])
        ks = [sb(f"ks{j}", [P, 2, P]) for j in range(2)]
        v = [sb(f"v{j}", [P, 2, 2, P], FP32R) for j in range(4)]
        qT, kT = sb("l1_qT", [P, 2, GROUP * SEQ]), sb("l1_kT", [P, 2, P])
        nmax, bias = sb("nmax", [P, 4]), sb("bias", [P, 4])
        psum_, prec = sb("psums", [P, 4]), sb("prec", [P, 4])
        pe_, pn = sb("p_exp", [P, 4, P]), sb("p_norm", [P, 4, P])
        pT = sb("pT", [P, 2, 2, GROUP * SEQ], FP32R)
        oT = sb("oT", [P, 2, GROUP, P], FP32R)
        kvp, qp, qtp, ktp = ps("kvp"), ps("l1_qp"), ps("qtp"), ps("ktp")
        sp_, ptp, op, yp = ps("scp"), ps("ptp"), ps("l1_op"), ps("yp")
        S = sems
        w_in = [S[f"w_in{j}"] for j in range(RAW)]
        block = st.enter_context(nc.Block())

        def chunks_to(column):
            return -(-column // W_CHUNK)

        def slot(g):
            return g % 2

        def weights(g, part, first, count):
            sl = slot(g)
            if isinstance(sl, int):
                return w[:, sl, part, first:first + count]
            return w[:, bass.ds(sl, 1), part, first:first + count].rearrange("p s n -> p (s n)")

        def steps(repeat, step):
            for t in range(HP):
                step(0, t, [t >= lag for lag in range(LAG + 1)], True)
            with repeat(1, L1_KV - 1) as g:
                for t in range(HP):
                    step(g, t, [True] * (LAG + 1), True)
            for t in range(HP):
                step(L1_KV - 1, t, [True] * (LAG + 1), False)
            for t in range(LAG):
                step(L1_KV, t, [t < lag for lag in range(LAG + 1)], False)

        @block.sync
        def _(sp):
            sp.dma_start(qk_w[:], qk_d).then_inc(S["qk_in"], 16)

            def load(g, j):
                at_least(sp, S["w_split"], W_CHUNKS * g + j + 1 - RAW)
                src = w_d[g, :, j * W_CHUNK:(j + 1) * W_CHUNK] if isinstance(g, int) else \
                    w_d[bass.ds(g, 1), :, j * W_CHUNK:(j + 1) * W_CHUNK].rearrange("g p n -> p (g n)")
                sp.dma_start(raw[j % RAW][:], src).then_inc(w_in[j % RAW], 16)

            for j in range(W_CHUNKS):
                load(0, j)
            with sp.Fori(1, L1_KV) as g:
                for j in range(W_CHUNKS):
                    load(g, j)

        def chunk_in(engine, g, j):
            engine.wait_ge(w_in[j % RAW], (W_CHUNKS // RAW * g + j // RAW + 1) * 16)

        @block.tensor
        def _(pe):
            def three(out, stationary, moving, first, last):
                nc.tensor.matmul(out, stationary[0], moving[0], start=first, stop=False)
                nc.tensor.matmul(out, stationary[0], moving[1], start=False, stop=False)
                return nc.tensor.matmul(out, stationary[1], moving[0], start=False, stop=last)

            def step(g, t, on, split):
                i = HP * g + t
                if on[0]:
                    if t == 0:
                        pe.wait_ge(S["w_split"], W_CHUNKS * g + chunks_to(W_Q))
                    at_least(pe, S["k_scaled"], i)
                    for b in range(2):
                        for c in range(HC):
                            mm = three(kvp[:, b * 256:(b + 1) * 256],
                                       [kvT[:, c, t, part, b * P:(b + 1) * P] for part in range(2)],
                                       [weights(g, part, W_KV + c * 256, 256) for part in range(2)],
                                       c == 0, c == HC - 1)
                    mm.then_inc(S["kv_done"], 1)
                if on[1]:
                    pe.wait_ge(S["k_scaled"], i)
                    at_least(pe, S["kt_copied1"], i - 1)
                    for b in range(2):
                        mm = nc.tensor.transpose(ktp[:, b * P:(b + 1) * P], ks[(t - 1) % 2][:, b, :], ident[:])
                    mm.then_inc(S["kt_done"], 1)
                    pe.wait_ge(S["q_scaled"], i)
                    at_least(pe, S["qt_copied1"], i - 1)
                    for h in range(GROUP):
                        mm = nc.tensor.transpose(qtp[:, h * P:(h + 1) * P], qs[:, h * P:(h + 1) * P], ident[:])
                    mm.then_inc(S["qt_done"], 1)
                if on[0]:
                    at_least(pe, S["q_scaled"], i)
                    if t == 0:
                        pe.wait_ge(S["w_split"], W_CHUNKS * g + chunks_to(W_O))
                    for c in range(HC):
                        mm = three(qp[:], [kvT[:, c, t, part, SEQ:3 * SEQ] for part in range(2)],
                                   [weights(g, part, W_Q + c * 512, 512) for part in range(2)],
                                   c == 0, c == HC - 1)
                    mm.then_inc(S["q_done"], 1)
                if on[1]:
                    pe.wait_ge(S["kt_copied1"], i)
                    pe.wait_ge(S["qt_copied1"], i)
                    at_least(pe, S["p_done"], i - 1)
                    for b in range(2):
                        for hh in range(2):
                            at = (2 * b + hh) * P
                            mm = nc.tensor.matmul(sp_[:, at:at + P], qT[:, b, hh * P:(hh + 1) * P],
                                                  kT[:, b, :], start=True, stop=True)
                    mm.then_inc(S["s_done"], 1)
                if on[2]:
                    pe.wait_ge(S["p_normed"], i - 1)
                    at_least(pe, S["pt_split"], i - 2)
                    for a in range(4):
                        mm = nc.tensor.transpose(ptp[:, a * P:(a + 1) * P], pn[:, a, :], ident[:])
                    mm.then_inc(S["pt_done"], 1)
                if on[3]:
                    og = g if t >= LAG else g - 1
                    if t == LAG:
                        pe.wait_ge(S["w_split"], W_CHUNKS * (g + 1))
                    pe.wait_ge(S["o_split"], i - 2)
                    at_least(pe, S["y_added"], i - 3)
                    for h in range(GROUP):
                        mm = three(yp[:], [oT[:, part, h, :] for part in range(2)],
                                   [weights(og, part, W_O + h * 512, 512) for part in range(2)],
                                   h == 0, h == GROUP - 1)
                    mm.then_inc(S["y_done"], 1)
                if on[2]:
                    pe.wait_ge(S["pt_split"], i - 1)
                    at_least(pe, S["o_split"], i - 2)
                    vs = v[(t - 2) % 4]
                    for b in range(2):
                        mm = three(op[:, b * 256:(b + 1) * 256], [vs[:, part, b, :] for part in range(2)],
                                   [pT[:, part, b, :] for part in range(2)], True, True)
                    mm.then_inc(S["o_done1"], 1)

            steps(pe.Fori, step)

        def by_batch(t):
            return t.rearrange("p h (b q) -> p b h q", b=2)

        def by_head(t):
            return t[:].rearrange("p (b h q) -> p b h q", b=2, h=GROUP)

        def bank(t, b=2):
            return t[:].rearrange("p (b n) -> p b n", b=b)

        @block.scalar
        def _(act):
            def split_high(g, j):
                chunk_in(act, g, j)
                nc.scalar.activation(weights(g, 0, j * W_CHUNK, W_CHUNK), raw[j % RAW][:],
                                     ACT.Copy).then_inc(S["w_high"], 1)

            for j in range(W_CHUNKS):
                split_high(0, j)

            def step(g, t, on, split):
                i = HP * g + t
                if on[3]:
                    act.wait_ge(S["o_done1"], i - 2)
                    at_least(act, S["y_done"], i - 3)
                    nc.scalar.activation(by_batch(oT[:, 0, :, :]), by_head(op), ACT.Copy).then_inc(S["o_high"], 1)
                if on[0]:
                    act.wait_ge(S["kv_done"], i + 1)
                    at_least(act, S["k_summed"], i)
                    nc.scalar.activation(k_sq[:], bank(kvp)[:, :, 0:P], ACT.Square).then_inc(S["k_squared"], 1)
                    at_least(act, S["o_done1"], i - 3)
                    nc.scalar.activation(v[t % 4][:, 0, :, :], bank(kvp)[:, :, P:2 * P],
                                         ACT.Copy).then_inc(S["v_high"], 1)
                if on[1]:
                    act.wait_ge(S["kt_done"], i)
                    at_least(act, S["s_done"], i - 1)
                    nc.scalar.activation(kT[:], bank(ktp)[:, 0, :].rearrange("p (b n) -> p b n", b=2), ACT.Copy,
                                         scale=qk[:, 0:1]).then_inc(S["kt_copied1"], 1)
                    act.wait_ge(S["qt_done"], i)
                    nc.scalar.activation(qT[:].rearrange("p b (h q) -> p h b q", h=GROUP),
                                         qtp[:].rearrange("p (h b q) -> p h b q", h=GROUP, b=2),
                                         ACT.Copy).then_inc(S["qt_copied1"], 1)
                if split:
                    if t <= LAG:
                        at_least(act, S["q_done"], HP * g)
                    else:
                        at_least(act, S["y_done"], HP * g)
                    split_high(g + 1, t)
                if on[0]:
                    act.wait_ge(S["q_done"], i + 1)
                    at_least(act, S["q_summed"], i)
                    nc.scalar.activation(q_sq[:], qp[:], ACT.Square).then_inc(S["q_squared"], 1)
                if on[2]:
                    act.wait_ge(S["pt_done"], i - 1)
                    at_least(act, S["o_done1"], i - 2)
                    nc.scalar.activation(pT[:, 0, :, :].rearrange("p b n -> p (b n)"), ptp[:],
                                         ACT.Copy).then_inc(S["pt_high"], 1)
                if on[1]:
                    act.wait_ge(S["bias_ready"], i)
                    at_least(act, S["p_normed"], i - 1)
                    for a in range(4):
                        last = nc.scalar.activation(pe_[:, a, :], sp_[:, a * P:(a + 1) * P], ACT.Exp,
                                                    bias=bias[:, a:a + 1], scale=L1_SCALE,
                                                    accum_out=psum_[:, a:a + 1])
                    last.then_inc(S["p_done"], 1)

            steps(act.Fori, step)

        @block.gpsimd
        def _(pool):
            chain = Chain(pool, S["pool_chain3"])

            def split_low(g, j):
                pool.wait_ge(S["w_high"], W_CHUNKS * g + j + 1)
                nc.gpsimd.tensor_tensor(weights(g, 1, j * W_CHUNK, W_CHUNK), raw[j % RAW][:],
                                        plain(weights(g, 0, j * W_CHUNK, W_CHUNK)),
                                        ALU.subtract).then_inc(S["w_split"], 1)

            pool.wait_ge(S["w_split"], W_CHUNKS)

            def rms(total, mean, root, n):
                chain.link(nc.gpsimd.tensor_tensor(mean[:], total[:], consts[:, RMS_COL:RMS_COL + n], ALU.add))
                return nc.gpsimd.tensor_tensor(root[:], mean[:], consts[:, 0:n], ALU.pow)

            def step(g, t, on, split):
                i = HP * g + t
                if on[0]:
                    pool.wait_ge(S["k_summed"], i + 1)
                    rms(k_ss, k_ms, k_r, 2).then_inc(S["k_root"], 1)
                if split:
                    split_low(g + 1, t)
                if on[0]:
                    pool.wait_ge(S["q_summed"], i + 1)
                    rms(q_ss, q_ms, q_r, GROUP).then_inc(S["q_root"], 1)
                if on[1]:
                    pool.wait_ge(S["prec_ready"], i)
                    at_least(pool, S["pt_done"], i - 1)
                    nc.gpsimd.tensor_tensor(pn[:], pe_[:], spread(prec[:], P), ALU.mult).then_inc(S["p_normed"], 1)

            steps(lambda a, b: chain.repeat(a, b, 2 * HP), step)

        @block.vector
        def _(dve):
            chain = Chain(dve, S["dve_chain3"])
            link = chain.link
            dve.wait_ge(S["qk_in"], 16)
            link(nc.vector.scalar_tensor_tensor(qk[:], qk_w[:, 0:1], float(L1_DH), qk_w[:, 1:2], ALU.mult, ALU.mult))

            for j in range(W_CHUNKS):
                dve.wait_ge(S["w_high"], j + 1)
                nc.vector.tensor_tensor(weights(0, 1, j * W_CHUNK, W_CHUNK), raw[j % RAW][:],
                                        plain(weights(0, 0, j * W_CHUNK, W_CHUNK)),
                                        ALU.subtract).then_inc(S["w_split"], 1)

            def step(g, t, on, split):
                i = HP * g + t
                if on[3]:
                    dve.wait_ge(S["o_high"], i - 2)
                    at_least(dve, S["y_done"], i - 3)
                    nc.vector.tensor_tensor(by_batch(oT[:, 1, :, :]), by_head(op),
                                            plain(by_batch(oT[:, 0, :, :])), ALU.subtract).then_inc(S["o_split"], 1)
                if on[0]:
                    dve.wait_ge(S["k_squared"], i + 1)
                    nc.vector.tensor_reduce(k_ss[:], k_sq[:], AX.X, ALU.add).then_inc(S["k_summed"], 1)
                    dve.wait_ge(S["v_high"], i + 1)
                    nc.vector.tensor_tensor(v[t % 4][:, 1, :, :], bank(kvp)[:, :, P:2 * P],
                                            plain(v[t % 4][:, 0, :, :]), ALU.subtract).then_inc(S["v_split"], 1)
                    dve.wait_ge(S["k_root"], i + 1)
                    nc.vector.tensor_tensor(ks[t % 2][:], bank(kvp)[:, :, 0:P], spread(k_r[:], P),
                                            ALU.mult).then_inc(S["k_scaled"], 1)
                    dve.wait_ge(S["q_squared"], i + 1)
                    nc.vector.tensor_reduce(q_ss[:], q_sq[:].rearrange("p (h d) -> p h d", h=GROUP), AX.X,
                                            ALU.add).then_inc(S["q_summed"], 1)
                if on[1]:
                    dve.wait_ge(S["s_done"], i)
                    link(nc.vector.tensor_reduce(nmax[:], sp_[:].rearrange("p (a k) -> p a k", a=4), AX.X,
                                                 ALU.max, negate=True))
                    nc.vector.tensor_scalar(bias[:], nmax[:], L1_SCALE, None, ALU.mult).then_inc(S["bias_ready"], 1)
                if on[2]:
                    dve.wait_ge(S["pt_high"], i - 1)
                    nc.vector.tensor_tensor(pT[:, 1, :, :].rearrange("p b n -> p (b n)"), ptp[:],
                                            plain(pT[:, 0, :, :].rearrange("p b n -> p (b n)")),
                                            ALU.subtract).then_inc(S["pt_split"], 1)
                if on[0]:
                    dve.wait_ge(S["q_root"], i + 1)
                    nc.vector.tensor_tensor(qs[:].rearrange("p (h d) -> p h d", h=GROUP),
                                            qp[:].rearrange("p (h d) -> p h d", h=GROUP), spread(q_r[:], P),
                                            ALU.mult).then_inc(S["q_scaled"], 1)
                if on[1]:
                    dve.wait_ge(S["p_done"], i)
                    nc.vector.reciprocal(prec[:], psum_[:]).then_inc(S["prec_ready"], 1)
                if on[3]:
                    dve.wait_ge(S["y_done"], i - 2)
                    at = xres[:, (t - LAG) % HP, :]
                    nc.vector.tensor_tensor(at, yp[:], at, ALU.add).then_inc(S["y_added"], 1)

            steps(lambda a, b: chain.repeat(a, b, HP), step)


def quantised_ffn(nc, sems, half, const, xres, dram, out):
    ident, consts = const
    wq_d, sc_d = dram
    st = ExitStack()
    with st:
        sb = lambda name, shape, dt=FP32: st.enter_context(nc.sbuf_tensor(name, shape, dt))
        ps = lambda name: st.enter_context(nc.psum_tensor(name, [P, 512], FP32))
        wq, sc, wf = (sb(f"f1_{n}", [P, HC, HIDDEN], dt) for n, dt in (("wq", INT32), ("sc", FP32), ("w", FP32)))
        w_h, w_l = sb("f1_wh", [P, HC, HIDDEN], FP32R), sb("f1_wl", [P, HC, HIDDEN], FP32R)
        u = sb("u", [P, HIDDEN])
        uT_h = [sb(f"uT_h{j}", [P, HIDDEN], FP32R) for j in range(2)]
        uT_l = [sb(f"uT_l{j}", [P, HIDDEN], FP32R) for j in range(2)]
        ustats, umom, ur = sb("ustats", [P, 6]), sb("umom", [P, 2]), sb("ur", [P, 3])
        spare = sb("spare3", [P, 1])
        utp, fp = ps("utp"), [ps(f"f1p{j}") for j in range(2)]
        S = sems
        w_in = [S[f"u_in{c}"] for c in range(HC)]
        block = st.enter_context(nc.Block())

        def steps(repeat, step):
            for k in range(2):
                step(k, k, 2)
            with repeat(1, HP // 2 - 1) as j:
                for s in range(2):
                    step(2 * j + s, s, 2)
            for s in range(2):
                step(HP - 2 + s, s, 1 - s)
            step(HP, 0, -1)

        @block.sync
        def _(sp):
            for c in range(HC):
                sp.dma_start(wq[:, c, :], wq_d[:, c * HIDDEN:(c + 1) * HIDDEN]).then_inc(w_in[c], 16)
            with sp.Fori(0, HP) as k:
                sp.wait_ge(S["out_ready"], k + 1)
                sp.dma_start(out[bass.ds((half * HP + k) * P, P), :], pair_of(xres, k)).then_inc(S["stored"], 16)
            sp.wait_ge(S["stored"], 16 * HP)

        @block.tensor
        def _(pe):
            def step(k, s, ahead):
                first = isinstance(k, int) and k == 1
                if ahead >= 0:
                    pe.wait_ge(S["un_ready"], k + 1)
                    at_least(pe, S["ut_split"], k)
                    for c in range(HC):
                        mm = nc.tensor.transpose(utp[:, c * P:(c + 1) * P], u[:, c * P:(c + 1) * P], ident[:])
                    mm.then_inc(S["ut_done"], 1)
                if not (isinstance(k, int) and k == 0):
                    pe.wait_ge(S["ut_split"], k)
                    at_least(pe, S["out_ready"], k - 2)
                    bank, uh, ul = fp[1 - s], uT_h[1 - s], uT_l[1 - s]
                    for c in range(HC):
                        if first:
                            pe.wait_ge(S["w_split1"], c + 1)
                        xc = slice(c * P, (c + 1) * P)
                        nc.tensor.matmul(bank[:], uh[:, xc], w_h[:, c, :], start=(c == 0), stop=False)
                        nc.tensor.matmul(bank[:], uh[:, xc], w_l[:, c, :], start=False, stop=False)
                        mm = nc.tensor.matmul(bank[:], ul[:, xc], w_h[:, c, :], start=False, stop=(c == HC - 1))
                    mm.then_inc(S["uf_done"], 1)

            steps(pe.Fori, step)

        @block.scalar
        def _(act):
            for c in range(HC):
                act.dma_start(sc[:, c, :], sc_d[:, c * HIDDEN:(c + 1) * HIDDEN]).then_inc(w_in[c], 16)

            def normalise(k):
                act.wait_ge(S["ur_ready"], k + 1)
                at_least(act, S["ut_done"], k)
                nc.scalar.activation(u[:], pair_of(xres, k), ACT.Identity, bias=ur[:, 2:3],
                                     scale=ur[:, 1:2]).then_inc(S["un_ready"], 1)

            normalise(0)
            for c in range(HC):
                act.wait_ge(S["w_made"], c + 1)
                nc.scalar.activation(w_h[:, c, :], wf[:, c, :], ACT.Copy).then_inc(S["w_high1"], 1)

            def step(k, s, ahead):
                if ahead >= 0:
                    act.wait_ge(S["ut_done"], k + 1)
                    at_least(act, S["uf_done"], k - 1)
                    nc.scalar.activation(uT_h[s][:], utp[:], ACT.Copy).then_inc(S["ut_high"], 1)
                if ahead >= 1:
                    normalise(k + 1)

            steps(act.Fori, step)

        @block.gpsimd
        def _(pool):
            chain = Chain(pool, S["pool_chain4"])

            def root(k):
                pool.wait_ge(S["ustats_ready"], k + 1)
                at_least(pool, S["un_ready"], k)
                inverse_root(nc, chain, umom, ur, consts).then_inc(S["ur_ready"], 1)

            root(0)
            for c in range(HC):
                pool.wait_ge(S["w_high1"], c + 1)
                nc.gpsimd.tensor_tensor(w_l[:, c, :], wf[:, c, :], plain(w_h[:, c, :]),
                                        ALU.subtract).then_inc(S["w_split1"], 1)

            def step(k, s, ahead):
                if ahead >= 1:
                    root(k + 1)

            steps(lambda a, b: chain.repeat(a, b, 6), step)

        @block.vector
        def _(dve):
            chain = Chain(dve, S["dve_chain4"])

            def ln_stats(k):
                at_least(dve, S["ustats_ready"], k)
                nc.vector.memset(spare[:], 0.0)
                chain.link(nc.vector.bn_stats(ustats[:], pair_of(xres, k)))
                at_least(dve, S["ur_ready"], k)
                nc.vector.memset(spare[:], 0.0)
                nc.vector.bn_aggr(umom[:], ustats[:]).then_inc(S["ustats_ready"], 1)

            ln_stats(0)
            for c in range(HC):
                dve.wait_ge(w_in[c], 32)
                nc.vector.scalar_tensor_tensor(wf[:, c, :], wq[:, c, :], -128.0, sc[:, c, :], ALU.add,
                                               ALU.mult).then_inc(S["w_made"], 1)
            ln_stats(1)

            def step(k, s, ahead):
                if ahead >= 0:
                    dve.wait_ge(S["ut_high"], k + 1)
                    nc.vector.tensor_tensor(uT_l[s][:], utp[:], plain(uT_h[s][:]),
                                            ALU.subtract).then_inc(S["ut_split"], 1)
                if ahead >= 2:
                    ln_stats(k + 2)
                if not (isinstance(k, int) and k == 0):
                    dve.wait_ge(S["uf_done"], k)
                    nc.vector.tensor_tensor(pair_of(xres, k - 1), fp[1 - s][:], pair_of(xres, k - 1),
                                            ALU.add).then_inc(S["out_ready"], 1)

            steps(lambda a, b: chain.repeat(a, b, 2), step)


A1_SEMS = """w_in x_first x_rest c_in0 c_in1 ct_in0 ct_in1 wvo_done w_ready stats_ready rstd_ready
    xn_ready x_high c_high x_stacked c_stacked k_proj q_proj k_max k_exp q_max q_sub q_exp q_rec
    q_norm tk_done tq_done kt_copied qt_copied ct_high ct_split g_step g_copied m_done m_scaled
    krec_done o_done o_stored dve_chain pool_chain"""
A2_SEMS = """f_in f_ready sq_done ss_done ssum_ready rnorm_ready rwide_ready rp_done scaled_ready
    x1_ready yn_ready yt_done yt_copied rl_done logit_ready e_done low_ready lt_done lt_copied
    f_done x2_ready zn_ready zt_done z_high z_split ystats_ready yr_ready zstats_ready zr_ready
    dve_chain2 pool_chain2"""
B_SEMS = """qk_in w_in0 w_in1 w_in2 w_in3 w_high w_split kv_done q_done kt_done qt_done s_done pt_done y_done
    o_done1 k_squared k_summed k_root k_scaled q_squared q_summed q_root q_scaled v_high v_split
    kt_copied1 qt_copied1 bias_ready p_done prec_ready p_normed pt_high pt_split o_high o_split
    y_added dve_chain3 pool_chain3"""
C_SEMS = """u_in0 u_in1 u_in2 u_in3 w_made w_high1 w_split1 ustats_ready ur_ready un_ready ut_done ut_high
    ut_split uf_done out_ready stored dve_chain4 pool_chain4"""



def build(nc, x, ctx, ctx_t, l0_wq, l0_wk, l0_wv, l0_wo, l0_bo, l0_g, ffn_in, ffn_out, ffn_br, l1_w, l1_qk,
          f1_wq, f1_sc, out):
    with ExitStack() as st:
        xres = st.enter_context(nc.sbuf_tensor("xres", [P, HP, HIDDEN], FP32))
        kvT = st.enter_context(nc.sbuf_tensor("kvT", [P, HC, HP, 2, 2 * P], FP32R))
        ident = st.enter_context(nc.sbuf_tensor("ident", [P, P], FP32))
        consts = st.enter_context(nc.sbuf_tensor("consts", [P, MINUS_COL + 1], FP32))
        made = st.enter_context(nc.semaphore("const_made"))
        a1, a2 = semaphores(nc, st, A1_SEMS), semaphores(nc, st, A2_SEMS)
        b_, c_ = semaphores(nc, st, B_SEMS), semaphores(nc, st, C_SEMS)
        const = (ident, consts)
        with nc.Block() as block:
            @block.gpsimd
            def _(pool):
                nc.gpsimd.memset(consts[:, 0:LN_COL], -0.5)
                nc.gpsimd.memset(consts[:, LN_COL:RMS_COL], LN_EPS)
                nc.gpsimd.memset(consts[:, RMS_COL:MINUS_COL], L1_DH * RMS_EPS)
                nc.gpsimd.memset(consts[:, MINUS_COL:], -1.0)
                nc.gpsimd.memset(ident[:], 0.0).then_inc(made, 1)
                pool.wait_ge(made, 1)
                nc.gpsimd.affine_select(out=ident[:], in_=ident[:], compare_op=ALU.not_equal, fill=1.0, base=0,
                                        pattern=[[-1, P]], channel_multiplier=1).then_inc(made, 1)
                pool.wait_ge(made, 2)
        with nc.Fori(0, HALVES) as half:
            with nc.sbuf_tensor("obuf", [P, HP, HIDDEN], FP32) as obuf:
                linear_attention(nc, a1, half, const, xres, kvT, obuf,
                                 (x, ctx, ctx_t, l0_wq, l0_wk, l0_wv, l0_wo, l0_bo))
                clear(nc, a1)
                norm_and_ffn(nc, a2, const, xres, kvT, obuf, (l0_g, ffn_in, ffn_out, ffn_br))
                clear(nc, a2)
            grouped_attention(nc, b_, half, const, xres, kvT, (l1_w, l1_qk))
            clear(nc, b_)
            quantised_ffn(nc, c_, half, const, xres, (f1_wq, f1_sc), out)
            clear(nc, c_)


def kernel(**inputs):
    import numpy as _np
    import concourse.bacc as _bacc
    from concourse import mybir as _mybir
    from concourse.bass_utils import run_bass_kernel_spmd as _run

    a = {k: _np.asarray(v) for k, v in inputs.items()}
    x = a["x"].reshape(BATCHES * SEQ, HIDDEN)
    ctx = a["ctx_4096"].reshape(BATCHES * SEQ, HIDDEN)
    ctx_t = a["ctx_4096"].reshape(BATCHES, SEQ, HC, P).transpose(0, 3, 2, 1).reshape(BATCHES, P, HC * SEQ)
    twice = lambda w: _np.concatenate([w, w], axis=0)
    by_chunk = lambda w: w.reshape(-1, P, w.shape[-1]).transpose(1, 0, 2)
    ffn_in = by_chunk(_np.concatenate([a["L0_ffn_A"].reshape(FFN_LOW, HIDDEN), a["L0_ffn_Wr"]], axis=0).T)
    wq, wk, wv = (by_chunk(a[f"L1_xattn_{n}"]) for n in ("Wq", "Wk", "Wv"))
    wo = a["L1_xattn_Wo"].reshape(L1_HEADS, L1_DH, HIDDEN)
    groups = []
    for g in range(L1_KV):
        kv = slice(g * L1_DH, (g + 1) * L1_DH)
        q = slice(g * GROUP * L1_DH, (g + 1) * GROUP * L1_DH)
        groups.append(_np.concatenate([
            _np.concatenate([wk[:, :, kv], wv[:, :, kv]], axis=2).reshape(P, -1),
            wq[:, :, q].reshape(P, -1),
            wo[g * GROUP:(g + 1) * GROUP].transpose(1, 0, 2).reshape(P, -1)], axis=1))
    ins = {
        "x": x, "ctx": ctx, "ctx_t": ctx_t,
        "l0_wq": twice(a["L0_xattn_Wq"].T), "l0_wk": twice(a["L0_xattn_Wk"].T),
        "l0_wv": by_chunk(a["L0_xattn_Wv"]), "l0_wo": by_chunk(a["L0_xattn_Wo"].T),
        "l0_bo": twice(a["L0_xattn_bo"].reshape(SEQ, 1)), "l0_g": twice(a["L0_xattn_g"].reshape(SEQ, 1)),
        "ffn_in": ffn_in, "ffn_out": a["L0_ffn_B"].transpose(0, 2, 1).reshape(FFN_LOW, HIDDEN),
        "ffn_br": _np.repeat(a["L0_ffn_br"].reshape(1, FFN_HEADS), P, axis=0),
        "l1_w": _np.stack(groups),
        "l1_qk": _np.stack([a["L1_xattn_q_norm_w"], a["L1_xattn_k_norm_w"]], axis=1),
        "f1_wq": by_chunk(a["L1_ffn_w_q"].T).reshape(P, -1),
        "f1_sc": by_chunk(_np.repeat(a["L1_ffn_scales"].T, HIDDEN // a["L1_ffn_scales"].shape[1], axis=0)).reshape(P, -1),
    }
    ins = {k: _np.ascontiguousarray(v) for k, v in ins.items()}
    nc = _bacc.Bacc("TRN2", target_bir_lowering=False, num_devices=1)
    args = [nc.dram_tensor(f"in_{k}", v.shape, _mybir.dt.from_np(v.dtype), kind="ExternalInput").ap()
            for k, v in ins.items()]
    out = nc.dram_tensor("out", (BATCHES * SEQ, HIDDEN), FP32, kind="ExternalOutput").ap()
    build(nc, *args, out)
    r = _run(nc, [{f"in_{k}": v for k, v in ins.items()}], core_ids=[0])
    return r.results[0]["out"].reshape(BATCHES, SEQ, HIDDEN)
```

```python
import math
from contextlib import ExitStack, contextmanager

import concourse.bass as bass
from concourse import mybir

P = 128
FP32 = mybir.dt.float32
FP32R = mybir.dt.float32r
INT32 = mybir.dt.int32
ALU = mybir.AluOpType
ACT = mybir.ActivationFunctionType
AX = mybir.AxisListType

BATCHES, SEQ, HIDDEN = 32, 64, 512
HC = HIDDEN // P
HALVES = 2
HB = BATCHES // HALVES
HP = HB // 2
L0_HEADS, L0_DH = 8, 64
FFN_HEADS, FFN_R, FFN_SCALING = 8, 16, 32 / 16
FFN_LOW = FFN_HEADS * FFN_R
L1_HEADS, L1_KV, L1_DH = 32, 8, 128
GROUP = L1_HEADS // L1_KV
L1_SCALE = 1.0 / math.sqrt(L1_DH)
LN_EPS, RMS_EPS = 1e-5, 1e-6
LN_COL = max(GROUP, 2 * HC)
RMS_COL, MINUS_COL = LN_COL + 1, LN_COL + 1 + GROUP
W_KV, W_Q, W_O = 0, HC * 2 * L1_DH, HC * 2 * L1_DH + HC * GROUP * L1_DH
W_COLS = W_O + GROUP * HIDDEN
W_CHUNKS = HP
W_CHUNK = W_COLS // W_CHUNKS
RAW = 4


def at_least(engine, sem, value):
    if not (isinstance(value, int) and value <= 0):
        engine.wait_ge(sem, value)


class Chain:

    def __init__(self, engine, sem):
        self.engine, self.sem, self.count, self.base = engine, sem, 0, 0

    def link(self, instruction):
        instruction.then_inc(self.sem, 1)
        self.count += 1
        self.engine.wait_ge(self.sem, self.base + self.count)

    @contextmanager
    def repeat(self, first, end, links):
        before = self.count
        with self.engine.Fori(first, end) as i:
            self.base = (i - first) * links
            yield i
            assert self.count - before == links, f"{self.count - before} links"
        self.base, self.count = 0, before + links * (end - first)


def plain(ap):
    return ap.bitcast(FP32)


def spread(ap, n):
    return ap.unsqueeze(len(ap.shape)).to_broadcast([*ap.shape, n])


def semaphores(nc, stack, names):
    made = {name: stack.enter_context(nc.semaphore(name)) for name in names.split()}
    numbers = [s.num for s in made.values()]
    assert numbers == list(range(numbers[0], numbers[0] + len(numbers)))
    return made


def clear(nc, sems):
    first = min(s.num for s in sems.values())
    nc.all_engine_barrier(sems_to_clear=range(first, first + len(sems)))


def inverse_root(nc, chain, mom, r, consts):
    chain.link(nc.gpsimd.tensor_tensor(r[:, 0:1], mom[:, 1:2], consts[:, LN_COL:LN_COL + 1], ALU.add))
    chain.link(nc.gpsimd.tensor_tensor(r[:, 1:2], r[:, 0:1], consts[:, 0:1], ALU.pow))
    chain.link(nc.gpsimd.tensor_tensor(r[:, 0:1], mom[:, 0:1], r[:, 1:2], ALU.mult))
    return nc.gpsimd.tensor_tensor(r[:, 2:3], r[:, 0:1], consts[:, MINUS_COL:MINUS_COL + 1], ALU.mult)


def linear_attention(nc, sems, half, const, xres, kvT, obuf, dram):
    ident, consts = const
    x, ctx, ctx_t, wq_d, wk_d, wv_d, wo_d, bo_d = dram
    st = ExitStack()
    with st:
        sb = lambda name, shape, dt=FP32: st.enter_context(nc.sbuf_tensor(name, shape, dt))
        ps = lambda name: st.enter_context(nc.psum_tensor(name, [P, 512], FP32))
        wq_h, wq_l = sb("l0_wq_h", [P, HIDDEN], FP32R), sb("l0_wq_l", [P, HIDDEN], FP32R)
        wk_h, wk_l = sb("l0_wk_h", [P, HIDDEN], FP32R), sb("l0_wk_l", [P, HIDDEN], FP32R)
        wvo = sb("l0_wvo", [P, HIDDEN])
        bo = sb("l0_bo", [P, 1])
        x_st = [sb(f"x_stack{s}", [P, HIDDEN], FP32R) for s in range(2)]
        c_st = [sb(f"c_stack{s}", [P, HIDDEN], FP32R) for s in range(2)]
        xn = sb("xn", [P, HIDDEN])
        cn = sb("cn", [P, HIDDEN])
        cT = [sb(f"cT{s}", [P, HC, SEQ]) for s in range(2)]
        kexp = [sb(f"kexp{s}", [P, HC, HIDDEN]) for s in range(2)]
        qn = [sb(f"qn{s}", [P, HC, HIDDEN]) for s in range(2)]
        c_parts = [sb(f"c_parts{s}", [P, HC, 2, SEQ], FP32R) for s in range(2)]
        kT = [sb(f"kT{j}", [P, HIDDEN]) for j in range(2)]
        kT_h = [sb(f"kT_h{j}", [P, HIDDEN], FP32R) for j in range(2)]
        kT_l = [sb(f"kT_l{j}", [P, HIDDEN], FP32R) for j in range(2)]
        qT = [sb(f"qT{s}", [P, HC, HIDDEN]) for s in range(2)]
        gsb = sb("gsb", [P, HIDDEN])
        mT = [sb(f"mT{s}", [P, HC, SEQ]) for s in range(2)]
        stats, moments, rstd = sb("stats", [P, 6]), sb("moments", [P, 2]), sb("rstd", [P, 2])
        spare = sb("spare1", [P, 1])
        knmax, ksum, krec = (sb(n_, [P, 2, HC]) for n_ in ("knmax", "ksum", "krec"))
        qnmax, qsum = sb("qnmax", [P, HC, L0_HEADS]), sb("qsum", [P, HC, L0_HEADS])
        qrec = sb("qrec", [P, 2, HC, L0_HEADS])
        kp = [ps(f"kp{j}") for j in range(2)]
        qp = [ps(f"qp{j}") for j in range(2)]
        tkp, tqp, gmp, op = ps("tkp"), ps("tqp"), ps("gmp"), ps("op")
        S = sems

        wq_raw, wk_raw = kexp[0][:, 0, :], kexp[0][:, 1, :]
        wv_raw = kexp[1][:, 0, 0:HC * L0_DH].rearrange("p (c e) -> p c e", c=HC)
        wo_raw = kexp[1][:, 1, 0:HC * L0_DH].rearrange("p (c e) -> p c e", c=HC)

        def num(b):
            return 2 * b[0] + b[1]

        def before(b):
            return (b[0] - 1, 1) if b[1] == 0 else (b[0], 0)

        def after(b):
            return (b[0], 1) if b[1] == 0 else (b[0] + 1, 0)

        def rows(s):
            return slice(s * SEQ, s * SEQ + SEQ)

        def heads(t):
            return t.rearrange("p (h d) -> p h d", h=L0_HEADS)

        PEEL = 2

        def steps(repeat, step):
            for p in range(PEEL):
                for s in range(2):
                    step((p, s), True, 2 * p + s >= 1, 2 * p + s >= 2, True)
            with repeat(PEEL, HP - 1) as p:
                for s in range(2):
                    step((p, s), True, True, True, True)
            step((HP - 1, 0), True, True, True, True)
            step((HP - 1, 1), True, True, True, False)
            step((HP, 0), False, True, True, False)
            step((HP, 1), False, False, True, False)

        block = st.enter_context(nc.Block())

        @block.sync
        def _(sp):
            sp.dma_start(xres[:, 0:1, :], x[bass.ds(half * HP * P, P), :].rearrange(
                "(t p) n -> p t n", p=P)).then_inc(S["x_first"], 16)

            def load_c(b):
                at_least(sp, S["c_stacked"], num(b) - 1)
                sp.dma_start(cn[rows(b[1]), :], ctx[bass.ds((half * HB + num(b)) * SEQ, SEQ), :]).then_inc(
                    (S["c_in0"], S["c_in1"])[b[1]], 16)

            def load_ct(b):
                at_least(sp, S["ct_split"], num(b) - 1)
                sp.dma_start(cT[b[1]][:], ctx_t[bass.ds(half * HB + num(b), 1), :, :].rearrange(
                    "b p (c t) -> p (b c) t", c=HC)).then_inc((S["ct_in0"], S["ct_in1"])[b[1]], 16)

            load_c((0, 0))
            for dst, src in ((wv_raw, wv_d), (wo_raw, wo_d), (bo[:], bo_d)):
                sp.dma_start(dst, src).then_inc(S["wvo_in"], 16)
            sp.dma_start(xres[:, 1:HP, :], x[bass.ds(half * HP * P + P, (HP - 1) * P), :].rearrange(
                "(t p) n -> p t n", p=P)).then_inc(S["x_rest"], 16)
            for p in range(PEEL):
                for s in range(2):
                    load_c(after((p, s)))
                    load_ct((p, s))
            with sp.Fori(PEEL, HP - 1) as p:
                for s in range(2):
                    load_c(after((p, s)))
                    load_ct((p, s))
            load_c((HP - 1, 1))
            load_ct((HP - 1, 0))
            load_ct((HP - 1, 1))

        @block.tensor
        def _(pe):
            pe.wait_ge(S["w_ready"], 1)

            def project(b, j):
                n, s, cols = num(b), b[1], slice(j * P, (j + 1) * P)
                if j == 0:
                    pe.wait_ge(S["c_stacked"], n + 1)
                    pe.wait_ge(S["x_stacked"], n + 1)
                at_least(pe, S["q_sub"], HC * n + j - 1)
                nc.tensor.matmul(qp[j % 2][:], x_st[s][:, cols], wq_h[:], start=True, stop=False)
                nc.tensor.matmul(qp[j % 2][:], x_st[s][:, cols], wq_l[:], start=False,
                                 stop=True).then_inc(S["q_proj"], 1)
                at_least(pe, S["k_exp"], HC * n + j - 1)
                nc.tensor.matmul(kp[j % 2][:], wk_h[:, cols], c_st[s][:], start=True, stop=False)
                nc.tensor.matmul(kp[j % 2][:], wk_l[:, cols], c_st[s][:], start=False,
                                 stop=True).then_inc(S["k_proj"], 1)

            def transpose_q(m, ms, j):
                if j == 0:
                    pe.wait_ge(S["q_norm"], HC * (m + 1))
                at_least(pe, S["qt_copied"], HC * m + j)
                for c in range(HC):
                    mm = nc.tensor.transpose(tqp[:, c * P:(c + 1) * P], qn[ms][:, c, j * P:(j + 1) * P], ident[:])
                mm.then_inc(S["tq_done"], 1)

            def transpose_k(m, ms, j):
                if j == 0:
                    pe.wait_ge(S["k_exp"], HC * (m + 1))
                at_least(pe, S["kt_copied"], HC * m + j)
                if j % 2 == 0:
                    at_least(pe, S["kt_high1"], HC // 2 * m + j // 2)
                for c in range(HC):
                    mm = nc.tensor.transpose(tkp[:, c * P:(c + 1) * P], kexp[ms][:, c, j * P:(j + 1) * P], ident[:])
                mm.then_inc(S["tk_done"], 1)

            def context(m, ms, j):
                if j == 0:
                    pe.wait_ge(S["ct_split"], m + 1)
                    if isinstance(m, int) and m == 0:
                        pe.wait_ge(S["wvo_ready"], 1)
                    at_least(pe, S["g_copied"], m)
                pe.wait_ge(S["kt_low"], HC * m + j + 1)
                both = c_parts[ms][:, j, :, :].rearrange("p r t -> p (r t)")
                nc.tensor.matmul(gmp[:], both, kT_h[j % 2][:], start=(j == 0), stop=False)
                nc.tensor.matmul(gmp[:], both, kT_l[j % 2][:], start=False,
                                 stop=(j == HC - 1)).then_inc(S["g_step"], 1)

            project((0, 0), 0)

            def value_output():
                pe.wait_ge(S["wvo_in"], 48)
                for r, bank in ((0, gmp), (1, op)):
                    for c in range(HC):
                        last = nc.tensor.matmul(bank[0:SEQ, c * L0_DH:(c + 1) * L0_DH], wv_raw[rows(r), c, :],
                                                wo_raw[rows(r), c, :], start=True, stop=True)
                last.then_inc(S["wvo_done"], 1)

            def step(b, front, back, last_, more):
                n, s = num(b), b[1]
                m, ms = n - 1, 1 - s
                o = n - 2
                for j in range(HC):
                    if last_ and j == 0:
                        transpose_q(o, s, HC - 1)
                    if back and j >= 1:
                        transpose_q(m, ms, j - 1)
                    if back:
                        transpose_k(m, ms, j)
                    if last_ and j == 0:
                        context(o, s, HC - 1)
                    if last_ and j == 1:
                        pe.wait_ge(S["g_copied"], o + 1)
                        at_least(pe, S["o_stored"], o)
                        for c in range(HC):
                            mm = nc.tensor.matmul(op[:, c * P:(c + 1) * P], gsb[:, c * P:(c + 1) * P],
                                                  wvo[:, c * P:(c + 1) * P], start=True, stop=True)
                        mm.then_inc(S["m_done"], 1)
                    if front and j < HC - 1:
                        project(b, j + 1)
                    if isinstance(n, int) and n == 0 and j == 0:
                        value_output()
                    if more and j == HC - 1:
                        project(after(b), 0)
                    if last_ and j == HC - 1:
                        pe.wait_ge(S["m_scaled"], o + 1)
                        pe.wait_ge(S["qt_copied"], HC * (o + 1))
                        for c in range(HC):
                            mm = nc.tensor.matmul(op[rows(s), :], mT[s][:, c, :], qT[s][:, c, :], start=(c == 0),
                                                  stop=(c == HC - 1))
                        mm.then_inc(S["o_done"], 1)
                    if back and j >= 1:
                        context(m, ms, j - 1)

            steps(pe.Fori, step)

        @block.scalar
        def _(act):
            def stack_high(b):
                s, r = b[1], rows(b[1])
                act.wait_ge(S["xn_ready"], b[0] + 1)
                at_least(act, S["k_proj"], HC * (num(b) - 1))
                nc.scalar.activation(x_st[s][r, :], xn[r, :], ACT.Copy).then_inc(S["x_high"], 1)
                act.wait_ge((S["c_in0"], S["c_in1"])[s], 16 * (b[0] + 1))
                nc.scalar.activation(c_st[s][r, :], cn[r, :], ACT.Copy).then_inc(S["c_high"], 1)

            for dst, src in ((wq_raw, wq_d), (wk_raw, wk_d)):
                act.dma_start(dst, src).then_inc(S["w_in"], 16)
            act.wait_ge(S["spare_ready"], 1)
            nc.scalar.activation(spare[:], spare[:], ACT.Exp).then_inc(S["spare_used"], 1)
            stack_high((0, 0))

            def copy_q(m, ms, j):
                act.wait_ge(S["tq_done"], HC * m + j + 1)
                at_least(act, S["o_done"], m - 1)
                nc.scalar.activation(qT[ms][:, j, :], tqp[:], ACT.Copy).then_inc(S["qt_copied"], 1)

            def step(b, front, back, last_, more):
                n, s = num(b), b[1]
                m, ms = n - 1, 1 - s
                o = n - 2
                for j in range(HC):
                    if last_ and j == 0:
                        copy_q(o, s, HC - 1)
                    if back and j >= 1:
                        copy_q(m, ms, j - 1)
                    if back:
                        act.wait_ge(S["tk_done"], HC * m + j + 1)
                        at_least(act, S["kt_low"], HC * m + j - 1)
                        nc.scalar.activation(kT[j % 2][:], tkp[:], ACT.Copy).then_inc(S["kt_copied"], 1)
                        if j % 2 == 1:
                            at_least(act, S["g_step"], HC * m + j - 1)
                            nc.scalar.activation(kT_h[1][:], tkp[:], ACT.Copy).then_inc(S["kt_high1"], 1)
                    if last_ and j == 0:
                        act.wait_ge(S["g_step"], HC * (o + 1))
                        at_least(act, S["m_done"], o)
                        nc.scalar.activation(gsb[:], gmp[:], ACT.Copy).then_inc(S["g_copied"], 1)
                    if front:
                        if j == 0:
                            at_least(act, S["tk_done"], HC * (n - 1))
                            at_least(act, S["krec_done"], n - 1)
                            if isinstance(n, int) and n == 1:
                                act.wait_ge(S["wvo_done"], 1)
                        act.wait_ge(S["k_max"], HC * n + j + 1)
                        nc.scalar.activation(kexp[s][:, j, :], kp[j % 2][:], ACT.Exp, bias=knmax[:, s, j:j + 1],
                                             accum_out=ksum[:, s, j:j + 1]).then_inc(S["k_exp"], 1)
                        act.wait_ge(S["q_sub"], HC * n + j + 1)
                        nc.scalar.activation(qn[s][:, j, :], qn[s][:, j, :], ACT.Exp).then_inc(S["q_exp"], 1)
                    if more and j == 0:
                        stack_high(after(b))
                    if front and j == 2:
                        act.wait_ge((S["ct_in0"], S["ct_in1"])[s], 16 * (b[0] + 1))
                        at_least(act, S["g_step"], HC * (n - 1))
                        at_least(act, S["ct_stored"], n - 1)
                        nc.scalar.activation(c_parts[s][:, :, 0, :], cT[s][:], ACT.Copy).then_inc(S["ct_high"], 1)
                if last_:
                    act.wait_ge(S["o_done"], o + 1)
                    nc.scalar.activation(pair_rows(obuf, b[0] - 1, rows(s)), op[rows(s), :], ACT.Identity,
                                         bias=bo[rows(s), :]).then_inc(S["o_stored"], 1)

            steps(act.Fori, step)

        @block.vector
        def _(dve):
            chain = Chain(dve, S["dve_chain"])
            link = chain.link

            def layer_stats(p):
                link(nc.vector.bn_stats(stats[:], pair_of(xres, p)))
                nc.vector.memset(spare[:], 0.0)
                nc.vector.bn_aggr(moments[:], stats[:]).then_inc(S["stats_ready"], 1)

            def normalise(p):
                dve.wait_ge(S["rstd_ready"], p + 1)
                at_least(dve, S["x_stacked"], 2 * p)
                nc.vector.tensor_scalar(xn[:], pair_of(xres, p), moments[:, 0:1], rstd[:, 1:2],
                                        ALU.subtract, ALU.mult).then_inc(S["xn_ready"], 1)

            def stack_low(b):
                s, r, other = b[1], rows(b[1]), rows(1 - b[1])
                dve.wait_ge(S["c_high"], num(b) + 1)
                nc.vector.tensor_tensor(c_st[s][other, :], cn[r, :], plain(c_st[s][r, :]),
                                        ALU.subtract).then_inc(S["c_stacked"], 1)

            nc.vector.memset(spare[:], 0.0).then_inc(S["spare_ready"], 1)
            dve.wait_ge(S["spare_used"], 1)
            nc.vector.memset(krec[:], 0.0)
            dve.wait_ge(S["x_first"], 16)
            layer_stats(0)
            dve.wait_ge(S["w_in"], 32)
            nc.vector.tensor_copy(wq_h[:], wq_raw)
            link(nc.vector.tensor_copy(wk_h[:], wk_raw))
            normalise(0)
            nc.vector.tensor_tensor(wq_l[:], wq_raw, plain(wq_h[:]), ALU.subtract)
            nc.vector.tensor_tensor(wk_l[:], wk_raw, plain(wk_h[:]), ALU.subtract).then_inc(S["w_ready"], 1)
            stack_low((0, 0))

            def scale_value_output():
                dve.wait_ge(S["wvo_done"], 1)
                for half_rows in (rows(0), rows(1)):
                    by_head = wvo[half_rows, :].rearrange("p (c r o) -> p c r o", c=HC, r=2)
                    for r, bank in ((0, gmp), (1, op)):
                        last = nc.vector.tensor_scalar(by_head[:, :, r, :],
                                                       bank[0:SEQ, 0:HC * L0_DH].rearrange("p (c o) -> p c o", c=HC),
                                                       L0_DH ** -0.5, None, ALU.mult)
                last.then_inc(S["wvo_ready"], 1)

            def q_sum(n, s, j):
                dve.wait_ge(S["q_exp"], HC * n + j + 1)
                nc.vector.tensor_reduce(qsum[:, j, :], heads(qn[s][:, j, :]), AX.X, ALU.add).then_inc(S["q_summed0"], 1)

            def q_reciprocal(n, s, j):
                dve.wait_ge(S["q_summed0"], HC * n + j + 1)
                nc.vector.reciprocal(qrec[:, s, j, :], qsum[:, j, :]).then_inc(S["q_rec"], 1)

            def step(b, front, back, last_, more):
                n, s = num(b), b[1]
                m, ms = n - 1, 1 - s
                o = n - 2
                if more and s == 1:
                    if isinstance(n, int) and n == 1:
                        dve.wait_ge(S["x_rest"], 16)
                        nc.vector.memset(spare[:], 0.0)
                    layer_stats(b[0] + 1)
                for j in range(HC):
                    if isinstance(n, int) and n == 0 and j == 2:
                        scale_value_output()
                    if front:
                        dve.wait_ge(S["q_proj"], HC * n + j + 1)
                        nc.vector.tensor_reduce(qnmax[:, j, :], heads(qp[j % 2][:]), AX.X, ALU.max,
                                                negate=True).then_inc(S["q_max"], 1)
                        dve.wait_ge(S["k_proj"], HC * n + j + 1)
                        nc.vector.tensor_reduce(knmax[:, s, j:j + 1], kp[j % 2][:], AX.X, ALU.max,
                                                negate=True).then_inc(S["k_max"], 1)
                        dve.wait_ge(S["q_max"], HC * n + j + 1)
                        if j == 0:
                            at_least(dve, S["tq_done"], HC * (n - 1))
                        nc.vector.tensor_tensor(heads(qn[s][:, j, :]), heads(qp[j % 2][:]),
                                                spread(qnmax[:, j, :], L0_DH), ALU.add).then_inc(S["q_sub"], 1)
                    if front and j >= 1:
                        q_sum(n, s, j - 1)
                    if back and j % 2 == 0:
                        dve.wait_ge(S["kt_copied"], HC * m + j + 1)
                        at_least(dve, S["g_step"], HC * m + j - 1)
                        nc.vector.tensor_copy(kT_h[0][:], kT[0][:]).then_inc(S["kt_high0"], 1)
                    if front and j >= 1:
                        q_reciprocal(n, s, j - 1)
                    if back and j == 0:
                        dve.wait_ge(S["k_exp"], HC * (m + 1))
                        nc.vector.reciprocal(krec[:, ms, :], ksum[:, ms, :]).then_inc(S["krec_done"], 1)
                    if last_ and j == 1:
                        dve.wait_ge(S["m_done"], o + 1)
                        dve.wait_ge(S["krec_done"], o + 1)
                        at_least(dve, S["o_done"], o - 1)
                        for r in range(2):
                            mm = nc.vector.tensor_tensor(
                                mT[s][rows(r), :, :],
                                op[rows(r), :].rearrange("p (c r o) -> p c r o", c=HC, r=2)[:, :, r, :],
                                spread(krec[rows(r), s, :], SEQ), ALU.mult)
                        mm.then_inc(S["m_scaled"], 1)
                    if more and s == 1 and j == 0:
                        normalise(b[0] + 1)
                    if more and j == 1:
                        stack_low(after(b))
                    if back and j == 3:
                        dve.wait_ge(S["ct_split"], m + 1)
                        nc.vector.tensor_copy(context_columns(kvT, before(b)),
                                              c_parts[ms][:]).then_inc(S["ct_stored"], 1)
                if front:
                    q_sum(n, s, HC - 1)
                    q_reciprocal(n, s, HC - 1)

            steps(lambda a, b: chain.repeat(a, b, 1), step)

        @block.gpsimd
        def _(pool):
            chain = Chain(pool, S["pool_chain"])

            def layer_rstd(p):
                pool.wait_ge(S["stats_ready"], p + 1)
                chain.link(nc.gpsimd.tensor_tensor(rstd[:, 0:1], moments[:, 1:2], consts[:, LN_COL:LN_COL + 1],
                                                   ALU.add))
                nc.gpsimd.tensor_tensor(rstd[:, 1:2], rstd[:, 0:1], consts[:, 0:1],
                                        ALU.pow).then_inc(S["rstd_ready"], 1)

            layer_rstd(0)

            def stack_low(b):
                s, r, other = b[1], rows(b[1]), rows(1 - b[1])
                pool.wait_ge(S["x_high"], num(b) + 1)
                nc.gpsimd.tensor_tensor(x_st[s][other, :], xn[r, :], plain(x_st[s][r, :]),
                                        ALU.subtract).then_inc(S["x_stacked"], 1)
                pool.wait_ge(S["x_stacked"], num(b) + 1)

            def q_normalise(n, s, j):
                pool.wait_ge(S["q_rec"], HC * n + j + 1)
                nc.gpsimd.tensor_tensor(heads(qn[s][:, j, :]), heads(qn[s][:, j, :]),
                                        spread(qrec[:, s, j, :], L0_DH), ALU.mult).then_inc(S["q_norm"], 1)

            stack_low((0, 0))

            def step(b, front, back, last_, more):
                n, s = num(b), b[1]
                m, ms = n - 1, 1 - s
                if more and s == 1:
                    layer_rstd(b[0] + 1)
                for j in range(HC):
                    if back:
                        pool.wait_ge((S["kt_high0"], S["kt_high1"])[j % 2], HC // 2 * m + j // 2 + 1)
                        nc.gpsimd.tensor_tensor(kT_l[j % 2][:], kT[j % 2][:], plain(kT_h[j % 2][:]),
                                                ALU.subtract).then_inc(S["kt_low"], 1)
                    if front and j >= 1:
                        q_normalise(n, s, j - 1)
                    if more and j == 1:
                        pool.wait_ge(S["q_norm"], HC * n + 1)
                        stack_low(after(b))
                    if front and j == 2:
                        pool.wait_ge(S["ct_high"], n + 1)
                        nc.gpsimd.tensor_tensor(c_parts[s][:, :, 1, :], cT[s][:], plain(c_parts[s][:, :, 0, :]),
                                                ALU.subtract).then_inc(S["ct_split"], 1)
                if front:
                    q_normalise(n, s, HC - 1)

            steps(lambda a, b: chain.repeat(a, b, 1), step)


def pair_of(t, p):
    return t[:, bass.ds(p, 1), :].rearrange("p t n -> p (t n)")


def context_columns(kvT, batch):
    pair, s = batch
    return kvT[:, :, bass.ds(pair, 1), :, s * 3 * SEQ:s * 3 * SEQ + SEQ].rearrange("p c b r t -> p (c b) r t")


def x_columns(kvT, p, part):
    return kvT[:, :, bass.ds(p, 1), part, SEQ:3 * SEQ].rearrange("p c b t -> p (c b) t")


def pair_rows(t, p, r):
    return t[r, bass.ds(p, 1), :].rearrange("p t n -> p (t n)")


def norm_and_ffn(nc, sems, attention_sems, const, xres, kvT, obuf, raw, dram):
    ident, consts = const
    g_d, in_d, out_d, br_d, w_d = dram
    NR = FFN_LOW + FFN_HEADS
    st = ExitStack()
    with st:
        sb = lambda name, shape, dt=FP32: st.enter_context(nc.sbuf_tensor(name, shape, dt))
        ps = lambda name: st.enter_context(nc.psum_tensor(name, [P, 512], FP32))
        w_in, w_out = sb("ffn_in", [P, HC, NR]), sb("ffn_out", [P, HIDDEN])
        g, g8, br = sb("g", [P, 1]), sb("g8", [P, 1]), sb("br", [P, FFN_HEADS])
        same_batch = sb("same_batch", [P, P])
        sq, scaled = sb("sq", [P, HIDDEN]), sb("scaled", [P, HIDDEN])
        ssum, rnorm = sb("ssum", [P, 2 * HC]), sb("rnorm", [P, 2 * HC])
        rwide = sb("rwide", [P, HC, 2, SEQ])
        yn, yT = sb("yn", [P, HIDDEN]), sb("yT", [P, HIDDEN])
        zn = sb("zn", [P, HIDDEN])
        logit, share = sb("logit", [P, FFN_HEADS]), sb("share", [P, FFN_HEADS])
        e8, small = sb("e8", [P, FFN_HEADS]), sb("small", [P, 4])
        low, lowT = sb("low", [P, FFN_LOW]), sb("lowT", [P, FFN_LOW])
        ystats, ymom, yr = sb("ystats", [P, 6]), sb("ymom", [P, 2]), sb("yr", [P, 3])
        zstats, zmom, zr = sb("zstats", [P, 6]), sb("zmom", [P, 2]), sb("zr", [P, 3])
        spare = sb("spare2", [P, 1])
        ssp, rp, ytp, ztp = ps("ssp"), ps("rp"), ps("ytp"), ps("ztp")
        rlp, ltp, fp = ps("rlp"), ps("ltp"), ps("fp")
        S = sems
        block = st.enter_context(nc.Block())

        def steps(repeat, step):
            for k in range(4):
                step(k, 2, True, k >= 1, k >= 2, k >= 3)
            with repeat(4, HP - 2) as k:
                step(k, 2, True, True, True, True)
            for k in range(HP - 2, HP):
                step(k, HP - 1 - k, True, True, True, True)
            step(HP, 0, False, True, True, True)
            step(HP + 1, 0, False, False, True, True)
            step(HP + 2, 0, False, False, False, True)

        @block.sync
        def _(sp):
            for dst, src in ((w_in[:], in_d), (w_out[:], out_d), (g[:], g_d), (br[:], br_d)):
                sp.dma_start(dst, src).then_inc(S["f_in"], 16)
            for j in range(RAW):
                sp.dma_start(raw[j][:], w_d[0, :, j * W_CHUNK:(j + 1) * W_CHUNK]).then_inc(
                    attention_sems[f"w_in{j}"], 16)

        @block.tensor
        def _(pe):
            pe.wait_ge(S["ones_ready"], 1)

            def sum_squares(k):
                pe.wait_ge(S["sq_done"], k + 1)
                at_least(pe, S["ssum_ready"], k)
                for c in range(HC):
                    mm = nc.tensor.matmul(ssp[:, c * P:(c + 1) * P], sq[:, c * P:(c + 1) * P], same_batch[:],
                                          start=True, stop=True)
                mm.then_inc(S["ss_done"], 1)

            sum_squares(0)

            def step(k, ahead, a, r, f, z):
                if a:
                    pe.wait_ge(S["rwide_ready"], k + 1)
                    at_least(pe, S["scaled_ready"], k)
                    for c in range(HC):
                        mm = nc.tensor.transpose(rp[:, c * P:(c + 1) * P],
                                                 rwide[:, c, :, :].rearrange("p b o -> p (b o)"), ident[:])
                    mm.then_inc(S["rp_done"], 1)
                if z:
                    pe.wait_ge(S["zn_ready"], k - 2)
                    at_least(pe, S["z_split"], k - 3)
                    for c in range(HC):
                        mm = nc.tensor.transpose(ztp[:, c * P:(c + 1) * P], zn[:, c * P:(c + 1) * P], ident[:])
                    mm.then_inc(S["zt_done"], 1)
                if f:
                    pe.wait_ge(S["low_ready"], k - 1)
                    at_least(pe, S["lt_copied"], k - 2)
                    nc.tensor.transpose(ltp[:, 0:P], low[:], ident[:]).then_inc(S["lt_done"], 1)
                if ahead >= 1:
                    sum_squares(k + 1)
                if f:
                    pe.wait_ge(S["lt_copied"], k - 1)
                    at_least(pe, S["x2_ready"], k - 2)
                    nc.tensor.matmul(fp[:], lowT[:], w_out[:], start=True, stop=True).then_inc(S["f_done"], 1)
                if r:
                    pe.wait_ge(S["yn_ready"], k)
                    at_least(pe, S["yt_copied"], k - 1)
                    for c in range(HC):
                        mm = nc.tensor.transpose(ytp[:, c * P:(c + 1) * P], yn[:, c * P:(c + 1) * P], ident[:])
                    mm.then_inc(S["yt_done"], 1)
                if r:
                    if isinstance(k, int) and k == 1:
                        pe.wait_ge(S["f_ready"], 1)
                    pe.wait_ge(S["yt_copied"], k)
                    at_least(pe, S["low_ready"], k - 1)
                    for c in range(HC):
                        mm = nc.tensor.matmul(rlp[:, 0:NR], yT[:, c * P:(c + 1) * P], w_in[:, c, :],
                                              start=(c == 0), stop=(c == HC - 1))
                    mm.then_inc(S["rl_done"], 1)

            steps(pe.Fori, step)

        @block.scalar
        def _(act):
            def square(k):
                at_least(act, S["ss_done"], k)
                nc.scalar.activation(sq[:], pair_of(obuf, k), ACT.Square).then_inc(S["sq_done"], 1)

            square(0)
            square(1)

            def step(k, ahead, a, r, f, z):
                if z:
                    act.wait_ge(S["zr_ready"], k - 2)
                    at_least(act, S["zt_done"], k - 3)
                    nc.scalar.activation(zn[:], pair_of(xres, k - 3), ACT.Identity, bias=zr[:, 2:3],
                                         scale=zr[:, 1:2]).then_inc(S["zn_ready"], 1)
                if f:
                    act.wait_ge(S["lt_done"], k - 1)
                    at_least(act, S["f_done"], k - 2)
                    nc.scalar.activation(lowT[:], ltp[:, 0:P], ACT.Copy).then_inc(S["lt_copied"], 1)
                if r:
                    act.wait_ge(S["yr_ready"], k)
                    at_least(act, S["yt_done"], k - 1)
                    nc.scalar.activation(yn[:], pair_of(xres, k - 1), ACT.Identity, bias=yr[:, 2:3],
                                         scale=yr[:, 1:2]).then_inc(S["yn_ready"], 1)
                if z:
                    act.wait_ge(S["zt_done"], k - 2)
                    nc.scalar.activation(x_columns(kvT, k - 3, 0), ztp[:].rearrange("p (c t) -> p c t", c=HC),
                                         ACT.Copy).then_inc(S["z_high"], 1)
                if r:
                    act.wait_ge(S["yt_done"], k)
                    at_least(act, S["rl_done"], k - 1)
                    nc.scalar.activation(yT[:], ytp[:], ACT.Copy).then_inc(S["yt_copied"], 1)
                if ahead == 2:
                    square(k + 2)
                if r:
                    act.wait_ge(S["logit_ready"], k)
                    nc.scalar.activation(e8[:], logit[:], ACT.Exp, bias=small[:, 0:1],
                                         accum_out=small[:, 1:2]).then_inc(S["e_done"], 1)

            steps(act.Fori, step)

        @block.gpsimd
        def _(pool):
            chain = Chain(pool, S["pool_chain2"])

            def inverse_norm(k):
                pool.wait_ge(S["ssum_ready"], k + 1)
                at_least(pool, S["rwide_ready"], k)
                nc.gpsimd.tensor_tensor(rnorm[:], ssum[:], consts[:, 0:2 * HC], ALU.pow).then_inc(S["rnorm_ready"], 1)

            inverse_norm(0)

            def step(k, ahead, a, r, f, z):
                if r:
                    pool.wait_ge(S["ystats_ready"], k)
                    at_least(pool, S["yn_ready"], k - 1)
                    inverse_root(nc, chain, ymom, yr, consts).then_inc(S["yr_ready"], 1)
                if a:
                    pool.wait_ge(S["scaled_ready"], k + 1)
                    nc.gpsimd.tensor_tensor(pair_of(xres, k), pair_of(xres, k), scaled[:],
                                            ALU.add).then_inc(S["x1_ready"], 1)
                if ahead >= 1:
                    inverse_norm(k + 1)
                if f:
                    pool.wait_ge(S["zstats_ready"], k - 1)
                    at_least(pool, S["zn_ready"], k - 2)
                    inverse_root(nc, chain, zmom, zr, consts).then_inc(S["zr_ready"], 1)

            steps(lambda a, b: chain.repeat(a, b, 6), step)

        @block.vector
        def _(dve):
            chain = Chain(dve, S["dve_chain2"])
            link = chain.link
            link(nc.vector.memset(same_batch[:], 0.0))
            nc.vector.memset(same_batch[0:SEQ, 0:SEQ], 1.0)
            nc.vector.memset(same_batch[SEQ:P, SEQ:P], 1.0).then_inc(S["ones_ready"], 1)

            def bound_sum(k):
                dve.wait_ge(S["ss_done"], k + 1)
                at_least(dve, S["rnorm_ready"], k)
                nc.vector.tensor_scalar(ssum[:], ssp[:].rearrange("p (n o) -> p n o", o=SEQ)[:, :, 0], 1e-24, None,
                                        ALU.max).then_inc(S["ssum_ready"], 1)

            def widen(k):
                dve.wait_ge(S["rnorm_ready"], k + 1)
                at_least(dve, S["rp_done"], k)
                nc.vector.tensor_copy(rwide[:], spread(rnorm[:].rearrange("p (c b) -> p c b", c=HC),
                                                       SEQ)).then_inc(S["rwide_ready"], 1)

            bound_sum(0)
            widen(0)
            dve.wait_ge(S["f_in"], 64)
            link(nc.vector.tensor_scalar(g8[:], g[:], math.sqrt(SEQ), None, ALU.mult))
            nc.vector.memset(small[:], 0.0).then_inc(S["f_ready"], 1)

            def step(k, ahead, a, r, f, z):
                if r:
                    dve.wait_ge(S["x1_ready"], k)
                    nc.vector.memset(spare[:], 0.0)
                    link(nc.vector.bn_stats(ystats[:], pair_of(xres, k - 1)))
                    at_least(dve, S["yr_ready"], k - 1)
                    nc.vector.memset(spare[:], 0.0)
                    nc.vector.bn_aggr(ymom[:], ystats[:]).then_inc(S["ystats_ready"], 1)
                if f:
                    dve.wait_ge(S["e_done"], k - 1)
                    link(nc.vector.reciprocal(small[:, 2:3], small[:, 1:2]))
                    link(nc.vector.tensor_scalar(share[:], e8[:], small[:, 2:3], FFN_HEADS * FFN_SCALING,
                                                 ALU.mult, ALU.mult))
                    at_least(dve, S["lt_done"], k - 2)
                    nc.vector.tensor_tensor(low[:].rearrange("p (h r) -> p h r", h=FFN_HEADS),
                                            rlp[:, 0:FFN_LOW].rearrange("p (h r) -> p h r", h=FFN_HEADS),
                                            spread(share[:], FFN_R), ALU.mult).then_inc(S["low_ready"], 1)
                if a:
                    dve.wait_ge(S["rp_done"], k + 1)
                    at_least(dve, S["x1_ready"], k)
                    nc.vector.scalar_tensor_tensor(scaled[:], pair_of(obuf, k), g8[:], rp[:],
                                                   ALU.mult, ALU.mult).then_inc(S["scaled_ready"], 1)
                if ahead >= 1:
                    bound_sum(k + 1)
                if f:
                    dve.wait_ge(S["f_done"], k - 1)
                    nc.vector.tensor_tensor(pair_of(xres, k - 2), fp[:], pair_of(xres, k - 2),
                                            ALU.add).then_inc(S["x2_ready"], 1)
                    dve.wait_ge(S["x2_ready"], k - 1)
                    nc.vector.memset(spare[:], 0.0)
                    link(nc.vector.bn_stats(zstats[:], pair_of(xres, k - 2)))
                    at_least(dve, S["zr_ready"], k - 2)
                    nc.vector.memset(spare[:], 0.0)
                    nc.vector.bn_aggr(zmom[:], zstats[:]).then_inc(S["zstats_ready"], 1)
                if z:
                    dve.wait_ge(S["z_high"], k - 2)
                    nc.vector.tensor_tensor(x_columns(kvT, k - 3, 1), ztp[:].rearrange("p (c t) -> p c t", c=HC),
                                            plain(x_columns(kvT, k - 3, 0)), ALU.subtract).then_inc(S["z_split"], 1)
                if ahead >= 1:
                    widen(k + 1)
                if r:
                    dve.wait_ge(S["rl_done"], k)
                    link(nc.vector.tensor_tensor(logit[:], rlp[:, FFN_LOW:NR], br[:], ALU.add))
                    nc.vector.tensor_reduce(small[:, 0:1], logit[:], AX.X, ALU.max,
                                            negate=True).then_inc(S["logit_ready"], 1)

            steps(lambda a, b: chain.repeat(a, b, 5), step)


def ffn_raw(raw, c):
    return raw[2 * c][:, 0:HIDDEN].bitcast(INT32), raw[2 * c + 1][:, 0:HIDDEN]


def grouped_attention(nc, sems, ffn_sems, half, const, xres, kvT, raw, dram, ffn_dram):
    ident, consts = const
    w_d, qk_d = dram
    STEPS = L1_KV * HP
    LAG = 3
    st = ExitStack()
    with st:
        sb = lambda name, shape, dt=FP32: st.enter_context(nc.sbuf_tensor(name, shape, dt))
        ps = lambda name: st.enter_context(nc.psum_tensor(name, [P, 512], FP32))
        w = sb("l1_w", [P, 2, 2, W_COLS], FP32R)
        qk_w, qk = sb("qk_w", [P, 2]), sb("qk", [P, 1])
        q_sq, k_sq = sb("q_sq", [P, 512]), sb("k_sq", [P, 2, P])
        q_ss, k_ss = sb("q_ss", [P, GROUP]), sb("k_ss", [P, 2])
        q_ms, k_ms = sb("q_ms", [P, GROUP]), sb("k_ms", [P, 2])
        q_r, k_r = sb("q_r", [P, GROUP]), sb("k_r", [P, 2])
        qs = sb("qs", [P, 512])
        ks = [sb(f"ks{j}", [P, 2, P]) for j in range(2)]
        v = [sb(f"v{j}", [P, 2, 2, P], FP32R) for j in range(4)]
        qT, kT = sb("l1_qT", [P, 2, GROUP * SEQ]), sb("l1_kT", [P, 2, P])
        nmax, bias = sb("nmax", [P, 4]), sb("bias", [P, 4])
        psum_, prec = sb("psums", [P, 4]), sb("prec", [P, 4])
        pe_, pn = sb("p_exp", [P, 4, P]), sb("p_norm", [P, 4, P])
        pT = sb("pT", [P, 2, 2, GROUP * SEQ], FP32R)
        oT = sb("oT", [P, 2, GROUP, P], FP32R)
        kvp, qp, qtp, ktp = ps("kvp"), ps("l1_qp"), ps("qtp"), ps("ktp")
        sp_, ptp, op, yp = ps("scp"), ps("ptp"), ps("l1_op"), ps("yp")
        S = sems
        w_in = [S[f"w_in{j}"] for j in range(RAW)]
        block = st.enter_context(nc.Block())

        def chunks_to(column):
            return -(-column // W_CHUNK)

        def slot(g):
            return g % 2

        def weights(g, part, first, count):
            sl = slot(g)
            if isinstance(sl, int):
                return w[:, sl, part, first:first + count]
            return w[:, bass.ds(sl, 1), part, first:first + count].rearrange("p s n -> p (s n)")

        def steps(repeat, step):
            for t in range(HP):
                step(0, t, [t >= lag for lag in range(LAG + 1)], True)
            with repeat(1, L1_KV - 1) as g:
                for t in range(HP):
                    step(g, t, [True] * (LAG + 1), True)
            for t in range(HP):
                step(L1_KV - 1, t, [True] * (LAG + 1), False)
            for t in range(LAG):
                step(L1_KV, t, [t < lag for lag in range(LAG + 1)], False)

        @block.sync
        def _(sp):
            sp.dma_start(qk_w[:], qk_d).then_inc(S["qk_in"], 16)

            def load(g, j):
                at_least(sp, S["w_split"], W_CHUNKS * g + j + 1 - RAW)
                src = w_d[g, :, j * W_CHUNK:(j + 1) * W_CHUNK] if isinstance(g, int) else \
                    w_d[bass.ds(g, 1), :, j * W_CHUNK:(j + 1) * W_CHUNK].rearrange("g p n -> p (g n)")
                sp.dma_start(raw[j % RAW][:], src).then_inc(w_in[j % RAW], 16)

            for j in range(RAW, W_CHUNKS):
                load(0, j)
            with sp.Fori(1, L1_KV) as g:
                for j in range(W_CHUNKS):
                    load(g, j)
            sp.wait_ge(S["w_split"], W_CHUNKS * L1_KV)
            for c in range(RAW // 2):
                integers, scales = ffn_raw(raw, c)
                for dst, src in ((integers, ffn_dram[0]), (scales, ffn_dram[1])):
                    sp.dma_start(dst, src[:, c * HIDDEN:(c + 1) * HIDDEN]).then_inc(ffn_sems[f"u_in{c}"], 16)

        def chunk_in(engine, g, j):
            engine.wait_ge(w_in[j % RAW], (W_CHUNKS // RAW * g + j // RAW + 1) * 16)

        @block.tensor
        def _(pe):
            def three(out, stationary, moving, first, last):
                nc.tensor.matmul(out, stationary[0], moving[0], start=first, stop=False)
                nc.tensor.matmul(out, stationary[0], moving[1], start=False, stop=False)
                return nc.tensor.matmul(out, stationary[1], moving[0], start=False, stop=last)

            def step(g, t, on, split):
                i = HP * g + t
                if on[0]:
                    if t == 0:
                        pe.wait_ge(S["w_split"], W_CHUNKS * g + chunks_to(W_Q))
                    at_least(pe, S["k_scaled"], i)
                    for b in range(2):
                        for c in range(HC):
                            mm = three(kvp[:, b * 256:(b + 1) * 256],
                                       [kvT[:, c, t, part, b * P:(b + 1) * P] for part in range(2)],
                                       [weights(g, part, W_KV + c * 256, 256) for part in range(2)],
                                       c == 0, c == HC - 1)
                    mm.then_inc(S["kv_done"], 1)
                if on[1]:
                    pe.wait_ge(S["k_scaled"], i)
                    at_least(pe, S["kt_copied1"], i - 1)
                    for b in range(2):
                        mm = nc.tensor.transpose(ktp[:, b * P:(b + 1) * P], ks[(t - 1) % 2][:, b, :], ident[:])
                    mm.then_inc(S["kt_done"], 1)
                    pe.wait_ge(S["q_scaled"], i)
                    at_least(pe, S["qt_copied1"], i - 1)
                    for h in range(GROUP):
                        mm = nc.tensor.transpose(qtp[:, h * P:(h + 1) * P], qs[:, h * P:(h + 1) * P], ident[:])
                    mm.then_inc(S["qt_done"], 1)
                if on[0]:
                    at_least(pe, S["q_scaled"], i)
                    if t == 0:
                        pe.wait_ge(S["w_split"], W_CHUNKS * g + chunks_to(W_O))
                    for c in range(HC):
                        mm = three(qp[:], [kvT[:, c, t, part, SEQ:3 * SEQ] for part in range(2)],
                                   [weights(g, part, W_Q + c * 512, 512) for part in range(2)],
                                   c == 0, c == HC - 1)
                    mm.then_inc(S["q_done"], 1)
                if on[1]:
                    pe.wait_ge(S["kt_copied1"], i)
                    pe.wait_ge(S["qt_copied1"], i)
                    at_least(pe, S["p_done"], i - 1)
                    for b in range(2):
                        for hh in range(2):
                            at = (2 * b + hh) * P
                            mm = nc.tensor.matmul(sp_[:, at:at + P], qT[:, b, hh * P:(hh + 1) * P],
                                                  kT[:, b, :], start=True, stop=True)
                    mm.then_inc(S["s_done"], 1)
                if on[2]:
                    pe.wait_ge(S["p_normed"], i - 1)
                    at_least(pe, S["pt_split"], i - 2)
                    for a in range(4):
                        mm = nc.tensor.transpose(ptp[:, a * P:(a + 1) * P], pn[:, a, :], ident[:])
                    mm.then_inc(S["pt_done"], 1)
                if on[3]:
                    og = g if t >= LAG else g - 1
                    if t == LAG:
                        pe.wait_ge(S["w_split"], W_CHUNKS * (g + 1))
                    pe.wait_ge(S["o_split"], i - 2)
                    at_least(pe, S["y_added"], i - 3)
                    for h in range(GROUP):
                        mm = three(yp[:], [oT[:, part, h, :] for part in range(2)],
                                   [weights(og, part, W_O + h * 512, 512) for part in range(2)],
                                   h == 0, h == GROUP - 1)
                    mm.then_inc(S["y_done"], 1)
                if on[2]:
                    pe.wait_ge(S["pt_split"], i - 1)
                    at_least(pe, S["o_split"], i - 2)
                    vs = v[(t - 2) % 4]
                    for b in range(2):
                        mm = three(op[:, b * 256:(b + 1) * 256], [vs[:, part, b, :] for part in range(2)],
                                   [pT[:, part, b, :] for part in range(2)], True, True)
                    mm.then_inc(S["o_done1"], 1)

            steps(pe.Fori, step)

        def by_batch(t):
            return t.rearrange("p h (b q) -> p b h q", b=2)

        def by_head(t):
            return t[:].rearrange("p (b h q) -> p b h q", b=2, h=GROUP)

        def bank(t, b=2):
            return t[:].rearrange("p (b n) -> p b n", b=b)

        @block.scalar
        def _(act):
            def split_high(g, j):
                chunk_in(act, g, j)
                nc.scalar.activation(weights(g, 0, j * W_CHUNK, W_CHUNK), raw[j % RAW][:],
                                     ACT.Copy).then_inc(S["w_high"], 1)

            for j in range(W_CHUNKS):
                split_high(0, j)

            def step(g, t, on, split):
                i = HP * g + t
                if on[3]:
                    act.wait_ge(S["o_done1"], i - 2)
                    at_least(act, S["y_done"], i - 3)
                    nc.scalar.activation(by_batch(oT[:, 0, :, :]), by_head(op), ACT.Copy).then_inc(S["o_high"], 1)
                if on[0]:
                    act.wait_ge(S["kv_done"], i + 1)
                    at_least(act, S["k_summed"], i)
                    nc.scalar.activation(k_sq[:], bank(kvp)[:, :, 0:P], ACT.Square).then_inc(S["k_squared"], 1)
                    at_least(act, S["o_done1"], i - 3)
                    nc.scalar.activation(v[t % 4][:, 0, :, :], bank(kvp)[:, :, P:2 * P],
                                         ACT.Copy).then_inc(S["v_high"], 1)
                if on[1]:
                    act.wait_ge(S["kt_done"], i)
                    at_least(act, S["s_done"], i - 1)
                    nc.scalar.activation(kT[:], bank(ktp)[:, 0, :].rearrange("p (b n) -> p b n", b=2), ACT.Copy,
                                         scale=qk[:, 0:1]).then_inc(S["kt_copied1"], 1)
                    act.wait_ge(S["qt_done"], i)
                    nc.scalar.activation(qT[:].rearrange("p b (h q) -> p h b q", h=GROUP),
                                         qtp[:].rearrange("p (h b q) -> p h b q", h=GROUP, b=2),
                                         ACT.Copy).then_inc(S["qt_copied1"], 1)
                if split:
                    if t <= LAG:
                        at_least(act, S["q_done"], HP * g)
                    else:
                        at_least(act, S["y_done"], HP * g)
                    split_high(g + 1, t)
                if on[0]:
                    act.wait_ge(S["q_done"], i + 1)
                    at_least(act, S["q_summed"], i)
                    nc.scalar.activation(q_sq[:], qp[:], ACT.Square).then_inc(S["q_squared"], 1)
                if on[2]:
                    act.wait_ge(S["pt_done"], i - 1)
                    at_least(act, S["o_done1"], i - 2)
                    nc.scalar.activation(pT[:, 0, :, :].rearrange("p b n -> p (b n)"), ptp[:],
                                         ACT.Copy).then_inc(S["pt_high"], 1)
                if on[1]:
                    act.wait_ge(S["bias_ready"], i)
                    at_least(act, S["p_normed"], i - 1)
                    for a in range(4):
                        last = nc.scalar.activation(pe_[:, a, :], sp_[:, a * P:(a + 1) * P], ACT.Exp,
                                                    bias=bias[:, a:a + 1], scale=L1_SCALE,
                                                    accum_out=psum_[:, a:a + 1])
                    last.then_inc(S["p_done"], 1)

            steps(act.Fori, step)

        @block.gpsimd
        def _(pool):
            chain = Chain(pool, S["pool_chain3"])

            def split_low(g, j):
                pool.wait_ge(S["w_high"], W_CHUNKS * g + j + 1)
                nc.gpsimd.tensor_tensor(weights(g, 1, j * W_CHUNK, W_CHUNK), raw[j % RAW][:],
                                        plain(weights(g, 0, j * W_CHUNK, W_CHUNK)),
                                        ALU.subtract).then_inc(S["w_split"], 1)

            pool.wait_ge(S["w_split"], W_CHUNKS)

            def rms(total, mean, root, n):
                chain.link(nc.gpsimd.tensor_tensor(mean[:], total[:], consts[:, RMS_COL:RMS_COL + n], ALU.add))
                return nc.gpsimd.tensor_tensor(root[:], mean[:], consts[:, 0:n], ALU.pow)

            def step(g, t, on, split):
                i = HP * g + t
                if on[0]:
                    pool.wait_ge(S["k_summed"], i + 1)
                    rms(k_ss, k_ms, k_r, 2).then_inc(S["k_root"], 1)
                if split:
                    split_low(g + 1, t)
                if on[0]:
                    pool.wait_ge(S["q_summed"], i + 1)
                    rms(q_ss, q_ms, q_r, GROUP).then_inc(S["q_root"], 1)
                if on[1]:
                    pool.wait_ge(S["prec_ready"], i)
                    at_least(pool, S["pt_done"], i - 1)
                    nc.gpsimd.tensor_tensor(pn[:], pe_[:], spread(prec[:], P), ALU.mult).then_inc(S["p_normed"], 1)

            steps(lambda a, b: chain.repeat(a, b, 2 * HP), step)

        @block.vector
        def _(dve):
            chain = Chain(dve, S["dve_chain3"])
            link = chain.link
            dve.wait_ge(S["qk_in"], 16)
            link(nc.vector.scalar_tensor_tensor(qk[:], qk_w[:, 0:1], float(L1_DH), qk_w[:, 1:2], ALU.mult, ALU.mult))

            for j in range(W_CHUNKS):
                dve.wait_ge(S["w_high"], j + 1)
                nc.vector.tensor_tensor(weights(0, 1, j * W_CHUNK, W_CHUNK), raw[j % RAW][:],
                                        plain(weights(0, 0, j * W_CHUNK, W_CHUNK)),
                                        ALU.subtract).then_inc(S["w_split"], 1)

            def step(g, t, on, split):
                i = HP * g + t
                if on[3]:
                    dve.wait_ge(S["o_high"], i - 2)
                    at_least(dve, S["y_done"], i - 3)
                    nc.vector.tensor_tensor(by_batch(oT[:, 1, :, :]), by_head(op),
                                            plain(by_batch(oT[:, 0, :, :])), ALU.subtract).then_inc(S["o_split"], 1)
                if on[0]:
                    dve.wait_ge(S["k_squared"], i + 1)
                    nc.vector.tensor_reduce(k_ss[:], k_sq[:], AX.X, ALU.add).then_inc(S["k_summed"], 1)
                    dve.wait_ge(S["v_high"], i + 1)
                    nc.vector.tensor_tensor(v[t % 4][:, 1, :, :], bank(kvp)[:, :, P:2 * P],
                                            plain(v[t % 4][:, 0, :, :]), ALU.subtract).then_inc(S["v_split"], 1)
                    dve.wait_ge(S["k_root"], i + 1)
                    nc.vector.tensor_tensor(ks[t % 2][:], bank(kvp)[:, :, 0:P], spread(k_r[:], P),
                                            ALU.mult).then_inc(S["k_scaled"], 1)
                    dve.wait_ge(S["q_squared"], i + 1)
                    nc.vector.tensor_reduce(q_ss[:], q_sq[:].rearrange("p (h d) -> p h d", h=GROUP), AX.X,
                                            ALU.add).then_inc(S["q_summed"], 1)
                if on[1]:
                    dve.wait_ge(S["s_done"], i)
                    link(nc.vector.tensor_reduce(nmax[:], sp_[:].rearrange("p (a k) -> p a k", a=4), AX.X,
                                                 ALU.max, negate=True))
                    nc.vector.tensor_scalar(bias[:], nmax[:], L1_SCALE, None, ALU.mult).then_inc(S["bias_ready"], 1)
                if on[2]:
                    dve.wait_ge(S["pt_high"], i - 1)
                    nc.vector.tensor_tensor(pT[:, 1, :, :].rearrange("p b n -> p (b n)"), ptp[:],
                                            plain(pT[:, 0, :, :].rearrange("p b n -> p (b n)")),
                                            ALU.subtract).then_inc(S["pt_split"], 1)
                if on[0]:
                    dve.wait_ge(S["q_root"], i + 1)
                    nc.vector.tensor_tensor(qs[:].rearrange("p (h d) -> p h d", h=GROUP),
                                            qp[:].rearrange("p (h d) -> p h d", h=GROUP), spread(q_r[:], P),
                                            ALU.mult).then_inc(S["q_scaled"], 1)
                if on[1]:
                    dve.wait_ge(S["p_done"], i)
                    nc.vector.reciprocal(prec[:], psum_[:]).then_inc(S["prec_ready"], 1)
                if on[3]:
                    dve.wait_ge(S["y_done"], i - 2)
                    at = xres[:, (t - LAG) % HP, :]
                    nc.vector.tensor_tensor(at, yp[:], at, ALU.add).then_inc(S["y_added"], 1)

            steps(lambda a, b: chain.repeat(a, b, HP), step)


def quantised_ffn(nc, sems, half, const, xres, raw, dram, out):
    ident, consts = const
    wq_d, sc_d = dram
    st = ExitStack()
    with st:
        sb = lambda name, shape, dt=FP32: st.enter_context(nc.sbuf_tensor(name, shape, dt))
        ps = lambda name: st.enter_context(nc.psum_tensor(name, [P, 512], FP32))
        early = RAW // 2
        loaded = [ffn_raw(raw, c) for c in range(early)] + [
            (sb(f"f1_wq{c}", [P, HIDDEN], INT32)[:], sb(f"f1_sc{c}", [P, HIDDEN])[:]) for c in range(early, HC)]
        wf = sb("f1_w", [P, HC, HIDDEN])
        w_h, w_l = sb("f1_wh", [P, HC, HIDDEN], FP32R), sb("f1_wl", [P, HC, HIDDEN], FP32R)
        u = sb("u", [P, HIDDEN])
        uT_h = [sb(f"uT_h{j}", [P, HIDDEN], FP32R) for j in range(2)]
        uT_l = [sb(f"uT_l{j}", [P, HIDDEN], FP32R) for j in range(2)]
        ustats, umom, ur = sb("ustats", [P, 6]), sb("umom", [P, 2]), sb("ur", [P, 3])
        spare = sb("spare3", [P, 1])
        utp, fp = ps("utp"), [ps(f"f1p{j}") for j in range(2)]
        S = sems
        w_in = [S[f"u_in{c}"] for c in range(HC)]
        block = st.enter_context(nc.Block())

        def steps(repeat, step):
            for k in range(2):
                step(k, k, 2)
            with repeat(1, HP // 2 - 1) as j:
                for s in range(2):
                    step(2 * j + s, s, 2)
            for s in range(2):
                step(HP - 2 + s, s, 1 - s)
            step(HP, 0, -1)

        @block.sync
        def _(sp):
            for c in range(early, HC):
                sp.dma_start(loaded[c][0], wq_d[:, c * HIDDEN:(c + 1) * HIDDEN]).then_inc(w_in[c], 16)
            with sp.Fori(0, HP) as k:
                sp.wait_ge(S["out_ready"], k + 1)
                sp.dma_start(out[bass.ds((half * HP + k) * P, P), :], pair_of(xres, k)).then_inc(S["stored"], 16)
            sp.wait_ge(S["stored"], 16 * HP)

        @block.tensor
        def _(pe):
            def step(k, s, ahead):
                first = isinstance(k, int) and k == 1
                if ahead >= 0:
                    pe.wait_ge(S["un_ready"], k + 1)
                    at_least(pe, S["ut_split"], k)
                    for c in range(HC):
                        mm = nc.tensor.transpose(utp[:, c * P:(c + 1) * P], u[:, c * P:(c + 1) * P], ident[:])
                    mm.then_inc(S["ut_done"], 1)
                if not (isinstance(k, int) and k == 0):
                    pe.wait_ge(S["ut_split"], k)
                    at_least(pe, S["out_ready"], k - 2)
                    bank, uh, ul = fp[1 - s], uT_h[1 - s], uT_l[1 - s]
                    for c in range(HC):
                        if first:
                            pe.wait_ge(S["w_split1"], c + 1)
                        xc = slice(c * P, (c + 1) * P)
                        nc.tensor.matmul(bank[:], uh[:, xc], w_h[:, c, :], start=(c == 0), stop=False)
                        nc.tensor.matmul(bank[:], uh[:, xc], w_l[:, c, :], start=False, stop=False)
                        mm = nc.tensor.matmul(bank[:], ul[:, xc], w_h[:, c, :], start=False, stop=(c == HC - 1))
                    mm.then_inc(S["uf_done"], 1)

            steps(pe.Fori, step)

        @block.scalar
        def _(act):
            for c in range(early, HC):
                act.dma_start(loaded[c][1], sc_d[:, c * HIDDEN:(c + 1) * HIDDEN]).then_inc(w_in[c], 16)

            def normalise(k):
                act.wait_ge(S["ur_ready"], k + 1)
                at_least(act, S["ut_done"], k)
                nc.scalar.activation(u[:], pair_of(xres, k), ACT.Identity, bias=ur[:, 2:3],
                                     scale=ur[:, 1:2]).then_inc(S["un_ready"], 1)

            def weight_high(c):
                act.wait_ge(S["w_made"], c + 1)
                nc.scalar.activation(w_h[:, c, :], wf[:, c, :], ACT.Copy).then_inc(S["w_high1"], 1)

            normalise(0)
            weight_high(0)

            def step(k, s, ahead):
                if ahead >= 0:
                    act.wait_ge(S["ut_done"], k + 1)
                    at_least(act, S["uf_done"], k - 1)
                    nc.scalar.activation(uT_h[s][:], utp[:], ACT.Copy).then_inc(S["ut_high"], 1)
                if ahead >= 1:
                    normalise(k + 1)
                if isinstance(k, int) and k == 0:
                    for c in range(1, HC):
                        weight_high(c)

            steps(act.Fori, step)

        @block.gpsimd
        def _(pool):
            chain = Chain(pool, S["pool_chain4"])

            def root(k):
                pool.wait_ge(S["ustats_ready"], k + 1)
                at_least(pool, S["un_ready"], k)
                inverse_root(nc, chain, umom, ur, consts).then_inc(S["ur_ready"], 1)

            def weight_low(c):
                pool.wait_ge(S["w_high1"], c + 1)
                nc.gpsimd.tensor_tensor(w_l[:, c, :], wf[:, c, :], plain(w_h[:, c, :]),
                                        ALU.subtract).then_inc(S["w_split1"], 1)

            root(0)

            def step(k, s, ahead):
                if ahead >= 1:
                    root(k + 1)
                if isinstance(k, int) and k == 0:
                    for c in range(HC):
                        weight_low(c)

            steps(lambda a, b: chain.repeat(a, b, 6), step)

        @block.vector
        def _(dve):
            chain = Chain(dve, S["dve_chain4"])

            def ln_stats(k):
                at_least(dve, S["ustats_ready"], k)
                nc.vector.memset(spare[:], 0.0)
                chain.link(nc.vector.bn_stats(ustats[:], pair_of(xres, k)))
                at_least(dve, S["ur_ready"], k)
                nc.vector.memset(spare[:], 0.0)
                nc.vector.bn_aggr(umom[:], ustats[:]).then_inc(S["ustats_ready"], 1)

            def weight(c):
                dve.wait_ge(w_in[c], 32)
                nc.vector.scalar_tensor_tensor(wf[:, c, :], loaded[c][0], -128.0, loaded[c][1], ALU.add,
                                               ALU.mult).then_inc(S["w_made"], 1)

            ln_stats(0)
            weight(0)
            ln_stats(1)
            weight(1)

            def step(k, s, ahead):
                if isinstance(k, int) and k == 1:
                    for c in range(2, HC):
                        weight(c)
                if ahead >= 0:
                    dve.wait_ge(S["ut_high"], k + 1)
                    nc.vector.tensor_tensor(uT_l[s][:], utp[:], plain(uT_h[s][:]),
                                            ALU.subtract).then_inc(S["ut_split"], 1)
                if ahead >= 2:
                    ln_stats(k + 2)
                if not (isinstance(k, int) and k == 0):
                    dve.wait_ge(S["uf_done"], k)
                    nc.vector.tensor_tensor(pair_of(xres, k - 1), fp[1 - s][:], pair_of(xres, k - 1),
                                            ALU.add).then_inc(S["out_ready"], 1)

            steps(lambda a, b: chain.repeat(a, b, 2), step)


A1_SEMS = """w_in wvo_in wvo_ready spare_ready spare_used x_first x_rest c_in0 c_in1 ct_in0 ct_in1
    wvo_done w_ready stats_ready rstd_ready xn_ready x_high c_high x_stacked c_stacked k_proj
    q_proj k_max k_exp q_max q_sub q_exp q_summed0 q_rec q_norm tk_done tq_done kt_copied kt_high0
    kt_high1 kt_low qt_copied ct_high ct_split ct_stored g_step g_copied m_done m_scaled krec_done
    o_done o_stored dve_chain pool_chain"""
A2_SEMS = """ones_ready f_in f_ready sq_done ss_done ssum_ready rnorm_ready rwide_ready rp_done
    scaled_ready x1_ready yn_ready yt_done yt_copied rl_done logit_ready e_done low_ready lt_done
    lt_copied f_done x2_ready zn_ready zt_done z_high z_split ystats_ready yr_ready zstats_ready
    zr_ready dve_chain2 pool_chain2"""
B_SEMS = """qk_in w_in0 w_in1 w_in2 w_in3 w_high w_split kv_done q_done kt_done qt_done s_done
    pt_done y_done o_done1 k_squared k_summed k_root k_scaled q_squared q_summed q_root q_scaled
    v_high v_split kt_copied1 qt_copied1 bias_ready p_done prec_ready p_normed pt_high pt_split
    o_high o_split y_added dve_chain3 pool_chain3"""
C_SEMS = """u_in0 u_in1 u_in2 u_in3 w_made w_high1 w_split1 ustats_ready ur_ready un_ready ut_done
    ut_high ut_split uf_done out_ready stored dve_chain4 pool_chain4"""


def build(nc, x, ctx, ctx_t, l0_wq, l0_wk, l0_wv, l0_wo, l0_bo, l0_g, ffn_in, ffn_out, ffn_br, l1_w, l1_qk,
          f1_wq, f1_sc, out):
    with ExitStack() as st:
        xres = st.enter_context(nc.sbuf_tensor("xres", [P, HP, HIDDEN], FP32))
        kvT = st.enter_context(nc.sbuf_tensor("kvT", [P, HC, HP, 2, 2 * P], FP32R))
        ident = st.enter_context(nc.sbuf_tensor("ident", [P, P], FP32))
        consts = st.enter_context(nc.sbuf_tensor("consts", [P, MINUS_COL + 1], FP32))
        raw = [st.enter_context(nc.sbuf_tensor(f"raw{j}", [P, W_CHUNK], FP32)) for j in range(RAW)]
        made = st.enter_context(nc.semaphore("const_made"))
        a1, a2 = semaphores(nc, st, A1_SEMS), semaphores(nc, st, A2_SEMS)
        b_, c_ = semaphores(nc, st, B_SEMS), semaphores(nc, st, C_SEMS)
        const = (ident, consts)
        with nc.Block() as block:
            @block.gpsimd
            def _(pool):
                nc.gpsimd.memset(consts[:, 0:LN_COL], -0.5)
                nc.gpsimd.memset(consts[:, LN_COL:RMS_COL], LN_EPS)
                nc.gpsimd.memset(consts[:, RMS_COL:MINUS_COL], L1_DH * RMS_EPS)
                nc.gpsimd.memset(consts[:, MINUS_COL:], -1.0)
                nc.gpsimd.memset(ident[:], 0.0).then_inc(made, 1)
                pool.wait_ge(made, 1)
                nc.gpsimd.affine_select(out=ident[:], in_=ident[:], compare_op=ALU.not_equal, fill=1.0, base=0,
                                        pattern=[[-1, P]], channel_multiplier=1).then_inc(made, 1)
                pool.wait_ge(made, 2)
        with nc.Fori(0, HALVES) as half:
            with nc.sbuf_tensor("obuf", [P, HP, HIDDEN], FP32) as obuf:
                linear_attention(nc, a1, half, const, xres, kvT, obuf,
                                 (x, ctx, ctx_t, l0_wq, l0_wk, l0_wv, l0_wo, l0_bo))
                clear(nc, a1)
                norm_and_ffn(nc, a2, b_, const, xres, kvT, obuf, raw, (l0_g, ffn_in, ffn_out, ffn_br, l1_w))
                clear(nc, a2)
            grouped_attention(nc, b_, c_, half, const, xres, kvT, raw, (l1_w, l1_qk), (f1_wq, f1_sc))
            clear(nc, b_)
            quantised_ffn(nc, c_, half, const, xres, raw, (f1_wq, f1_sc), out)
            clear(nc, c_)


def kernel(**inputs):
    import numpy as _np
    import concourse.bacc as _bacc
    from concourse import mybir as _mybir
    from concourse.bass_utils import run_bass_kernel_spmd as _run

    a = {k: _np.asarray(v) for k, v in inputs.items()}
    x = a["x"].reshape(BATCHES * SEQ, HIDDEN)
    ctx = a["ctx_4096"].reshape(BATCHES * SEQ, HIDDEN)
    ctx_t = a["ctx_4096"].reshape(BATCHES, SEQ, HC, P).transpose(0, 3, 2, 1).reshape(BATCHES, P, HC * SEQ)
    twice = lambda w: _np.concatenate([w, w], axis=0)
    by_chunk = lambda w: w.reshape(-1, P, w.shape[-1]).transpose(1, 0, 2)
    ffn_in = by_chunk(_np.concatenate([a["L0_ffn_A"].reshape(FFN_LOW, HIDDEN), a["L0_ffn_Wr"]], axis=0).T)
    wq, wk, wv = (by_chunk(a[f"L1_xattn_{n}"]) for n in ("Wq", "Wk", "Wv"))
    wo = a["L1_xattn_Wo"].reshape(L1_HEADS, L1_DH, HIDDEN)
    groups = []
    for g in range(L1_KV):
        kv = slice(g * L1_DH, (g + 1) * L1_DH)
        q = slice(g * GROUP * L1_DH, (g + 1) * GROUP * L1_DH)
        groups.append(_np.concatenate([
            _np.concatenate([wk[:, :, kv], wv[:, :, kv]], axis=2).reshape(P, -1),
            wq[:, :, q].reshape(P, -1),
            wo[g * GROUP:(g + 1) * GROUP].transpose(1, 0, 2).reshape(P, -1)], axis=1))
    ins = {
        "x": x, "ctx": ctx, "ctx_t": ctx_t,
        "l0_wq": twice(a["L0_xattn_Wq"].T), "l0_wk": twice(a["L0_xattn_Wk"].T),
        "l0_wv": by_chunk(a["L0_xattn_Wv"]), "l0_wo": by_chunk(a["L0_xattn_Wo"].T),
        "l0_bo": twice(a["L0_xattn_bo"].reshape(SEQ, 1)), "l0_g": twice(a["L0_xattn_g"].reshape(SEQ, 1)),
        "ffn_in": ffn_in, "ffn_out": a["L0_ffn_B"].transpose(0, 2, 1).reshape(FFN_LOW, HIDDEN),
        "ffn_br": _np.repeat(a["L0_ffn_br"].reshape(1, FFN_HEADS), P, axis=0),
        "l1_w": _np.stack(groups),
        "l1_qk": _np.stack([a["L1_xattn_q_norm_w"], a["L1_xattn_k_norm_w"]], axis=1),
        "f1_wq": by_chunk(a["L1_ffn_w_q"].T).reshape(P, -1),
        "f1_sc": by_chunk(_np.repeat(a["L1_ffn_scales"].T, HIDDEN // a["L1_ffn_scales"].shape[1], axis=0)).reshape(P, -1),
    }
    ins = {k: _np.ascontiguousarray(v) for k, v in ins.items()}
    nc = _bacc.Bacc("TRN2", target_bir_lowering=False, num_devices=1)
    args = [nc.dram_tensor(f"in_{k}", v.shape, _mybir.dt.from_np(v.dtype), kind="ExternalInput").ap()
            for k, v in ins.items()]
    out = nc.dram_tensor("out", (BATCHES * SEQ, HIDDEN), FP32, kind="ExternalOutput").ap()
    build(nc, *args, out)
    r = _run(nc, [{f"in_{k}": v for k, v in ins.items()}], core_ids=[0])
    return r.results[0]["out"].reshape(BATCHES, SEQ, HIDDEN)
```
